# Optimizing a Trainium2 kernel written in Bass

```python
import numpy as np
import jax
import jax.numpy as jnp

def _softmax(x, axis=-1):
    return jax.nn.softmax(x, axis=axis)

def _gelu(x):
    return jax.nn.gelu(x, approximate=True)

def _silu(x):
    return jax.nn.silu(x)

def _sigmoid(x):
    return jax.nn.sigmoid(x)

def _layernorm(x, axis=-1, eps=1e-05):
    m = jnp.mean(x, axis=axis, keepdims=True)
    v = jnp.var(x, axis=axis, keepdims=True)
    return (x - m) / jnp.sqrt(v + eps)

def _scatter_add(tgt, idx, src, axis=0):
    return tgt.at[idx].add(src)

def _segment_sum(src, seg, n):
    return jax.ops.segment_sum(src, seg, n)
kernel_name = 'mk_gnn_resnorm_d4_gnn_r64_8ba5d5'

def setup_inputs(seed: int=0):
    np.random.seed(seed)
    _w = jnp.asarray

    def _rec_inputs():
        import jax
        import jax.numpy as jnp
        _gk = jax.random.key(seed)
        x = -0.000202 + 1 * jax.random.normal(jax.random.fold_in(_gk, 1), (100000, 128), jnp.float32)
        src = jax.random.randint(jax.random.fold_in(_gk, 2), (50000,), 0, 100000, jnp.int32)
        dst = jax.random.randint(jax.random.fold_in(_gk, 3), (50000,), 0, 100000, jnp.int32)
        _o = jnp.argsort(dst, stable=True)
        src = src[_o]
        dst = dst[_o]
        edge_attr_16 = 0.000254156 + 0.999948 * jax.random.normal(jax.random.fold_in(_gk, 12), (50000, 16), jnp.float32)
        edge_type_8 = jax.random.randint(jax.random.fold_in(_gk, 14), (50000,), 0, 8, jnp.int32)
        return (x, src, dst, edge_attr_16, edge_type_8)
    x, src, dst, edge_attr_16, edge_type_8 = _rec_inputs()

    def _L0_gnn_setup():
        import jax, jax.numpy as jnp
        import numpy as np
        N_NODES = 50000
        N_EDGES = 9375
        D = 128
        N_ETYPES = 8
        key = jax.random.key(seed)
        ks = jax.random.split(key, 9)
        nfeat = jax.random.normal(ks[0], (N_NODES, D), dtype=jnp.float32)
        head_w = jax.random.normal(ks[1], (D,), dtype=jnp.float32) * 0.1
        head_b = jax.random.normal(ks[2], (1,), dtype=jnp.float32)
        tail_w = jax.random.normal(ks[3], (D,), dtype=jnp.float32) * 0.1
        tail_b = jax.random.normal(ks[4], (1,), dtype=jnp.float32)
        rel_w = jax.random.normal(ks[5], (N_ETYPES,), dtype=jnp.float32)
        src = jax.random.randint(ks[6], (N_EDGES,), 0, N_NODES, dtype=jnp.int32)
        dst = jax.random.randint(ks[7], (N_EDGES,), 0, N_NODES, dtype=jnp.int32)
        etype = jax.random.randint(ks[8], (N_EDGES,), 0, N_ETYPES, dtype=jnp.int32)
        return {'nfeat': nfeat, 'head_w': head_w, 'head_b': head_b, 'tail_w': tail_w, 'tail_b': tail_b, 'rel_w': rel_w, 'src': src, 'dst': dst, 'etype': etype}
    _L0_gnn_all = _L0_gnn_setup()
    _L0_gnn_in = {k: v for k, v in _L0_gnn_all.items() if k in ('head_w', 'head_b', 'tail_w', 'tail_b', 'rel_w')}
    del _L0_gnn_all

    def _L1_gnn_setup():
        import jax, jax.numpy as jnp
        import numpy as np
        N_NODES = 50000
        key = jax.random.key(seed)
        k1, k2, k3, k4, k5 = jax.random.split(key, 5)
        N, E, D_IN, D_OUT = (N_NODES, 12500, 128, 128)
        features = jax.random.normal(k1, (N, D_IN), dtype=jnp.float32)
        src = jax.random.randint(k2, (E,), 0, N, dtype=jnp.int32)
        dst = jax.random.randint(k3, (E,), 0, N, dtype=jnp.int32)
        W_self = jax.random.normal(k4, (D_IN, D_OUT), dtype=jnp.float32) / np.sqrt(D_IN)
        W_neigh = jax.random.normal(k5, (D_IN, D_OUT), dtype=jnp.float32) / np.sqrt(D_IN)
        b = jnp.zeros((D_OUT,), dtype=jnp.float32)
        return {'features': features, 'src': src, 'dst': dst, 'W_self': W_self, 'W_neigh': W_neigh, 'b': b}
    _L1_gnn_all = _L1_gnn_setup()
    _L1_gnn_in = {k: v for k, v in _L1_gnn_all.items() if k in ('W_self', 'W_neigh', 'b')}
    del _L1_gnn_all

    def _L2_gnn_setup():
        import jax, jax.numpy as jnp
        import numpy as np
        N_NODES = 100000
        N_EDGES = 12500
        D_IN = 128
        D_OUT = 128
        E_DIM = 16
        key = jax.random.key(seed)
        k1, k2, k3, k4, k5 = jax.random.split(key, 5)
        x = jax.random.normal(k1, (N_NODES, D_IN), dtype=jnp.float32)
        edge_index = jax.random.randint(k2, (2, N_EDGES), 0, N_NODES, dtype=jnp.int64)
        edge_attr = jax.random.normal(k3, (N_EDGES, E_DIM), dtype=jnp.float32)
        W = jax.random.uniform(k4, (D_IN, D_OUT), dtype=jnp.float32, minval=-1.0, maxval=1.0) * float(np.sqrt(6.0 / (D_IN + D_OUT)))
        edge_w = jax.random.uniform(k5, (E_DIM, D_OUT), dtype=jnp.float32, minval=-1.0, maxval=1.0) * float(np.sqrt(6.0 / (E_DIM + D_OUT)))
        b = jnp.zeros((D_OUT,), dtype=jnp.float32)
        return {'x': x, 'edge_index': edge_index, 'edge_attr': edge_attr, 'W': W, 'edge_w': edge_w, 'b': b}
    _L2_gnn_all = _L2_gnn_setup()
    _L2_gnn_in = {k: v for k, v in _L2_gnn_all.items() if k in ('W', 'edge_w', 'b')}
    del _L2_gnn_all

    def _L3_gnn_setup():
        import jax, jax.numpy as jnp
        import numpy as np
        N = 50000
        E = 12500
        D = 128
        MAX_NODES = 4
        EPS = 1e-05

        def sort_conv(x, edge_index, blank, W, b, cw, cb, a):
            n, d = x.shape
            e = edge_index.shape[1]
            src, dst = (edge_index[0], edge_index[1])
            msgs = x[src]
            order = jnp.argsort(dst)
            dst_s = dst[order]
            counts = jax.ops.segment_sum(jnp.ones((e,), jnp.int32), dst, num_segments=n + 1)
            starts = jnp.concatenate([jnp.zeros((1,), jnp.int32), jnp.cumsum(counts)[:-1].astype(jnp.int32)])
            pos = jnp.arange(e, dtype=jnp.int32) - starts[dst_s]
            slot = jnp.where(pos < MAX_NODES, pos, MAX_NODES)
            dense = jnp.zeros((n + 1, MAX_NODES + 1, d), x.dtype).at[dst_s, slot].set(msgs[order])
            mask = jnp.zeros((n + 1, MAX_NODES + 1), bool).at[dst_s, slot].set(True)
            dense, mask = (dense[:, :MAX_NODES], mask[:, :MAX_NODES])
            blank_p = W @ blank + b
            filled = dense + (~mask)[..., None].astype(x.dtype) * blank_p
            srt = jnp.sort(filled, axis=1)
            out = jnp.einsum('nmd,m->nd', srt, cw) + cb
            node_out, blank_new = (out[:-1], out[-1])
            return (a * x + node_out, a * blank + blank_new)

        def batch_norm(h, g, be):
            mu = h.mean(0)
            var = h.var(0)
            return (h - mu) / jnp.sqrt(var + EPS) * g + be
        key = jax.random.key(seed)
        ks = jax.random.split(key, 16)
        inp = {'x': jax.random.normal(ks[0], (N, D), jnp.float32), 'edge_index': jax.random.randint(ks[1], (2, E), 0, N, jnp.int32)}
        for i in range(2):
            o = 2 + 6 * i
            W = jax.random.normal(ks[o], (D, D), jnp.float32) * (2.0 / (D + D)) ** 0.5
            W = W / jnp.linalg.norm(W, axis=1, keepdims=True)
            inp[f'W{i}'] = W
            inp[f'b{i}'] = jnp.zeros((D,), jnp.float32)
            inp[f'cw{i}'] = jax.random.normal(ks[o + 1], (MAX_NODES,), jnp.float32) * (2.0 / (MAX_NODES + 1)) ** 0.5
            inp[f'cb{i}'] = jnp.zeros((1,), jnp.float32)
            inp[f'a{i}'] = jax.random.uniform(ks[o + 2], (1,), jnp.float32, -1.0, 1.0)
            inp[f'g{i}'] = jnp.ones((D,), jnp.float32)
            inp[f'be{i}'] = jnp.zeros((D,), jnp.float32)
            inp[f'blank{i}'] = jnp.zeros((D,), jnp.float32)
        return inp
    _L3_gnn_all = _L3_gnn_setup()
    _L3_gnn_in = {k: v for k, v in _L3_gnn_all.items() if k in ('W0', 'b0', 'cw0', 'cb0', 'a0', 'g0', 'be0', 'blank0', 'W1', 'b1', 'cw1', 'cb1', 'a1', 'g1', 'be1', 'blank1')}
    del _L3_gnn_all
    return {'x': x, 'src': src, 'dst': dst, 'edge_attr_16': edge_attr_16, 'edge_type_8': edge_type_8, 'L0_gnn_head_w': _L0_gnn_in['head_w'], 'L0_gnn_head_b': _L0_gnn_in['head_b'], 'L0_gnn_tail_w': _L0_gnn_in['tail_w'], 'L0_gnn_tail_b': _L0_gnn_in['tail_b'], 'L0_gnn_rel_w': _L0_gnn_in['rel_w'], 'L1_gnn_W_self': _L1_gnn_in['W_self'], 'L1_gnn_W_neigh': _L1_gnn_in['W_neigh'], 'L1_gnn_b': _L1_gnn_in['b'], 'L2_gnn_W': _L2_gnn_in['W'], 'L2_gnn_edge_w': _L2_gnn_in['edge_w'], 'L2_gnn_b': _L2_gnn_in['b'], 'L3_gnn_W0': _L3_gnn_in['W0'], 'L3_gnn_b0': _L3_gnn_in['b0'], 'L3_gnn_cw0': _L3_gnn_in['cw0'], 'L3_gnn_cb0': _L3_gnn_in['cb0'], 'L3_gnn_a0': _L3_gnn_in['a0'], 'L3_gnn_g0': _L3_gnn_in['g0'], 'L3_gnn_be0': _L3_gnn_in['be0'], 'L3_gnn_blank0': _L3_gnn_in['blank0'], 'L3_gnn_W1': _L3_gnn_in['W1'], 'L3_gnn_b1': _L3_gnn_in['b1'], 'L3_gnn_cw1': _L3_gnn_in['cw1'], 'L3_gnn_cb1': _L3_gnn_in['cb1'], 'L3_gnn_a1': _L3_gnn_in['a1'], 'L3_gnn_g1': _L3_gnn_in['g1'], 'L3_gnn_be1': _L3_gnn_in['be1'], 'L3_gnn_blank1': _L3_gnn_in['blank1']}

def reference(x, src, dst, edge_attr_16, edge_type_8, L0_gnn_head_w, L0_gnn_head_b, L0_gnn_tail_w, L0_gnn_tail_b, L0_gnn_rel_w, L1_gnn_W_self, L1_gnn_W_neigh, L1_gnn_b, L2_gnn_W, L2_gnn_edge_w, L2_gnn_b, L3_gnn_W0, L3_gnn_b0, L3_gnn_cw0, L3_gnn_cb0, L3_gnn_a0, L3_gnn_g0, L3_gnn_be0, L3_gnn_blank0, L3_gnn_W1, L3_gnn_b1, L3_gnn_cw1, L3_gnn_cb1, L3_gnn_a1, L3_gnn_g1, L3_gnn_be1, L3_gnn_blank1):
    import jax
    import jax.numpy as jnp

    def _L0_gnn_ref(nfeat, head_w, head_b, tail_w, tail_b, rel_w, src, dst, etype):
        import jax, jax.numpy as jnp
        import numpy as np
        N_NODES = 50000
        N_EDGES = 9375
        D = 128
        N_ETYPES = 8
        n = nfeat.shape[0]
        el = nfeat @ head_w + head_b[0]
        er = nfeat @ tail_w + tail_b[0]
        logits = el[src] + er[dst] + rel_w[etype]
        seg_max = jax.ops.segment_max(logits, dst, num_segments=n)
        ex = jnp.exp(logits - seg_max[dst])
        seg_sum = jax.ops.segment_sum(ex, dst, num_segments=n)
        a = ex / seg_sum[dst]
        out = jax.ops.segment_sum(a[:, None] * nfeat[src], dst, num_segments=n)
        return out

    def _L1_gnn_ref(features, src, dst, W_self, W_neigh, b):
        import jax, jax.numpy as jnp
        import numpy as np
        N_NODES = 50000
        N = features.shape[0]
        neigh_sum = jax.ops.segment_sum(features[src], dst, num_segments=N)
        deg = jax.ops.segment_sum(jnp.ones_like(dst, dtype=features.dtype), dst, num_segments=N)
        h_neigh = neigh_sum / jnp.maximum(deg, 1.0)[:, None]
        return features @ W_self + h_neigh @ W_neigh + b

    def _L2_gnn_ref(x, edge_index, edge_attr, W, edge_w, b):
        import jax, jax.numpy as jnp
        import numpy as np
        N_NODES = 100000
        N_EDGES = 12500
        D_IN = 128
        D_OUT = 128
        E_DIM = 16
        src, dst = (edge_index[0], edge_index[1])
        xw = x @ W
        ew = edge_attr @ edge_w
        msg = xw[src] * ew
        out = jax.ops.segment_sum(msg, dst, num_segments=x.shape[0])
        out = out + b
        return out

    def _L3_gnn_ref(x, edge_index, W0, b0, cw0, cb0, a0, g0, be0, blank0, W1, b1, cw1, cb1, a1, g1, be1, blank1):
        import jax, jax.numpy as jnp
        import numpy as np
        N = 50000
        E = 12500
        D = 128
        MAX_NODES = 4
        EPS = 1e-05

        def sort_conv(x, edge_index, blank, W, b, cw, cb, a):
            n, d = x.shape
            e = edge_index.shape[1]
            src, dst = (edge_index[0], edge_index[1])
            msgs = x[src]
            order = jnp.argsort(dst)
            dst_s = dst[order]
            counts = jax.ops.segment_sum(jnp.ones((e,), jnp.int32), dst, num_segments=n + 1)
            starts = jnp.concatenate([jnp.zeros((1,), jnp.int32), jnp.cumsum(counts)[:-1].astype(jnp.int32)])
            pos = jnp.arange(e, dtype=jnp.int32) - starts[dst_s]
            slot = jnp.where(pos < MAX_NODES, pos, MAX_NODES)
            dense = jnp.zeros((n + 1, MAX_NODES + 1, d), x.dtype).at[dst_s, slot].set(msgs[order])
            mask = jnp.zeros((n + 1, MAX_NODES + 1), bool).at[dst_s, slot].set(True)
            dense, mask = (dense[:, :MAX_NODES], mask[:, :MAX_NODES])
            blank_p = W @ blank + b
            filled = dense + (~mask)[..., None].astype(x.dtype) * blank_p
            srt = jnp.sort(filled, axis=1)
            out = jnp.einsum('nmd,m->nd', srt, cw) + cb
            node_out, blank_new = (out[:-1], out[-1])
            return (a * x + node_out, a * blank + blank_new)

        def batch_norm(h, g, be):
            mu = h.mean(0)
            var = h.var(0)
            return (h - mu) / jnp.sqrt(var + EPS) * g + be
        layers = [(W0, b0, cw0, cb0, a0, g0, be0, blank0), (W1, b1, cw1, cb1, a1, g1, be1, blank1)]
        for W, b, cw, cb, a, g, be, blank in layers:
            h, _ = sort_conv(x, edge_index, blank, W, b, cw, cb, a)
            h = batch_norm(h, g, be)
            x = x + h
        return x
    edge_index = jnp.stack([src, dst])
    x = _layernorm(x + _L0_gnn_ref(x, L0_gnn_head_w, L0_gnn_head_b, L0_gnn_tail_w, L0_gnn_tail_b, L0_gnn_rel_w, src, dst, edge_type_8), axis=-1)
    x = _layernorm(x + _L1_gnn_ref(x, src, dst, L1_gnn_W_self, L1_gnn_W_neigh, L1_gnn_b), axis=-1)
    x = _layernorm(x + _L2_gnn_ref(x, edge_index, edge_attr_16, L2_gnn_W, L2_gnn_edge_w, L2_gnn_b), axis=-1)
    x = _layernorm(x + _L3_gnn_ref(x, edge_index, L3_gnn_W0, L3_gnn_b0, L3_gnn_cw0, L3_gnn_cb0, L3_gnn_a0, L3_gnn_g0, L3_gnn_be0, L3_gnn_blank0, L3_gnn_W1, L3_gnn_b1, L3_gnn_cw1, L3_gnn_cb1, L3_gnn_a1, L3_gnn_g1, L3_gnn_be1, L3_gnn_blank1), axis=-1)
    return x

_drawn_inputs = setup_inputs


def setup_inputs(seed=0):
    import zlib

    import numpy as np

    out = dict(_drawn_inputs(seed))
    spreads = {'L1_gnn_b': (0.0, 0.1),
     'L2_gnn_b': (0.0, 0.1),
     'L3_gnn_b0': (0.0, 0.1),
     'L3_gnn_g0': (1.0, 0.2),
     'L3_gnn_be0': (0.0, 0.1),
     'L3_gnn_blank0': (0.0, 0.1),
     'L3_gnn_b1': (0.0, 0.1),
     'L3_gnn_g1': (1.0, 0.2),
     'L3_gnn_be1': (0.0, 0.1),
     'L3_gnn_blank1': (0.0, 0.1)}
    factors = {}
    for name, (base, spread) in spreads.items():
        noise = np.random.default_rng([zlib.crc32(name.encode()), seed]).standard_normal(out[name].shape)
        drawn = base * np.exp(spread * noise) if base else spread * noise
        out[name] = jnp.asarray(drawn.astype(out[name].dtype))
    for name, factor in factors.items():
        out[name] = (out[name] * factor).astype(out[name].dtype)
    return out
```

```python
import concourse.bass as bass
from concourse import mybir
from contextlib import ExitStack, contextmanager

F32, I32 = mybir.dt.float32, mybir.dt.int32
ALU, ACT, AX = mybir.AluOpType, mybir.ActivationFunctionType, mybir.AxisListType

P = 128
D = 128
ROWS = 125
K = 8
HALF = K // 2
T = 17
GROUP = P * T
C4 = 4
SKIP = 1 << 23
LOW = -1.0e30
EPS = 1e-5


class Chain:

    def __init__(self, engine, sem, base=0):
        self.engine, self.sem, self.base, self.n = engine, sem, base, 0

    def __call__(self, ins):
        self.n += 1
        ins.then_inc(self.sem, 1)
        self.engine.wait_ge(self.sem, self.base + self.n)


class Env:

    def __init__(self, nc, ctx):
        self.nc, self.ctx, self.count, self.sems = nc, ctx, 0, []

    def sem(self, name):
        self.count += 1
        self.sems.append(self.nc.alloc_semaphore(name=f"{name}_{self.count}"))
        return self.sems[-1]

    @contextmanager
    def phase(self):
        with ExitStack() as ctx:
            yield ctx
        self.nc.clear_and_free_semaphores(self.sems)
        self.nc.all_engine_barrier()
        self.sems = []

    def sb(self, ctx, name, shape, dt=F32):
        self.count += 1
        return ctx.enter_context(self.nc.sbuf_tensor(f"{name}_{self.count}", shape, dt))

    def ps(self, ctx, name, shape):
        self.count += 1
        return ctx.enter_context(self.nc.psum_tensor(f"{name}_{self.count}", shape, F32))


def flat(ap):
    return ap.rearrange("p a b -> p (a b)")


def rounds(engine, n, body):
    body(0, True, False)
    if n > 2:
        with engine.Fori(1, n - 1) as i:
            body(i, False, False)
    body(n - 1, False, True)


def tables_phase(env, a, t):
    nc = env.nc
    E = a["src"].shape[0]
    NT = E // ROWS
    Q = NT // C4
    F = C4 * ROWS
    with env.phase() as ctx:
        dsti = env.sb(ctx, "dsti", [Q, F + 4], I32)
        srci = env.sb(ctx, "srci", [Q, F + 4], I32)
        dst = env.sb(ctx, "dst", [Q, F + 4])
        src = env.sb(ctx, "src", [Q, F + 4])
        wk = {n: env.sb(ctx, n, [Q, F]) for n in
              ("head", "lhead", "pos", "dstm", "tmp", "ones", "fwd", "bwd", "has1", "has2", "has3", "sidx3", "headpos")}
        pad = {n: env.sb(ctx, n, [Q, C4, ROWS + 1]) for n in ("gidx", "didx", "sidx", "row", "nx", "w1")}
        iotaf = env.sb(ctx, "iotaf", [Q, F])
        ps = [env.ps(ctx, f"ps{k}", [P, C4, P]) for k in range(6)]
        loaded, filled, iotas = env.sem("tables_loaded"), env.sem("tables_filled"), env.sem("tables_iotas")
        chain, transposed, used = env.sem("tables_chain"), env.sem("tables_transposed"), env.sem("tables_used")
        pe_ready = env.sem("tables_ready_for_pe")
        pe_done = env.sem("tables_pe_done")
        seg = SegTotals(env, ctx, Q, F)
        N_LOADS = 6
        OUTS = [("gidx", ROWS + 1), ("didx", ROWS + 1), ("sidx", ROWS + 1), ("row", ROWS + 1), ("nx", ROWS + 1),
                ("w1", ROWS + 1), ("has1", ROWS), ("has2", ROWS), ("has3", ROWS), ("sidx3", ROWS), ("gidx3", P)]
        with nc.Block() as block:
            @block.sync
            def _(sp):
                sp.wait_ge(filled, 1)
                with nc.allow_non_contiguous_dma(reason="halo columns"):
                    for tile, dram in ((dsti, a["dst"]), (srci, a["src"])):
                        v = dram.rearrange("(q f) -> q f", q=Q)
                        sp.dma_start(tile[:, 1:F + 1], v[:, :]).then_inc(loaded, 16)
                        sp.dma_start(tile[0:Q - 1, F + 1:F + 4], v[1:Q, 0:3]).then_inc(loaded, 16)
                        if tile is dsti:
                            sp.dma_start(tile[1:Q, 0:1], v[0:Q - 1, F - 1:F]).then_inc(loaded, 16)
                    sp.dma_start(t["etype_i"][:, :], a["etype"].rearrange("(q f) -> q f", q=Q)).then_inc(loaded, 16)
                sp.wait_ge(loaded, 16 * N_LOADS)

            @block.gpsimd
            def _(pool):
                nc.gpsimd.iota(iotaf[:], [[1, F]], base=0, channel_multiplier=0,
                               allow_small_or_imprecise_dtypes=True)
                nc.gpsimd.iota(t["cols"][:], [[1, P]], base=0, channel_multiplier=0,
                               allow_small_or_imprecise_dtypes=True)
                nc.gpsimd.iota(t["part"][:], [[0, 1]], base=0, channel_multiplier=1,
                               allow_small_or_imprecise_dtypes=True).then_inc(iotas, 1)

            @block.vector
            def _(dve):
                nc.vector.memset(dsti[:], -1)
                nc.vector.memset(srci[:], SKIP).then_inc(filled, 1)
                for n in ("gidx", "didx", "sidx", "gidx3", "sidx3"):
                    nc.vector.memset(t[n][:], SKIP)
                for n in ("row", "nx", "w1", "w0", "has1", "has2", "has3"):
                    nc.vector.memset(t[n][:], 0.0)
                nc.vector.memset(t["one"][:], 1.0)
                nc.vector.memset(wk["ones"][:], 1.0)
                for n in ("gidx", "didx", "sidx"):
                    nc.vector.memset(pad[n][:, :, 0:1], float(SKIP))
                for n in ("row", "w1"):
                    nc.vector.memset(pad[n][:, :, 0:1], 1.0)
                link = Chain(dve, chain)
                dve.wait_ge(iotas, 1)
                link(nc.vector.tensor_scalar(t["ident"][:], t["cols"][:], t["part"][:, 0:1], None, ALU.is_equal))
                dve.wait_ge(loaded, 16 * N_LOADS)
                link(nc.vector.tensor_copy(dst[:], dsti[:]))
                link(nc.vector.tensor_copy(src[:], srci[:]))
                me, before, after = dst[:, 1:F + 1], dst[:, 0:F], dst[:, 2:F + 2]
                me4 = me.rearrange("q (c p) -> q c p", c=C4)
                link(nc.vector.tensor_tensor(t["same"][:], me, before, ALU.is_equal))
                link(nc.vector.tensor_tensor(t["nsame"][:], me, after, ALU.is_equal))
                link(nc.vector.tensor_scalar(t["sadd"][:], t["same"][:], -LOW, LOW, ALU.mult, ALU.add))
                link(nc.vector.tensor_scalar(t["nadd"][:], t["nsame"][:], -LOW, LOW, ALU.mult, ALU.add))
                link(nc.vector.tensor_tensor(t["thru"][:, 0:1], dst[:, F:F + 1], dst[:, 0:1], ALU.is_equal))
                link(nc.vector.tensor_tensor(t["thru"][:, 1:2], dst[:, 1:2], dst[:, F + 1:F + 2], ALU.is_equal))
                link(nc.vector.tensor_scalar(t["thru"][:, 2:4], t["thru"][:, 0:2], -LOW, LOW, ALU.mult, ALU.add))
                nxt = dst[:, ROWS + 1:F + 2:ROWS].unsqueeze(2)
                link(nc.vector.tensor_tensor(pad["nx"][:, :, 1:], me4, nxt.to_broadcast([Q, C4, ROWS]), ALU.is_equal))
                link(nc.vector.tensor_copy(pad["nx"][:, :, 0:1], pad["nx"][:, :, 1:2]))
                link(nc.vector.tensor_scalar(wk["head"][:], t["same"][:], -1.0, 1.0, ALU.mult, ALU.add))
                link(nc.vector.tensor_copy(wk["lhead"][:], wk["head"][:]))
                link(nc.vector.memset(wk["lhead"][:, 0:F:ROWS], 1.0))
                link(nc.vector.tensor_tensor(wk["tmp"][:], wk["lhead"][:], iotaf[:], ALU.mult))
                link(nc.vector.memset(wk["dstm"][:], 0.0))
                link(nc.vector.tensor_tensor_scan(wk["headpos"][:], wk["dstm"][:], wk["tmp"][:], 0.0, ALU.add, ALU.max))
                for c in range(C4):
                    link(nc.vector.tensor_scalar(pad["row"][:, c, 1:], wk["headpos"][:, c * ROWS:(c + 1) * ROWS],
                                                 float(1 - c * ROWS), None, ALU.add))
                link(nc.vector.tensor_scalar(wk["dstm"][:], me, float(-SKIP), None, ALU.add))
                link(nc.vector.tensor_scalar(pad["sidx"][:, :, 1:], pad["nx"][:, :, 1:], -1.0, 1.0, ALU.mult, ALU.add))
                link(nc.vector.tensor_tensor(pad["sidx"][:, :, 1:], pad["sidx"][:, :, 1:],
                                             wk["lhead"][:].rearrange("q (c p) -> q c p", c=C4), ALU.mult))
                link(nc.vector.tensor_tensor(pad["sidx"][:, :, 1:], pad["sidx"][:, :, 1:],
                                             wk["dstm"][:].rearrange("q (c p) -> q c p", c=C4), ALU.mult))
                link(nc.vector.tensor_scalar(pad["sidx"][:, :, 1:], pad["sidx"][:, :, 1:], float(SKIP), None, ALU.add))
                link(nc.vector.tensor_copy(pad["gidx"][:, :, 1:], src[:, 1:F + 1].rearrange("q (c p) -> q c p", c=C4)))
                link(nc.vector.tensor_copy(pad["didx"][:, :, 1:], me4))
                link(nc.vector.tensor_tensor(wk["sidx3"][:], wk["head"][:], wk["dstm"][:], ALU.mult))
                link(nc.vector.tensor_scalar(wk["sidx3"][:], wk["sidx3"][:], float(SKIP), None, ALU.add))
                seg.vector(link, dve, t, wk["ones"][:], wk["fwd"][:], wk["bwd"][:], "sum")
                for k in (1, 2, 3):
                    link(nc.vector.tensor_scalar(wk[f"has{k}"][:], wk["fwd"][:], k + 0.5, None, ALU.is_gt))
                nc.vector.reciprocal(pad["w1"][:, :, 1:], wk["fwd"][:].rearrange("q (c p) -> q c p", c=C4)
                                     ).then_inc(pe_ready, 1)
                for j, (n, rows) in enumerate(OUTS):
                    dve.wait_ge(transposed, j + 1)
                    nc.vector.tensor_copy(t[n][0:rows, :].rearrange("p (q c) -> p c q", c=C4),
                                          ps[j % 6][0:rows, :, 0:Q]).then_inc(used, 1)
                dve.wait_ge(used, len(OUTS))

            @block.tensor
            def _(pe):
                seg.tensor(pe, t, 0)
                pe.wait_ge(pe_ready, 1)
                for j, (n, rows) in enumerate(OUTS):
                    if j >= 6:
                        pe.wait_ge(used, j - 5)
                    for c in range(C4):
                        if n == "gidx3":
                            s = src[:, 1 + c * ROWS:1 + c * ROWS + P]
                        elif n in pad:
                            s = pad[n][:, c, :]
                        else:
                            s = wk[n][:, c * ROWS:(c + 1) * ROWS]
                        last = nc.tensor.transpose(ps[j % 6][0:rows, c, 0:Q], s, t["ident"][0:Q, 0:Q])
                    last.then_inc(transposed, 1)


class SegTotals:

    def __init__(self, env, ctx, Q, F):
        self.env, self.Q, self.F = env, Q, F
        self.row = env.sb(ctx, "seg_row", [1, 2, P])
        self.carry = env.sb(ctx, "seg_carry", [1, P + 1])
        self.cin = env.sb(ctx, "seg_cin", [P, 1])
        self.psr = env.ps(ctx, "seg_psr", [P, 2, P])
        self.psc = env.ps(ctx, "seg_psc", [P, 1])
        self.ready = env.sem("seg_column_ready")
        self.rows = env.sem("seg_rows_transposed")
        self.scanned = env.sem("seg_carries_scanned")
        self.cols = env.sem("seg_carry_column_done")
        self.ask = []
        self.calls = 0

    def vector(self, link, dve, t, val, fwd, bwd, kind):
        nc, Q, F = self.env.nc, self.Q, self.F
        if kind == "max":
            op0, op1, init, d0, thru = ALU.add, ALU.max, LOW, ("sadd", "nadd"), (2, 3)
        else:
            op0, op1, init, d0, thru = ALU.mult, ALU.add, 0.0, ("same", "nsame"), (0, 1)
        for side, out in ((0, fwd), (1, bwd)):
            def way(ap):
                return ap[:, ::-1] if side else ap
            last = out[:, 0:1] if side else out[:, F - 1:F]
            link(nc.vector.tensor_tensor_scan(way(out), way(t[d0[side]][:]), way(val), init, op0, op1))
            self.ask.append((last, thru[side], side))
            nc.vector.memset(self.carry[:], init).then_inc(self.ready, 1)
            self.calls += 1
            n = self.calls
            dve.wait_ge(self.rows, n)
            link(nc.vector.tensor_copy(self.row[:, :, 0:Q], self.psr[0:1, :, 0:Q]))
            to = self.carry[:, 0:Q] if side else self.carry[:, 1:Q + 1]
            nc.vector.tensor_tensor_scan(way(to), way(self.row[:, 1, 0:Q]), way(self.row[:, 0, 0:Q]),
                                         init, op0, op1).then_inc(self.scanned, 1)
            dve.wait_ge(self.cols, n)
            link(nc.vector.tensor_copy(self.cin[0:Q, :], self.psc[0:Q, :]))
            link(nc.vector.tensor_tensor_scan(way(out), way(t[d0[side]][:]), way(val), self.cin[0:Q, 0:1], op0, op1))
        if kind == "max":
            link(nc.vector.tensor_tensor(fwd, fwd, bwd, ALU.max))
        else:
            link(nc.vector.tensor_tensor(fwd, fwd, bwd, ALU.add))
            link(nc.vector.tensor_tensor(fwd, fwd, val, ALU.subtract))

    def tensor(self, pe, t, since):
        nc, Q = self.env.nc, self.Q
        for n, (last, thru, side) in enumerate(self.ask[since:], since):
            pe.wait_ge(self.ready, n + 1)
            nc.tensor.transpose(self.psr[0:1, 0, 0:Q], last, t["ident"][0:Q, 0:Q])
            nc.tensor.transpose(self.psr[0:1, 1, 0:Q], t["thru"][:, thru:thru + 1],
                                t["ident"][0:Q, 0:Q]).then_inc(self.rows, 1)
            pe.wait_ge(self.scanned, n + 1)
            nc.tensor.matmul(self.psc[0:Q, :], self.carry[0:1, side:side + Q], t["one"][0:1, 0:1],
                             start=True, stop=True).then_inc(self.cols, 1)


def logits_phase(env, a, t, edge_rows, agg, scratch):
    nc, x = env.nc, a["x"]
    N, E = x.shape[0], a["src"].shape[0]
    NB = E // (ROWS * K)
    NG = agg.shape[0] // GROUP
    ZB = -(-NG // (NB // 2))
    with env.phase() as ctx:
        g = [env.sb(ctx, f"rows_src_dst{b}", [P, K, 2, D]) for b in range(2)]
        prod = env.sb(ctx, "prod", [P, K, 2 * D])
        w = env.sb(ctx, "head_tail_w", [P, 2 * D])
        zeros = env.sb(ctx, "zeros", [P, T * D])
        idx = [env.sb(ctx, f"idx{b}", [P, 2, K], I32) for b in range(2)]
        begun = env.sem("dma_series_begun")
        cleared, idx_ready, w_loaded = env.sem("cleared"), env.sem("idx_ready"), env.sem("w_loaded")
        gathered = [env.sem(f"gathered{b}") for b in range(2)]
        stored = [env.sem(f"stored{b}") for b in range(2)]
        used, multiplied, zeroed = env.sem("rows_used"), env.sem("multiplied"), env.sem("zeroed")
        with nc.Block() as block:
            @block.gpsimd
            def _(pool):
                bound = pool.to_reg(N - 1)

                def body(i, first, last):
                    for b in range(2):
                        n = 2 * i + b
                        pool.wait_ge(idx_ready, n + 1)
                        if not first:
                            pool.wait_ge(used, n - 1)
                            pool.wait_ge(stored[b], 16 * i)
                        pool.sem_inc(begun, 1)
                        for k in range(K):
                            for s in range(2):
                                pool.indirect_dma_start(
                                    out=g[b][:, k, s, :], out_offset=None, in_=x[:, :],
                                    in_offset=bass.IndirectOffsetOnAxis(ap=idx[b][:, s, k:k + 1], axis=0),
                                    bounds_check=bound, oob_is_err=False).then_inc(gathered[b], 16)
                pool.wait_ge(cleared, 1)
                rounds(pool, NB // 2, body)

            @block.sync
            def _(sp):
                sp.dma_start(w[:, 0:D], a["head_w"].unsqueeze(0).to_broadcast([P, D])).then_inc(w_loaded, 16)
                sp.dma_start(w[:, D:], a["tail_w"].unsqueeze(0).to_broadcast([P, D])).then_inc(w_loaded, 16)

                def body(i, first, last):
                    for b in range(2):
                        n = 2 * i + b
                        sp.wait_ge(gathered[b], 16 * 2 * K * (i + 1))
                        sp.dma_start(edge_rows[bass.ds(n * P, P), :].rearrange("p (k d) -> p k d", k=K),
                                     g[b][:, :, 0, :]).then_inc(stored[b], 16)
                rounds(sp, NB // 2, body)
                for b in range(2):
                    sp.wait_ge(stored[b], 16 * (NB // 2))
                sp.wait_ge(w_loaded, 32)

            @block.scalar
            def _(act):
                act.wait_ge(cleared, 1)
                pads = scratch[0].shape[0] - N
                for s in scratch:
                    act.dma_start(s[N:N + pads, :], zeros[0:pads, 0:D]).then_inc(zeroed, 16)
                zero_groups = NG // ZB
                with act.Fori(0, zero_groups) as i:
                    act.wait_ge(used, (i + 1) * (NB // zero_groups))
                    for z in range(ZB):
                        act.dma_start(agg[bass.ds((i * ZB + z) * GROUP, GROUP), :].rearrange("(p t) d -> p (t d)", p=P),
                                      zeros[:, :]).then_inc(zeroed, 16)
                act.wait_ge(zeroed, 16 * (zero_groups * ZB + len(scratch)))

            @block.vector
            def _(dve):
                nc.vector.memset(g[0][:], 0.0)
                nc.vector.memset(g[1][:], 0.0)
                nc.vector.memset(zeros[:], 0.0).then_inc(cleared, 1)

                def indices(i, b, free):
                    if free:
                        dve.wait_ge(gathered[b], 16 * 2 * K * i)
                    nc.vector.tensor_copy(idx[b][:, 0, :], t["gidx"][:, bass.ds((2 * i + b) * K, K)])
                    nc.vector.tensor_copy(idx[b][:, 1, :], t["didx"][:, bass.ds((2 * i + b) * K, K)]).then_inc(idx_ready, 1)

                def body(i, first, last):
                    for b in range(2):
                        n = 2 * i + b
                        dve.wait_ge(gathered[b], 16 * 2 * K * (i + 1))
                        if not (first and b == 0):
                            dve.wait_ge(used, n)
                        nc.vector.tensor_tensor(prod[:], g[b][:].rearrange("p k s d -> p k (s d)"),
                                                w[:].unsqueeze(1).to_broadcast([P, K, 2 * D]), ALU.mult).then_inc(multiplied, 1)
                        if not last:
                            indices(i + 1, b, True)
                        dve.wait_ge(multiplied, n + 1)
                        nc.vector.tensor_reduce(t["logit"][:, bass.ds(n * K, K)], prod[:], AX.X, ALU.add).then_inc(used, 1)
                indices(0, 0, False)
                indices(0, 1, False)
                dve.wait_ge(w_loaded, 32)
                rounds(dve, NB // 2, body)
                dve.wait_ge(used, NB)


def softmax_phase(env, a, t):
    nc = env.nc
    E = a["src"].shape[0]
    NT = E // ROWS
    Q = NT // C4
    F = C4 * ROWS
    NR = a["rel_w"].shape[0]
    with env.phase() as ctx:
        lg, ex, fwd, bwd, et = (env.sb(ctx, n, [Q, F]) for n in ("lg", "ex", "fwd", "bwd", "et"))
        w = env.sb(ctx, "w0pad", [Q, C4, ROWS + 1])
        sc = env.sb(ctx, "rel_and_biases", [P, NR + 2])
        psl = env.ps(ctx, "psl", [P, C4, P])
        psw = env.ps(ctx, "psw", [P, C4, P])
        loaded, to_edges, ready, done = (env.sem(n) for n in ("sm_loaded", "sm_to_edges", "sm_ready", "sm_to_rows"))
        shifted, expd, chain = env.sem("sm_shifted"), env.sem("sm_exp"), env.sem("sm_chain")
        seg = SegTotals(env, ctx, Q, F)
        with nc.Block() as block:
            @block.sync
            def _(sp):
                for dram, lo, hi in ((a["rel_w"], 0, NR), (a["head_b"], NR, NR + 1), (a["tail_b"], NR + 1, NR + 2)):
                    sp.dma_start(sc[:, lo:hi], dram.unsqueeze(0).to_broadcast([P, hi - lo])).then_inc(loaded, 16)
                sp.wait_ge(loaded, 48)

            @block.vector
            def _(dve):
                link = Chain(dve, chain)
                dve.wait_ge(to_edges, 1)
                link(nc.vector.tensor_copy(lg[:].rearrange("q (c p) -> q c p", c=C4), psl[0:Q, :, 1:ROWS + 1]))
                link(nc.vector.tensor_copy(et[:], t["etype_i"][:, :]))
                dve.wait_ge(loaded, 48)
                link(nc.vector.tensor_scalar(lg[:], lg[:], sc[0:Q, NR:NR + 1], sc[0:Q, NR + 1:NR + 2], ALU.add, ALU.add))
                for r in range(NR):
                    link(nc.vector.tensor_scalar(ex[:], et[:], float(r), sc[0:Q, r:r + 1], ALU.is_equal, ALU.mult))
                    link(nc.vector.tensor_tensor(lg[:], lg[:], ex[:], ALU.add))
                seg.vector(link, dve, t, lg[:], fwd[:], bwd[:], "max")
                nc.vector.tensor_tensor(lg[:], lg[:], fwd[:], ALU.subtract).then_inc(shifted, 1)
                dve.wait_ge(expd, 1)
                seg.vector(link, dve, t, ex[:], fwd[:], bwd[:], "sum")
                link(nc.vector.reciprocal(fwd[:], fwd[:]))
                link(nc.vector.memset(w[:, :, 0:1], 1.0))
                nc.vector.tensor_tensor(w[:, :, 1:], ex[:].rearrange("q (c p) -> q c p", c=C4),
                                        fwd[:].rearrange("q (c p) -> q c p", c=C4), ALU.mult).then_inc(ready, 1)
                dve.wait_ge(done, 1)
                link(nc.vector.tensor_copy(t["w0"][0:ROWS + 1, :].rearrange("p (q c) -> p c q", c=C4),
                                           psw[0:ROWS + 1, :, 0:Q]))

            @block.scalar
            def _(act):
                act.wait_ge(shifted, 1)
                nc.scalar.activation(ex[:], lg[:], ACT.Exp).then_inc(expd, 1)

            @block.tensor
            def _(pe):
                by_tile = t["logit"][:].rearrange("p (q c) -> p c q", c=C4)
                for c in range(C4):
                    last = nc.tensor.transpose(psl[0:Q, c, :], by_tile[:, c, :], t["ident"][:])
                last.then_inc(to_edges, 1)
                seg.tensor(pe, t, 0)
                pe.wait_ge(ready, 1)
                for c in range(C4):
                    last = nc.tensor.transpose(psw[0:ROWS + 1, c, 0:Q], w[:, c, :], t["ident"][0:Q, 0:Q])
                last.then_inc(done, 1)


def edge_sums_phase(env, a, t, table, agg, layer, edge_rows):
    nc = env.nc
    N, E = a["x"].shape[0], a["src"].shape[0]
    NB = E // (ROWS * K)
    IT = NB // 2
    R1 = ROWS + 1
    gated, projected = layer == 2, layer == 1
    gathers = layer != 0
    weights = {0: "w0", 1: "w1", 2: None}[layer]
    with env.phase() as ctx:
        g = [env.sb(ctx, f"rows{b}", [P, K, D]) for b in range(2)]
        r = [env.sb(ctx, f"messages{b}", [P, K, D]) for b in range(2)] if gated else g
        s = [env.sb(ctx, f"onehot{b}", [P, K, R1]) for b in range(2)]
        res = [env.sb(ctx, f"sums{b}", [P, K, D]) for b in range(2)]
        gi = [env.sb(ctx, f"gi{b}", [P, K], I32) for b in range(2)]
        si = [env.sb(ctx, f"si{b}", [P, K], I32) for b in range(2)]
        acc = [env.ps(ctx, f"acc{b}", [P, K, D]) for b in range(2)]
        if gated or projected:
            mat = env.sb(ctx, "mat", [P, D])
            rt = [env.sb(ctx, f"transposed{h}", [P, HALF, P]) for h in range(2)]
            pst = env.ps(ctx, "pst", [P, HALF, P])
            psx = env.ps(ctx, "psx", [P, HALF, D])
        if projected:
            raw = env.sb(ctx, "raw_sums", [P, K, D])
        if gated:
            ea = [env.sb(ctx, f"ea{b}", [P, K, a["ea"].shape[1]]) for b in range(2)]
            eat = [env.sb(ctx, f"eat{b}", [P, R1]) for b in range(2)]
            ew = env.sb(ctx, "edge_w_blocks", [P, K, D])
            ews = [env.sb(ctx, f"gates{h}", [P, HALF, D]) for h in range(2)]
            pse = env.ps(ctx, "pse", [P, HALF, D])
            psa = env.ps(ctx, "psa", [P, R1])
            ea_loaded = [env.sem(f"ea_loaded{b}") for b in range(2)]
            ea_transposed, ea_copied, ea_used = env.sem("ea_transposed"), env.sem("ea_copied"), env.sem("ea_used")
            gates_done, gates_copied = env.sem("gates_done"), env.sem("gates_copied")
        S = env.sem
        begun = S("dma_series_begun")
        cleared, idx_ready, onehot_ready = S("cleared"), S("idx_ready"), S("onehot_ready")
        arrived = [S(f"rows_arrived{b}") for b in range(2)]
        scattered = [S(f"scattered{b}") for b in range(2)]
        carried, summed, res_ready = S("carried"), S("tile_summed"), S("sums_ready")
        compared, weighed = S("compared"), S("weighed")
        mats, transposed, tcopied, product, product_used = (
            S("mats_loaded"), S("transposed"), S("transposed_copied"), S("product"), S("product_used"))
        raw_ready = S("raw_ready")
        PER = 16 * (K if gathers else 1)
        EW = a["ea"].shape[1]
        with nc.Block() as block:
            def scatter(pool, bound, n, b):
                if projected:
                    pool.wait_ge(product_used, 2 * n + 2)
                else:
                    pool.wait_ge(res_ready, n + 1)
                pool.sem_inc(begun, 1)
                for k in range(K):
                    pool.indirect_dma_start(
                        out=agg[0:N, :], out_offset=bass.IndirectOffsetOnAxis(ap=si[b][:, k:k + 1], axis=0),
                        in_=res[b][:, k, :], in_offset=None,
                        bounds_check=bound, oob_is_err=False).then_inc(scattered[b], 16)

            @block.gpsimd
            def _(pool):
                bound = pool.to_reg(N - 1)

                def body(i, first, last):
                    for b in range(2):
                        n = 2 * i + b
                        pool.wait_ge(idx_ready, n + 1)
                        if gathers:
                            if not first:
                                if gated:
                                    pool.wait_ge(transposed, 2 * (n - 1))
                                else:
                                    pool.wait_ge(summed, K * (n - 1))
                            pool.sem_inc(begun, 1)
                            for k in range(K):
                                pool.indirect_dma_start(
                                    out=g[b][:, k, :], out_offset=None, in_=table[0:N, :],
                                    in_offset=bass.IndirectOffsetOnAxis(ap=gi[b][:, k:k + 1], axis=0),
                                    bounds_check=bound, oob_is_err=False).then_inc(arrived[b], 16)
                        if not (first and b == 0):
                            scatter(pool, bound, n - 1, 1 - b)
                pool.wait_ge(cleared, 1)
                rounds(pool, IT, body)
                scatter(pool, bound, NB - 1, 1)
                for b in range(2):
                    pool.wait_ge(scattered[b], 16 * K * IT)

            @block.sync
            def _(sp):
                if gated or projected:
                    sp.dma_start(mat[:], (a["W2"] if gated else a["W_neigh"])[:, :]).then_inc(mats, 16)
                if gated:
                    sp.wait_ge(cleared, 1)
                    for k in range(K):
                        sp.dma_start(ew[EW * k:EW * (k + 1), k, :], a["edge_w"][:, :]).then_inc(mats, 16)

                def body(i, first, last):
                    for b in range(2):
                        n = 2 * i + b
                        if not gathers:
                            if not first:
                                sp.wait_ge(summed, K * (n - 1))
                            sp.dma_start(flat(g[b][:]), edge_rows[bass.ds(n * P, P), :]).then_inc(arrived[b], 16)
                        if gated:
                            if not first:
                                sp.wait_ge(ea_transposed, n - 1)
                            e0 = n * (K * ROWS)
                            with nc.allow_non_contiguous_dma(reason="rows of edge attributes"):
                                sp.dma_start(ea[b][0:ROWS, :, :],
                                             a["ea"][bass.ds(e0, K * ROWS), :].rearrange("(k p) j -> p k j", k=K)
                                             ).then_inc(ea_loaded[b], 16)
                if gated or not gathers:
                    if not gathers:
                        sp.wait_ge(cleared, 1)
                    rounds(sp, IT, body)
                if gated or projected:
                    sp.wait_ge(mats, 16 * (1 + (K if gated else 0)))

            @block.tensor
            def _(pe):
                if gated or projected:
                    pe.wait_ge(mats, 16 * (1 + (K if gated else 0)))

                def through_matrix(n, h):
                    pe.wait_ge(tcopied, 2 * n + h + 1)
                    for k in range(HALF):
                        last = nc.tensor.matmul(psx[0:R1, k, :], rt[h][:, k, 0:R1], mat[:], start=True, stop=True)
                    last.then_inc(product, 1)

                def pre(n, i, b, first):
                    pe.wait_ge(arrived[b], PER * (i + 1))
                    pe.wait_ge(ea_loaded[b], 16 * (i + 1))
                    nc.tensor.transpose(psa[:, 0:ROWS], flat(ea[b][0:ROWS, :, :]), t["ident"][0:ROWS, 0:ROWS]
                                        ).then_inc(ea_transposed, 1)
                    for h in range(2):
                        c = 2 * n + h
                        if not (first and b == 0 and h == 0):
                            pe.wait_ge(tcopied, c)
                        for k in range(HALF):
                            last = nc.tensor.transpose(pst[:, k, 0:R1], g[b][0:R1, h * HALF + k, :],
                                                       t["ident"][0:R1, 0:R1])
                        last.then_inc(transposed, 1)
                        if h == 0:
                            pe.wait_ge(ea_copied, n + 1)
                        if not (first and b == 0 and h == 0):
                            pe.wait_ge(gates_copied, c)
                            pe.wait_ge(product_used, c)
                        for k in range(HALF):
                            last = nc.tensor.matmul(pse[0:R1, k, :], eat[b][:, :], ew[:, h * HALF + k, :],
                                                    start=True, stop=True)
                        last.then_inc(gates_done, 1)
                        through_matrix(n, h)

                def sums(n, i, b, first):
                    pe.wait_ge(onehot_ready, n + 1)
                    if not gated:
                        pe.wait_ge(arrived[b], PER * (i + 1))
                    if not first:
                        pe.wait_ge(raw_ready if projected else res_ready, n - 1)
                    for k in range(K):
                        pe.wait_ge(carried, K * n + k + 1)
                        nc.tensor.matmul(acc[b][0:R1, k, :], s[b][0:R1, k, :], r[b][0:R1, k, :],
                                         start=True, stop=True).then_inc(summed, 1)

                def post(n, first):
                    pe.wait_ge(raw_ready, n + 1)
                    for h in range(2):
                        c = 2 * n + h
                        if not (first and h == 0):
                            pe.wait_ge(tcopied, c)
                            pe.wait_ge(product_used, c)
                        for k in range(HALF):
                            last = nc.tensor.transpose(pst[:, k, 0:R1], raw[0:R1, h * HALF + k, :],
                                                       t["ident"][0:R1, 0:R1])
                        last.then_inc(transposed, 1)
                        through_matrix(n, h)

                def body(i, first, last):
                    for b in range(2):
                        n = 2 * i + b
                        if gated:
                            pre(n, i, b, first)
                        sums(n, i, b, first)
                        if projected:
                            post(n, first and b == 0)
                rounds(pe, IT, body)

            @block.scalar
            def _(act):
                def pre(n, i, b, first):
                    act.wait_ge(ea_transposed, n + 1)
                    nc.scalar.copy(eat[b][:, 1:R1], psa[:, 0:ROWS]).then_inc(ea_copied, 1)
                    for h in range(2):
                        c = 2 * n + h
                        act.wait_ge(transposed, c + 1)
                        nc.scalar.copy(rt[h][:, :, 0:R1], pst[:, :, 0:R1]).then_inc(tcopied, 1)
                        act.wait_ge(gates_done, c + 1)
                        if not first:
                            act.wait_ge(product_used, c - 1)
                        nc.scalar.copy(ews[h][0:R1, :, :], pse[0:R1, :, :]).then_inc(gates_copied, 1)

                def carries(n, i, b, last):
                    for k in range(K):
                        act.wait_ge(summed, K * n + k + 1)
                        if k < K - 1:
                            nc.scalar.copy(r[b][0:1, k + 1, :], acc[b][0:1, k, :]).then_inc(carried, 1)
                    if not last and not gated:
                        act.wait_ge(arrived[1 - b], PER * (i + 1 + b))
                        nc.scalar.copy(r[1 - b][0:1, 0, :], acc[b][0:1, K - 1, :]).then_inc(carried, 1)

                def post(n):
                    for h in range(2):
                        act.wait_ge(transposed, 2 * n + h + 1)
                        nc.scalar.copy(rt[h][:, :, 0:R1], pst[:, :, 0:R1]).then_inc(tcopied, 1)

                def body(i, first, last):
                    for b in range(2):
                        n = 2 * i + b
                        if gated:
                            pre(n, i, b, first)
                            if not (first and b == 0):
                                act.wait_ge(product_used, 2 * n + 2)
                                nc.scalar.copy(r[b][0:1, 0, :], acc[1 - b][0:1, K - 1, :]).then_inc(carried, 1)
                        carries(n, i, b, last and b == 1)
                        if projected:
                            post(n)
                act.wait_ge(cleared, 1)
                if not gated:
                    act.wait_ge(arrived[0], PER)
                    nc.scalar.copy(r[0][0:1, 0, :], t["zero"][0:1, :]).then_inc(carried, 1)
                rounds(act, IT, body)

            @block.vector
            def _(dve):
                for b in range(2):
                    nc.vector.memset(g[b][:], 0.0)
                    nc.vector.memset(res[b][:], 0.0)
                    if gated:
                        nc.vector.memset(eat[b][:], 0.0)
                if gated:
                    nc.vector.memset(ew[:], 0.0)
                nc.vector.memset(t["zero"][:], 0.0).then_inc(cleared, 1)

                def prepare(n, i, b, first):
                    at = bass.ds(n * K, K)
                    if not first:
                        if gathers:
                            dve.wait_ge(arrived[b], PER * i)
                        dve.wait_ge(scattered[b], 16 * K * i)
                    if gathers:
                        nc.vector.tensor_copy(gi[b][:], t["gidx"][:, at])
                    nc.vector.tensor_copy(si[b][:], t["sidx"][:, at]).then_inc(idx_ready, 1)
                    if not first:
                        dve.wait_ge(summed, K * (n - 1))
                    row = t["row"][:, at].unsqueeze(2).to_broadcast([P, K, ROWS])
                    cols = t["cols"][:, 1:R1].unsqueeze(1).to_broadcast([P, K, ROWS])
                    one = nc.vector.tensor_tensor(s[b][:, :, 1:R1], row, cols, ALU.is_equal)
                    if weights:
                        one.then_inc(compared, 1)
                        nc.vector.tensor_tensor(s[b][:, :, 0:1], t["nx"][:, at].unsqueeze(2),
                                                t[weights][:, at].unsqueeze(2), ALU.mult)
                        dve.wait_ge(compared, n + 1)
                        nc.vector.tensor_tensor(s[b][:, :, 1:R1], s[b][:, :, 1:R1],
                                                t[weights][:, at].unsqueeze(2).to_broadcast([P, K, ROWS]),
                                                ALU.mult).then_inc(onehot_ready, 1)
                    else:
                        nc.vector.tensor_copy(s[b][:, :, 0:1], t["nx"][:, at].unsqueeze(2)).then_inc(onehot_ready, 1)

                def gate(n, b, first):
                    if not first:
                        dve.wait_ge(summed, K * (n - 1))
                    for h in range(2):
                        c = 2 * n + h
                        dve.wait_ge(product, c + 1)
                        dve.wait_ge(gates_copied, c + 1)
                        nc.vector.tensor_tensor(r[b][0:R1, h * HALF:(h + 1) * HALF, :], psx[0:R1, :, :],
                                                ews[h][0:R1, :, :], ALU.mult).then_inc(product_used, 1)

                def finish(n, b, free, final=False):
                    dve.wait_ge(summed, K * (n + 1))
                    if not gated and not final:
                        dve.wait_ge(carried, K * (n + 1) + 1)
                    if projected:
                        if free:
                            dve.wait_ge(transposed, 2 * n)
                        nc.vector.tensor_copy(flat(raw[0:R1, :, :]), flat(acc[b][0:R1, :, :])).then_inc(raw_ready, 1)
                        for h in range(2):
                            dve.wait_ge(product, 2 * n + h + 1)
                            nc.vector.tensor_copy(res[b][0:R1, h * HALF:(h + 1) * HALF, :], psx[0:R1, :, :]
                                                  ).then_inc(product_used, 1)
                    else:
                        nc.vector.tensor_copy(flat(res[b][0:R1, :, :]), flat(acc[b][0:R1, :, :])).then_inc(res_ready, 1)

                def body(i, first, last):
                    for b in range(2):
                        n = 2 * i + b
                        prepare(n, i, b, first)
                        if not (first and b == 0):
                            finish(n - 1, 1 - b, not (first and b == 1))
                        if gated:
                            gate(n, b, first)
                            if first and b == 0:
                                dve.wait_ge(product_used, 2)
                                nc.vector.memset(r[0][0:1, 0, :], 0.0).then_inc(carried, 1)
                rounds(dve, IT, body)
                finish(NB - 1, 1, True, final=True)


def layer3_constants_phase(env, a, t):
    nc = env.nc
    with env.phase() as ctx:
        loaded, chain = env.sem("l3_loaded"), env.sem("l3_chain")
        w = [env.sb(ctx, f"w{l}", [P, D]) for l in range(2)]
        bl = [env.sb(ctx, f"bl{l}", [P, D]) for l in range(2)]
        bcol = [env.sb(ctx, f"bcol{l}", [P, 1]) for l in range(2)]
        cw = [env.sb(ctx, f"cw{l}", [P, 4]) for l in range(2)]
        cb = [env.sb(ctx, f"cb{l}", [P, 1]) for l in range(2)]
        scw = env.sb(ctx, "sum_cw", [P, 2])
        col = env.sb(ctx, "blank_column", [P, 2])
        diag = env.sb(ctx, "diag", [P, 2, D])
        prod = env.sb(ctx, "prod", [P, D])
        ps = env.ps(ctx, "ps", [P, 2, D])
        ready, spread = env.sem("l3_diag_ready"), env.sem("l3_spread")
        N_LOADS = 8 * 2
        with nc.Block() as block:
            @block.sync
            def _(sp):
                for l in range(2):
                    sp.dma_start(w[l][:], a[f"W3_{l}"][:, :]).then_inc(loaded, 16)
                    sp.dma_start(bl[l][:], a[f"blank{l}"].unsqueeze(0).to_broadcast([P, D])).then_inc(loaded, 16)
                    sp.dma_start(bcol[l][:], a[f"b{l}"].unsqueeze(1)).then_inc(loaded, 16)
                    sp.dma_start(cw[l][:], a[f"cw{l}"].unsqueeze(0).to_broadcast([P, 4])).then_inc(loaded, 16)
                    sp.dma_start(cb[l][:], a[f"cb{l}"].unsqueeze(0).to_broadcast([P, 1])).then_inc(loaded, 16)
                    sp.dma_start(t[f"a{l}"][:], a[f"a{l}"].unsqueeze(0).to_broadcast([P, 1])).then_inc(loaded, 16)
                    sp.dma_start(t[f"g{l}"][:], a[f"g{l}"].unsqueeze(0).to_broadcast([P, D])).then_inc(loaded, 16)
                    sp.dma_start(t[f"be{l}"][:], a[f"be{l}"].unsqueeze(0).to_broadcast([P, D])).then_inc(loaded, 16)
                sp.wait_ge(loaded, 16 * N_LOADS)

            @block.vector
            def _(dve):
                link = Chain(dve, chain)
                nc.vector.memset(t["ones"][:], 1.0)
                for k in range(1, 4):
                    nc.vector.tensor_scalar(t["shift"][:, k - 1, :], t["cols"][:], float(k), t["part"][:, 0:1],
                                            ALU.add, ALU.is_equal)
                dve.wait_ge(loaded, 16 * N_LOADS)
                for l in range(2):
                    for k in range(4):
                        nc.vector.tensor_scalar(t[f"cwi{l}"][:, k, :], t["ident"][:], cw[l][:, k:k + 1], None, ALU.mult)
                    link(nc.vector.tensor_tensor(prod[:], w[l][:], bl[l][:], ALU.mult))
                    link(nc.vector.tensor_reduce(col[:, l:l + 1], prod[:], AX.X, ALU.add))
                    link(nc.vector.tensor_tensor(col[:, l:l + 1], col[:, l:l + 1], bcol[l][:], ALU.add))
                    link(nc.vector.tensor_reduce(scw[:, l:l + 1], cw[l][:], AX.X, ALU.add))
                    nc.vector.tensor_scalar(diag[:, l, :], t["ident"][:], col[:, l:l + 1], None, ALU.mult).then_inc(ready, 1)
                dve.wait_ge(spread, 1)
                for l in range(2):
                    link(nc.vector.tensor_copy(t[f"bp{l}"][:], ps[:, l, :]))
                    link(nc.vector.tensor_scalar(t[f"c{l}"][:], t[f"bp{l}"][:], scw[:, l:l + 1], cb[l][:, 0:1],
                                                 ALU.mult, ALU.add))

            @block.tensor
            def _(pe):
                pe.wait_ge(ready, 2)
                for l in range(2):
                    last = nc.tensor.matmul(ps[:, l, :], t["ones"][:], diag[:, l, :], start=True, stop=True)
                last.then_inc(spread, 1)


def edge_sorts_phase(env, a, t, table, agg, l):
    nc = env.nc
    N, E = a["x"].shape[0], a["src"].shape[0]
    NB = E // (ROWS * K)
    IT = NB // 2
    with env.phase() as ctx:
        g = [env.sb(ctx, f"rows{b}", [P, K, D]) for b in range(2)]
        v = [env.sb(ctx, f"slots{b}", [P, 4, K, D]) for b in range(2)]
        mn, mx = (env.sb(ctx, n, [P, 2, K, D]) for n in ("pair_min", "pair_max"))
        mid = [env.sb(ctx, f"middle{b}", [P, 2, K, D]) for b in range(2)]
        res = [env.sb(ctx, f"res{b}", [P, K, D]) for b in range(2)]
        gi = [env.sb(ctx, f"gi{b}", [P, K], I32) for b in range(2)]
        si = [env.sb(ctx, f"si{b}", [P, K], I32) for b in range(2)]
        has = [env.sb(ctx, f"has{b}", [P, 3, K]) for b in range(2)]
        psv = [env.ps(ctx, f"psv{j}", [P, HALF, D]) for j in range(4)]
        psw = [env.ps(ctx, f"psw{h}", [P, HALF, D]) for h in range(2)]
        S = env.sem
        begun = S("dma_series_begun")
        cleared, idx_ready, blanked = S("cleared"), S("idx_ready"), S("rows_less_blank")
        gathered = [S(f"gathered{b}") for b in range(2)]
        scattered = [S(f"scattered{b}") for b in range(2)]
        shifted, masked, pairs, ends, ordered = S("shifted"), S("masked"), S("pairs"), S("ends"), S("ordered")
        weighted, res_ready = S("weighted"), S("res_ready")
        with nc.Block() as block:
            @block.gpsimd
            def _(pool):
                bound = pool.to_reg(N - 1)

                def scatter(n, b):
                    pool.wait_ge(res_ready, 2 * n + 2)
                    pool.sem_inc(begun, 1)
                    for k in range(K):
                        pool.indirect_dma_start(
                            out=agg[0:N, :], out_offset=bass.IndirectOffsetOnAxis(ap=si[b][:, k:k + 1], axis=0),
                            in_=res[b][:, k, :], in_offset=None,
                            bounds_check=bound, oob_is_err=False).then_inc(scattered[b], 16)

                def body(i, first, last):
                    for b in range(2):
                        n = 2 * i + b
                        pool.wait_ge(idx_ready, n + 1)
                        if not first:
                            pool.wait_ge(blanked, n - 1)
                        pool.sem_inc(begun, 1)
                        for k in range(K):
                            pool.indirect_dma_start(
                                out=g[b][:, k, :], out_offset=None, in_=table[0:N, :],
                                in_offset=bass.IndirectOffsetOnAxis(ap=gi[b][:, k:k + 1], axis=0),
                                bounds_check=bound, oob_is_err=False).then_inc(gathered[b], 16)
                        if not (first and b == 0):
                            scatter(n - 1, 1 - b)
                pool.wait_ge(cleared, 1)
                rounds(pool, IT, body)
                scatter(NB - 1, 1)
                for b in range(2):
                    pool.wait_ge(scattered[b], 16 * K * IT)

            @block.vector
            def _(dve):
                nc.vector.memset(g[0][:], 0.0)
                nc.vector.memset(g[1][:], 0.0).then_inc(cleared, 1)

                def indices(n, i, b, first):
                    at = bass.ds(n * K, K)
                    if not first:
                        dve.wait_ge(gathered[b], 16 * K * i)
                        dve.wait_ge(scattered[b], 16 * K * i)
                        dve.wait_ge(masked, 6 * (n - 1))
                    for k in range(3):
                        nc.vector.tensor_copy(has[b][:, k, :], t[f"has{k + 1}"][:, at])
                    nc.vector.tensor_copy(gi[b][:], t["gidx3"][:, at])
                    nc.vector.tensor_copy(si[b][:], t["sidx3"][:, at]).then_inc(idx_ready, 1)

                def less_blank(n, i, b, first):
                    dve.wait_ge(gathered[b], 16 * K * (i + 1))
                    if not first:
                        dve.wait_ge(weighted, 2 * (n - 1))
                    nc.vector.tensor_tensor(v[b][:, 0, :, :], g[b][:],
                                            t[f"bp{l}"][:].unsqueeze(1).to_broadcast([P, K, D]),
                                            ALU.subtract).then_inc(blanked, 1)

                def sort(n, b, first):
                    dve.wait_ge(masked, 6 * (n + 1))
                    if not first:
                        dve.wait_ge(ordered, n)
                    nc.vector.tensor_tensor(mn[:], v[b][:, 0:4:2, :, :], v[b][:, 1:4:2, :, :], ALU.min)
                    nc.vector.tensor_tensor(mx[:], v[b][:, 0:4:2, :, :], v[b][:, 1:4:2, :, :], ALU.max).then_inc(pairs, 1)
                    dve.wait_ge(pairs, n + 1)
                    nc.vector.tensor_tensor(v[b][:, 1, :, :], mn[:, 0, :, :], mn[:, 1, :, :], ALU.max)
                    nc.vector.tensor_tensor(v[b][:, 2, :, :], mx[:, 0, :, :], mx[:, 1, :, :], ALU.min).then_inc(ends, 1)
                    nc.vector.tensor_tensor(v[b][:, 0, :, :], mn[:, 0, :, :], mn[:, 1, :, :], ALU.min)
                    nc.vector.tensor_tensor(v[b][:, 3, :, :], mx[:, 0, :, :], mx[:, 1, :, :], ALU.max)
                    dve.wait_ge(ends, n + 1)
                    nc.vector.tensor_tensor(mid[b][:, 0, :, :], v[b][:, 1, :, :], v[b][:, 2, :, :], ALU.min)
                    nc.vector.tensor_tensor(mid[b][:, 1, :, :], v[b][:, 1, :, :], v[b][:, 2, :, :], ALU.max
                                            ).then_inc(ordered, 1)

                def body(i, first, last):
                    for b in range(2):
                        n = 2 * i + b
                        less_blank(n, i, b, first)
                        if not (first and b == 0):
                            sort(n - 1, 1 - b, first and b == 1)
                            if not (last and b == 1):
                                indices(n + 1, i + b, 1 - b, False)
                indices(0, 0, 0, True)
                indices(1, 0, 1, True)
                rounds_from_one(dve, IT, body)
                sort(NB - 1, 1, False)

            @block.tensor
            def _(pe):
                def body(i, first, last):
                    for b in range(2):
                        n = 2 * i + b
                        pe.wait_ge(blanked, n + 1)
                        for k in range(3):
                            for h in range(2):
                                j = 2 * k + h
                                if not (first and b == 0 and j < 4):
                                    pe.wait_ge(masked, 6 * n + j - 3)
                                nc.tensor.matmul(psv[(6 * b + j) % 4][:].rearrange("p k d -> p (k d)"),
                                                 t["shift"][:, k, :], flat(v[b][:, 0, h * HALF:(h + 1) * HALF, :]),
                                                 start=True, stop=True).then_inc(shifted, 1)
                        if not (first and b == 0):
                            weigh(pe, n - 1, 1 - b, first)

                def weigh(pe, n, b, first):
                    pe.wait_ge(ordered, n + 1)
                    for h in range(2):
                        if not first:
                            pe.wait_ge(res_ready, 2 * n + h - 1)
                        part = slice(h * HALF, (h + 1) * HALF)
                        parts = [v[b][:, 0, part, :], mid[b][:, 0, part, :], mid[b][:, 1, part, :], v[b][:, 3, part, :]]
                        for k, s in enumerate(parts):
                            last = nc.tensor.matmul(flat(psw[h][:]), t[f"cwi{l}"][:, k, :], flat(s),
                                                    start=(k == 0), stop=(k == 3))
                        last.then_inc(weighted, 1)
                rounds(pe, IT, body)
                weigh(pe, NB - 1, 1, False)

            @block.scalar
            def _(act):
                def out(n, i, b, free):
                    for h in range(2):
                        act.wait_ge(weighted, 2 * n + h + 1)
                        if free and h == 0:
                            act.wait_ge(scattered[b], 16 * K * i)
                        nc.scalar.copy(res[b][:, h * HALF:(h + 1) * HALF, :], psw[h][:]).then_inc(res_ready, 1)

                def body(i, first, last):
                    for b in range(2):
                        n = 2 * i + b
                        for k in range(3):
                            for h in range(2):
                                j = 2 * k + h
                                act.wait_ge(shifted, 6 * n + j + 1)
                                for q in range(HALF):
                                    ins = nc.scalar.activation(v[b][:, k + 1, h * HALF + q, :],
                                                               psv[(6 * b + j) % 4][:, q, :], ACT.Copy,
                                                               scale=has[b][:, k, h * HALF + q:h * HALF + q + 1])
                                ins.then_inc(masked, 1)
                        if not (first and b == 0):
                            out(n - 1, i if b == 1 else i - 1, 1 - b, not first)
                rounds_from_one(act, IT, body)
                out(NB - 1, IT - 1, 1, True)


def rounds_from_one(engine, n, body):
    body(0, True, False)
    body(1, False, n == 2)
    if n > 3:
        with engine.Fori(2, n - 1) as i:
            body(i, False, False)
    if n > 2:
        body(n - 1, False, True)


def rows_of(dram, tile, n, N, whole):
    if whole:
        return [(dram[bass.ds(n * GROUP, GROUP), :].rearrange("(p t) d -> p (t d)", p=P), flat(tile[:]))]
    r0, left = n * GROUP, N - n * GROUP
    full, part = left // T, left % T
    pairs = [(dram[r0:r0 + full * T, :].rearrange("(p t) d -> p (t d)", p=full), flat(tile[0:full, :, :]))]
    if part:
        pairs.append((dram[r0 + full * T:N, :].unsqueeze(0), tile[full:full + 1, 0:part, :]))
    return pairs


class Loads:

    def __init__(self, env, ctx, arrays, N, NG):
        self.arrays, self.N, self.NG = arrays, N, NG
        self.bufs = {n: [env.sb(ctx, f"{n}{b}", [P, T, D]) for b in range(2)] for n in arrays}
        self.sems = {n: [env.sem(f"{n}_loaded{b}") for b in range(2)] for n in arrays}

    def pairs(self, name, n, b, last):
        dram = self.arrays[name]
        whole = not (last and b == 1) or dram.shape[0] == self.NG * GROUP
        return rows_of(dram, self.bufs[name][b], n, self.N, whole)

    def issue(self, sp, name, n, b, last):
        for dram, tile in self.pairs(name, n, b, last):
            sp.dma_start(tile, dram).then_inc(self.sems[name][b], 16)

    def wait(self, engine, name, i, b, last):
        engine.wait_ge(self.sems[name][b], 16 * i + 16 * len(self.pairs(name, 2 * i + b, b, last)))


def node_norm_phase(env, a, t, layer, arrays, out):
    nc = env.nc
    N = a["x"].shape[0]
    NG = -(-N // GROUP)
    IT = NG // 2
    banks = [(c, min(HALF, T - c)) for c in range(0, T, HALF)]
    NBK = len(banks)
    with env.phase() as ctx:
        ld = Loads(env, ctx, arrays, N, NG)
        xb, ab = ld.bufs["x"], ld.bufs["agg"]
        o = [env.sb(ctx, f"out{b}", [P, T, D]) for b in range(2)]
        st = env.sb(ctx, "stats", [P, T, 6])
        sm = {n: env.sb(ctx, n, [P, T]) for n in ("msum", "mdiff", "m2", "dsq", "v4", "var")}
        std = [env.sb(ctx, f"std{b}", [P, T]) for b in range(2)]
        rstd = [env.sb(ctx, f"rstd{b}", [P, T]) for b in range(2)]
        nbias = [env.sb(ctx, f"nbias{b}", [P, T]) for b in range(2)]
        S = env.sem
        pre_done, summed, var_ready, std_ready, norm_ready = (
            S("pool_done"), S("residual_summed"), S("variance_ready"), S("std_ready"), S("factors_ready"))
        pool_step, chain, normed = S("pool_step"), S("vector_chain"), S("normalised")
        stored = [S(f"out_stored{b}") for b in range(2)]
        consts = S("consts_loaded")
        if layer in (1, 2):
            bias = env.sb(ctx, "bias", [P, D])
        if layer == 1:
            wself = env.sb(ctx, "w_self", [P, D])
            xt = [env.sb(ctx, f"xt{j}", [P, HALF, P]) for j in range(2)]
            pst = [env.ps(ctx, f"pst{j}", [P, HALF, P]) for j in range(2)]
            psx = [env.ps(ctx, f"psx{j}", [P, HALF, D]) for j in range(2)]
            xtr, xcp, prod, added = S("x_transposed"), S("x_copied"), S("x_times_w"), S("product_added")
        NCONST = {0: 0, 1: 2, 2: 1, 3: 0}[layer]
        sum_buf = ld.bufs["x4"] if layer == 3 else xb
        with nc.Block() as block:
            @block.sync
            def _(sp):
                if layer in (1, 2):
                    sp.dma_start(bias[:], a[f"b_{layer}"].unsqueeze(0).to_broadcast([P, D])).then_inc(consts, 16)
                if layer == 1:
                    sp.dma_start(wself[:], a["W_self"][:, :]).then_inc(consts, 16)

                def body(i, first, last):
                    for b in range(2):
                        n = 2 * i + b
                        if not first:
                            sp.wait_ge(normed, n - 1)
                        for name in arrays:
                            ld.issue(sp, name, n, b, last)
                rounds_from_one(sp, IT, body)
                if NCONST:
                    sp.wait_ge(consts, 16 * NCONST)

            @block.gpsimd
            def _(pool):
                if layer == 0:
                    return

                def body(i, first, last):
                    for b in range(2):
                        n = 2 * i + b
                        ld.wait(pool, "agg", i, b, last)
                        if layer == 3:
                            nc.gpsimd.tensor_tensor(ab[b][:], ab[b][:], t["bn_scale"][:].unsqueeze(1).to_broadcast([P, T, D]),
                                                    ALU.mult).then_inc(pool_step, 1)
                            ld.wait(pool, "x", i, b, last)
                            pool.wait_ge(pool_step, n + 1)
                            nc.gpsimd.tensor_tensor(ab[b][:], ab[b][:], xb[b][:], ALU.add).then_inc(pre_done, 1)
                        else:
                            nc.gpsimd.tensor_tensor(ab[b][:], ab[b][:], bias[:].unsqueeze(1).to_broadcast([P, T, D]),
                                                    ALU.add).then_inc(pre_done, 1)
                if NCONST:
                    pool.wait_ge(consts, 16 * NCONST)
                rounds(pool, IT, body)

            if layer == 1:
                @block.tensor
                def _(pe):
                    pe.wait_ge(consts, 16 * NCONST)

                    def body(i, first, last):
                        for b in range(2):
                            n = 2 * i + b
                            ld.wait(pe, "x", i, b, last)

                            def times_w(j):
                                c, w = banks[j]
                                q = NBK * n + j
                                pe.wait_ge(xcp, q + 1)
                                if not (first and NBK * b + j < 2):
                                    pe.wait_ge(added, q - 1)
                                for k in range(w):
                                    m = nc.tensor.matmul(psx[(NBK * b + j) % 2][:, k, :], xt[(NBK * b + j) % 2][:, k, :],
                                                         wself[:], start=True, stop=True)
                                m.then_inc(prod, 1)
                            for j, (c, w) in enumerate(banks):
                                q = NBK * n + j
                                if not (first and NBK * b + j < 2):
                                    pe.wait_ge(xcp, q - 1)
                                for k in range(w):
                                    m = nc.tensor.transpose(pst[(NBK * b + j) % 2][:, k, :], xb[b][:, c + k, :], t["ident"][:])
                                m.then_inc(xtr, 1)
                                if j:
                                    times_w(j - 1)
                            times_w(NBK - 1)
                    rounds(pe, IT, body)

            @block.vector
            def _(dve):
                if NCONST:
                    dve.wait_ge(consts, 16 * NCONST)
                LINKS = 5 + (2 if layer == 3 else 0)

                def body(i, first, last):
                    link = Chain(dve, chain, 2 * LINKS * i)
                    for b in range(2):
                        n = 2 * i + b
                        x, s = xb[b], sum_buf[b]
                        for name in arrays:
                            ld.wait(dve, name, i, b, last)
                        if layer == 3:
                            link(nc.vector.tensor_tensor(s[:], s[:], t["bn_alpha"][:].unsqueeze(1).to_broadcast([P, T, D]), ALU.mult))
                            link(nc.vector.tensor_tensor(s[:], s[:], t["bn_shift"][:].unsqueeze(1).to_broadcast([P, T, D]), ALU.add))
                        if layer:
                            dve.wait_ge(pre_done, n + 1)
                        if layer == 1:
                            s = ab[b]
                            link(nc.vector.tensor_tensor(s[:], x[:], ab[b][:], ALU.add))
                            for j, (c, w) in enumerate(banks):
                                dve.wait_ge(prod, NBK * n + j + 1)
                                nc.vector.tensor_tensor(s[:, c:c + w, :], s[:, c:c + w, :],
                                                        psx[(NBK * b + j) % 2][:, 0:w, :], ALU.add).then_inc(added, 1)
                            dve.wait_ge(added, NBK * (n + 1))
                        else:
                            link(nc.vector.tensor_tensor(s[:], s[:], ab[b][:], ALU.add))
                        for k in range(T):
                            ins = nc.vector.bn_stats(st[:, k, :], s[:, k, :])
                        link(ins)
                        nc.vector.tensor_tensor(sm["msum"][:], st[:, :, 1], st[:, :, 4], ALU.add)
                        nc.vector.tensor_tensor(sm["m2"][:], st[:, :, 2], st[:, :, 5], ALU.add)
                        link(nc.vector.tensor_tensor(sm["mdiff"][:], st[:, :, 1], st[:, :, 4], ALU.subtract))
                        nc.vector.tensor_scalar(sm["v4"][:], sm["m2"][:], 1.0 / D, EPS, ALU.mult, ALU.add)
                        link(nc.vector.scalar_tensor_tensor(sm["dsq"][:], sm["mdiff"][:], 0.25, sm["mdiff"][:],
                                                            ALU.mult, ALU.mult))
                        nc.vector.tensor_tensor(sm["var"][:], sm["v4"][:], sm["dsq"][:], ALU.add).then_inc(var_ready, 1)
                        dve.wait_ge(std_ready, n + 1)
                        link(nc.vector.reciprocal(rstd[b][:], std[b][:]))
                        nc.vector.scalar_tensor_tensor(nbias[b][:], sm["msum"][:], -0.5, rstd[b][:],
                                                       ALU.mult, ALU.mult).then_inc(norm_ready, 1)
                    assert link.n == 2 * LINKS, link.n
                rounds(dve, IT, body)

            @block.scalar
            def _(act):
                def body(i, first, last):
                    for b in range(2):
                        n = 2 * i + b
                        if layer == 1:
                            for j, (c, w) in enumerate(banks):
                                q = NBK * n + j
                                act.wait_ge(xtr, q + 1)
                                if not (first and NBK * b + j < 2):
                                    act.wait_ge(prod, q - 1)
                                nc.scalar.copy(xt[(NBK * b + j) % 2][:, 0:w, :], pst[(NBK * b + j) % 2][:, 0:w, :]).then_inc(xcp, 1)
                        act.wait_ge(var_ready, n + 1)
                        nc.scalar.activation(std[b][:], sm["var"][:], ACT.Sqrt).then_inc(std_ready, 1)
                        act.wait_ge(norm_ready, n + 1)
                        if not first:
                            act.wait_ge(stored[b], 16 * i)
                        s = ab[b] if layer == 1 else sum_buf[b]
                        for k in range(T):
                            ins = nc.scalar.activation(o[b][:, k, :], s[:, k, :], ACT.Identity,
                                                       bias=nbias[b][:, k:k + 1], scale=rstd[b][:, k:k + 1])
                        ins.then_inc(normed, 1)
                        act.wait_ge(normed, n + 1)
                        for dram, tile in rows_of(out, o[b], n, N, not (last and b == 1)):
                            act.dma_start(dram, tile).then_inc(stored[b], 16)
                rounds(act, IT, body)
                act.wait_ge(stored[0], 16 * IT)
                act.wait_ge(stored[1], 16 * (IT - 1) + 16 * len(rows_of(out, o[1], NG - 1, N, False)))


def bn_stats_phase(env, a, t, x, agg, l):
    nc = env.nc
    N = a["x"].shape[0]
    NG = -(-N // GROUP)
    IT = NG // 2
    chunks = [(c, min(HALF, T - c)) for c in range(0, T, HALF)]
    with env.phase() as ctx:
        ld = Loads(env, ctx, {"x": x, "agg": agg}, N, NG)
        xb, ab = ld.bufs["x"], ld.bufs["agg"]
        h = [env.sb(ctx, f"h{b}", [P, T, D]) for b in range(2)]
        sq = [env.sb(ctx, f"sq{b}", [P, T, D]) for b in range(2)]
        acc = env.sb(ctx, "h_sums", [P, T, D])
        acc2 = env.sb(ctx, "sq_sums", [P, HALF, D])
        f = {n: env.sb(ctx, n, [P, D]) for n in ("mean", "ex2", "var", "std", "rstd", "tmp")}
        ps = [env.ps(ctx, f"ps{b}", [P, HALF, D]) for b in range(2)]
        psm = env.ps(ctx, "psm", [P, HALF, D])
        S = env.sem
        h_ready, squared, sq_summed, sq_added, chain = (
            S("h_ready"), S("squared"), S("squares_summed"), S("squares_added"), S("bn_chain"))
        acc_ready, acc_summed, var_ready, std_ready, h_added = (
            S("acc_ready"), S("acc_summed"), S("var_ready"), S("std_ready"), S("h_added"))
        with nc.Block() as block:
            @block.sync
            def _(sp):
                def body(i, first, last):
                    for b in range(2):
                        n = 2 * i + b
                        if not first:
                            sp.wait_ge(h_ready, n - 1)
                        ld.issue(sp, "x", n, b, last)
                        ld.issue(sp, "agg", n, b, last)
                rounds_from_one(sp, IT, body)

            @block.vector
            def _(dve):
                nc.vector.memset(acc[:], 0.0).then_inc(h_added, 1)
                nc.vector.memset(acc2[:], 0.0).then_inc(sq_added, 1)

                def add_squares(n, b):
                    dve.wait_ge(sq_summed, n + 1)
                    dve.wait_ge(sq_added, n + 1)
                    nc.vector.tensor_tensor(acc2[:], acc2[:], ps[b][:], ALU.add).then_inc(sq_added, 1)

                def body(i, first, last):
                    for b in range(2):
                        n = 2 * i + b
                        ld.wait(dve, "x", i, b, last)
                        ld.wait(dve, "agg", i, b, last)
                        if not first:
                            dve.wait_ge(squared, n - 1)
                        nc.vector.scalar_tensor_tensor(h[b][:], xb[b][:], t[f"a{l}"][:, 0:1], ab[b][:],
                                                       ALU.mult, ALU.add).then_inc(h_ready, 1)
                        if not (first and b == 0):
                            add_squares(n - 1, 1 - b)
                        dve.wait_ge(h_ready, n + 1)
                        dve.wait_ge(h_added, n + 1)
                        nc.vector.tensor_tensor(acc[:], acc[:], h[b][:], ALU.add).then_inc(h_added, 1)
                rounds(dve, IT, body)
                add_squares(NG - 1, 1)
                link = Chain(dve, chain)
                dve.wait_ge(sq_added, NG + 1)
                dve.wait_ge(acc_summed, 1)
                link(nc.vector.tensor_reduce(f["mean"][:], psm[:].rearrange("p k d -> p d k"), AX.X, ALU.add))
                link(nc.vector.tensor_reduce(f["ex2"][:], acc2[:].rearrange("p k d -> p d k"), AX.X, ALU.add))
                link(nc.vector.tensor_scalar(f["mean"][:], f["mean"][:], 1.0 / N, None, ALU.mult))
                link(nc.vector.tensor_scalar(f["ex2"][:], f["ex2"][:], 1.0 / N, EPS, ALU.mult, ALU.add))
                link(nc.vector.tensor_tensor(f["tmp"][:], f["mean"][:], f["mean"][:], ALU.mult))
                nc.vector.tensor_tensor(f["var"][:], f["ex2"][:], f["tmp"][:], ALU.subtract).then_inc(var_ready, 1)
                dve.wait_ge(std_ready, 1)
                link(nc.vector.reciprocal(f["rstd"][:], f["std"][:]))
                link(nc.vector.tensor_tensor(t["bn_scale"][:], t[f"g{l}"][:], f["rstd"][:], ALU.mult))
                link(nc.vector.tensor_scalar(t["bn_alpha"][:], t["bn_scale"][:], t[f"a{l}"][:, 0:1], 1.0, ALU.mult, ALU.add))
                link(nc.vector.tensor_tensor(f["mean"][:], f["mean"][:], t[f"c{l}"][:], ALU.add))
                link(nc.vector.tensor_tensor(f["tmp"][:], t[f"c{l}"][:], f["mean"][:], ALU.subtract))
                link(nc.vector.tensor_tensor(f["tmp"][:], f["tmp"][:], t["bn_scale"][:], ALU.mult))
                link(nc.vector.tensor_tensor(t["bn_shift"][:], f["tmp"][:], t[f"be{l}"][:], ALU.add))

            @block.scalar
            def _(act):
                def body(i, first, last):
                    for b in range(2):
                        n = 2 * i + b
                        act.wait_ge(h_ready, n + 1)
                        if not first:
                            act.wait_ge(sq_summed, n - 1)
                        nc.scalar.activation(sq[b][:], h[b][:], ACT.Square).then_inc(squared, 1)
                rounds(act, IT, body)
                act.wait_ge(var_ready, 1)
                nc.scalar.activation(f["std"][:], f["var"][:], ACT.Sqrt).then_inc(std_ready, 1)

            @block.tensor
            def _(pe):
                def body(i, first, last):
                    for b in range(2):
                        n = 2 * i + b
                        pe.wait_ge(squared, n + 1)
                        if not first:
                            pe.wait_ge(sq_added, n)
                        for c, w in chunks:
                            m = nc.tensor.matmul(flat(ps[b][:, 0:w, :]), t["ones"][:], flat(sq[b][:, c:c + w, :]),
                                                 start=(c == 0), stop=(c + w == T))
                        m.then_inc(sq_summed, 1)
                rounds(pe, IT, body)
                pe.wait_ge(h_added, NG + 1)
                for c, w in chunks:
                    m = nc.tensor.matmul(flat(psm[:, 0:w, :]), t["ones"][:], flat(acc[:, c:c + w, :]),
                                         start=(c == 0), stop=(c + w == T))
                m.then_inc(acc_summed, 1)


def bn_apply_phase(env, a, t, x, agg, out):
    nc = env.nc
    N = a["x"].shape[0]
    NG = -(-N // GROUP)
    IT = NG // 2
    with env.phase() as ctx:
        ld = Loads(env, ctx, {"x": x, "agg": agg}, N, NG)
        xb, ab = ld.bufs["x"], ld.bufs["agg"]
        o = [env.sb(ctx, f"o{b}", [P, T, D]) for b in range(2)]
        S = env.sem
        scaled, chain, done = S("agg_scaled"), S("apply_chain"), S("apply_done")
        stored = [S(f"apply_stored{b}") for b in range(2)]
        with nc.Block() as block:
            @block.sync
            def _(sp):
                def body(i, first, last):
                    for b in range(2):
                        n = 2 * i + b
                        if not first:
                            sp.wait_ge(done, n - 1)
                        ld.issue(sp, "x", n, b, last)
                        ld.issue(sp, "agg", n, b, last)
                rounds_from_one(sp, IT, body)

            @block.gpsimd
            def _(pool):
                def body(i, first, last):
                    for b in range(2):
                        ld.wait(pool, "agg", i, b, last)
                        nc.gpsimd.tensor_tensor(ab[b][:], ab[b][:], t["bn_scale"][:].unsqueeze(1).to_broadcast([P, T, D]),
                                                ALU.mult).then_inc(scaled, 1)
                rounds(pool, IT, body)

            @block.vector
            def _(dve):
                def body(i, first, last):
                    link = Chain(dve, chain, 4 * i)
                    for b in range(2):
                        n = 2 * i + b
                        ld.wait(dve, "x", i, b, last)
                        if not first:
                            dve.wait_ge(stored[b], 16 * i)
                        link(nc.vector.tensor_tensor(o[b][:], xb[b][:], t["bn_alpha"][:].unsqueeze(1).to_broadcast([P, T, D]), ALU.mult))
                        link(nc.vector.tensor_tensor(o[b][:], o[b][:], t["bn_shift"][:].unsqueeze(1).to_broadcast([P, T, D]), ALU.add))
                        dve.wait_ge(scaled, n + 1)
                        nc.vector.tensor_tensor(o[b][:], o[b][:], ab[b][:], ALU.add).then_inc(done, 1)
                rounds(dve, IT, body)

            @block.scalar
            def _(act):
                def body(i, first, last):
                    for b in range(2):
                        n = 2 * i + b
                        act.wait_ge(done, n + 1)
                        for dram, tile in rows_of(out, o[b], n, N, not (last and b == 1)):
                            act.dma_start(dram, tile).then_inc(stored[b], 16)
                rounds(act, IT, body)
                act.wait_ge(stored[0], 16 * IT)
                act.wait_ge(stored[1], 16 * (IT - 1) + 16 * len(rows_of(out, o[1], NG - 1, N, False)))


def gnn_program(nc, a, out):
    N, E = a["x"].shape[0], a["src"].shape[0]
    NT = E // ROWS
    NPAD = -(-N // GROUP) * GROUP
    Q, F = NT // C4, C4 * ROWS
    x1, x2, x3, x4, agg = (nc.dram_tensor(n, (NPAD, D), F32).ap() for n in ("x1", "x2", "x3", "x4", "agg"))
    edge_rows = nc.dram_tensor("edge_rows", (NT // K * P, K * D), F32).ap()
    with ExitStack() as ctx:
        env = Env(nc, ctx)
        t = {}
        for n in ("gidx", "didx", "sidx", "gidx3", "sidx3"):
            t[n] = env.sb(ctx, n, [P, NT], I32)
        for n in ("row", "nx", "w0", "w1", "has1", "has2", "has3", "logit"):
            t[n] = env.sb(ctx, n, [P, NT])
        for n in ("same", "nsame", "sadd", "nadd"):
            t[n] = env.sb(ctx, n, [Q, F])
        t["etype_i"] = env.sb(ctx, "etype_i", [Q, F], I32)
        t["thru"] = env.sb(ctx, "thru", [Q, 4])
        t["one"] = env.sb(ctx, "one", [1, 1])
        t["zero"] = env.sb(ctx, "zero", [1, D])
        t["part"] = env.sb(ctx, "part", [P, 1])
        for n in ("cols", "ident", "ones", "bn_scale", "bn_alpha", "bn_shift", "g0", "g1", "be0", "be1", "bp0", "bp1", "c0", "c1"):
            t[n] = env.sb(ctx, n, [P, P])
        for l in range(2):
            t[f"a{l}"] = env.sb(ctx, f"a{l}", [P, 1])
            t[f"cwi{l}"] = env.sb(ctx, f"cwi{l}", [P, 4, P])
        t["shift"] = env.sb(ctx, "shift", [P, 3, P])

        tables_phase(env, a, t)
        layer3_constants_phase(env, a, t)
        logits_phase(env, a, t, edge_rows, agg, [x1, x2, x3, x4])
        softmax_phase(env, a, t)
        edge_sums_phase(env, a, t, None, agg, 0, edge_rows)
        node_norm_phase(env, a, t, 0, {"x": a["x"], "agg": agg}, x1)
        edge_sums_phase(env, a, t, x1, agg, 1, None)
        node_norm_phase(env, a, t, 1, {"x": x1, "agg": agg}, x2)
        edge_sums_phase(env, a, t, x2, agg, 2, None)
        node_norm_phase(env, a, t, 2, {"x": x2, "agg": agg}, x3)
        edge_sorts_phase(env, a, t, x3, agg, 0)
        bn_stats_phase(env, a, t, x3, agg, 0)
        bn_apply_phase(env, a, t, x3, agg, x4)
        edge_sorts_phase(env, a, t, x4, agg, 1)
        bn_stats_phase(env, a, t, x4, agg, 1)
        node_norm_phase(env, a, t, 3, {"x": x3, "x4": x4, "agg": agg}, out)


_NAMES = {
    "x": "x", "src": "src", "dst": "dst", "edge_attr_16": "ea", "edge_type_8": "etype",
    "L0_gnn_head_w": "head_w", "L0_gnn_head_b": "head_b", "L0_gnn_tail_w": "tail_w", "L0_gnn_tail_b": "tail_b",
    "L0_gnn_rel_w": "rel_w", "L1_gnn_W_self": "W_self", "L1_gnn_W_neigh": "W_neigh", "L1_gnn_b": "b_1",
    "L2_gnn_W": "W2", "L2_gnn_edge_w": "edge_w", "L2_gnn_b": "b_2",
    "L3_gnn_W0": "W3_0", "L3_gnn_b0": "b0", "L3_gnn_cw0": "cw0", "L3_gnn_cb0": "cb0", "L3_gnn_a0": "a0",
    "L3_gnn_g0": "g0", "L3_gnn_be0": "be0", "L3_gnn_blank0": "blank0",
    "L3_gnn_W1": "W3_1", "L3_gnn_b1": "b1", "L3_gnn_cw1": "cw1", "L3_gnn_cb1": "cb1", "L3_gnn_a1": "a1",
    "L3_gnn_g1": "g1", "L3_gnn_be1": "be1", "L3_gnn_blank1": "blank1",
}


def kernel(**inputs):
    import numpy as _np
    import concourse.bacc as _bacc
    from concourse import mybir as _mybir
    from concourse.bass_utils import run_bass_kernel_spmd as _run

    nc = _bacc.Bacc("TRN2", target_bir_lowering=False, num_devices=1)
    arrays, args = {}, {}
    for name, short in _NAMES.items():
        v = _np.ascontiguousarray(inputs[name])
        arrays[f"in_{name}"] = v
        args[short] = nc.dram_tensor(f"in_{name}", v.shape, _mybir.dt.from_np(v.dtype), kind="ExternalInput").ap()
    out = nc.dram_tensor("out_x", inputs["x"].shape, _mybir.dt.float32, kind="ExternalOutput").ap()
    gnn_program(nc, args, out)
    r = _run(nc, [arrays], core_ids=[0])
    return r.results[0]["out_x"]
```

```python
import concourse.bass as bass
from concourse import mybir
from contextlib import ExitStack, contextmanager

F32, I32 = mybir.dt.float32, mybir.dt.int32
ALU, ACT, AX = mybir.AluOpType, mybir.ActivationFunctionType, mybir.AxisListType

P = 128
D = 128
ROWS = 125
K = 8
HALF = K // 2
T = 17
GROUP = P * T
C4 = 4
SKIP = 1 << 23
LOW = -1.0e30
EPS = 1e-5


class Chain:

    def __init__(self, engine, sem, base=0):
        self.engine, self.sem, self.base, self.n = engine, sem, base, 0

    def __call__(self, ins):
        self.n += 1
        ins.then_inc(self.sem, 1)
        self.engine.wait_ge(self.sem, self.base + self.n)


class Env:

    def __init__(self, nc, ctx):
        self.nc, self.ctx, self.count, self.sems = nc, ctx, 0, []

    def sem(self, name):
        self.count += 1
        self.sems.append(self.nc.alloc_semaphore(name=f"{name}_{self.count}"))
        return self.sems[-1]

    @contextmanager
    def phase(self):
        with ExitStack() as ctx:
            yield ctx
        self.nc.clear_and_free_semaphores(self.sems)
        self.nc.all_engine_barrier()
        self.sems = []

    def sb(self, ctx, name, shape, dt=F32):
        self.count += 1
        return ctx.enter_context(self.nc.sbuf_tensor(f"{name}_{self.count}", shape, dt))

    def ps(self, ctx, name, shape):
        self.count += 1
        return ctx.enter_context(self.nc.psum_tensor(f"{name}_{self.count}", shape, F32))


def wait_past(engine, sem, value):
    if not isinstance(value, int) or value > 0:
        engine.wait_ge(sem, value)


def flat(ap):
    return ap.rearrange("p a b -> p (a b)")


def rounds(engine, n, body):
    body(0, True, False)
    if n > 2:
        with engine.Fori(1, n - 1) as i:
            body(i, False, False)
    body(n - 1, False, True)


def tables_phase(env, a, t):
    nc = env.nc
    E = a["src"].shape[0]
    NT = E // ROWS
    Q = NT // C4
    F = C4 * ROWS
    with env.phase() as ctx:
        dsti = env.sb(ctx, "dsti", [Q, F + 4], I32)
        srci = env.sb(ctx, "srci", [Q, F + 4], I32)
        dst = env.sb(ctx, "dst", [Q, F + 4])
        src = env.sb(ctx, "src", [Q, F + 4])
        wk = {n: env.sb(ctx, n, [Q, F]) for n in
              ("head", "lhead", "pos", "dstm", "tmp", "ones", "fwd", "bwd", "has1", "has2", "has3", "sidx3", "headpos")}
        pad = {n: env.sb(ctx, n, [Q, C4, ROWS + 1]) for n in ("gidx", "didx", "sidx", "row", "nx", "w1")}
        iotaf = env.sb(ctx, "iotaf", [Q, F])
        ps = [env.ps(ctx, f"ps{k}", [P, C4, P]) for k in range(6)]
        loaded, filled, iotas = env.sem("tables_loaded"), env.sem("tables_filled"), env.sem("tables_iotas")
        chain, transposed, used = env.sem("tables_chain"), env.sem("tables_transposed"), env.sem("tables_used")
        pe_ready = env.sem("tables_ready_for_pe")
        pe_done = env.sem("tables_pe_done")
        NB = NT // K
        firsti = env.sb(ctx, "firsti", [K + 1, NT + 1], I32)
        first = env.sb(ctx, "first", [K + 1, NT + 1])
        picked = env.sb(ctx, "picked", [K, NB, K])
        nextcol = env.sb(ctx, "nextcol", [K, NB])
        later = env.sb(ctx, "later", [K, K + 1])
        seg = SegTotals(env, ctx, Q, F)
        N_LOADS = 7
        OUTS = [("gidx", ROWS + 1), ("didx", ROWS + 1), ("sidx", ROWS + 1), ("row", ROWS + 1), ("nx", ROWS + 1),
                ("w1", ROWS + 1), ("has1", ROWS), ("has2", ROWS), ("has3", ROWS), ("sidx3", ROWS), ("gidx3", P)]
        with nc.Block() as block:
            @block.sync
            def _(sp):
                sp.wait_ge(filled, 1)
                with nc.allow_non_contiguous_dma(reason="halo columns"):
                    for tile, dram in ((dsti, a["dst"]), (srci, a["src"])):
                        v = dram.rearrange("(q f) -> q f", q=Q)
                        sp.dma_start(tile[:, 1:F + 1], v[:, :]).then_inc(loaded, 16)
                        sp.dma_start(tile[0:Q - 1, F + 1:F + 4], v[1:Q, 0:3]).then_inc(loaded, 16)
                        if tile is dsti:
                            sp.dma_start(tile[1:Q, 0:1], v[0:Q - 1, F - 1:F]).then_inc(loaded, 16)
                    sp.dma_start(t["etype_i"][:, :], a["etype"].rearrange("(q f) -> q f", q=Q)).then_inc(loaded, 16)
                    sp.dma_start(firsti[:, 0:NT], a["dst"].rearrange("(n p) -> n p", p=ROWS)[:, 0:1].rearrange("n o -> o n")
                                 .to_broadcast([K + 1, NT])).then_inc(loaded, 16)
                sp.wait_ge(loaded, 16 * N_LOADS)

            @block.gpsimd
            def _(pool):
                nc.gpsimd.iota(iotaf[:], [[1, F]], base=0, channel_multiplier=0,
                               allow_small_or_imprecise_dtypes=True)
                nc.gpsimd.iota(t["cols"][:], [[1, P]], base=0, channel_multiplier=0,
                               allow_small_or_imprecise_dtypes=True)
                nc.gpsimd.iota(t["part"][:], [[0, 1]], base=0, channel_multiplier=1,
                               allow_small_or_imprecise_dtypes=True).then_inc(iotas, 1)

            @block.vector
            def _(dve):
                nc.vector.memset(dsti[:], -1)
                nc.vector.memset(firsti[:], -1)
                nc.vector.memset(srci[:], SKIP).then_inc(filled, 1)
                for n in ("gidx", "didx", "sidx", "gidx3", "sidx3"):
                    nc.vector.memset(t[n][:], SKIP)
                for n in ("row", "nx", "w1", "w0", "has1", "has2", "has3"):
                    nc.vector.memset(t[n][:], 0.0)
                nc.vector.memset(t["one"][:], 1.0)
                nc.vector.memset(wk["ones"][:], 1.0)
                for n in ("gidx", "didx", "sidx"):
                    nc.vector.memset(pad[n][:, :, 0:1], float(SKIP))
                for n in ("row", "nx", "w1"):
                    nc.vector.memset(pad[n][:, :, 0:1], 0.0)
                link = Chain(dve, chain)
                dve.wait_ge(iotas, 1)
                link(nc.vector.tensor_scalar(t["ident"][:], t["cols"][:], t["part"][:, 0:1], None, ALU.is_equal))
                dve.wait_ge(loaded, 16 * N_LOADS)
                link(nc.vector.tensor_copy(dst[:], dsti[:]))
                link(nc.vector.tensor_copy(src[:], srci[:]))
                me, before, after = dst[:, 1:F + 1], dst[:, 0:F], dst[:, 2:F + 2]
                me4 = me.rearrange("q (c p) -> q c p", c=C4)
                link(nc.vector.tensor_tensor(t["same"][:], me, before, ALU.is_equal))
                link(nc.vector.tensor_tensor(t["nsame"][:], me, after, ALU.is_equal))
                link(nc.vector.tensor_scalar(t["sadd"][:], t["same"][:], -LOW, LOW, ALU.mult, ALU.add))
                link(nc.vector.tensor_scalar(t["nadd"][:], t["nsame"][:], -LOW, LOW, ALU.mult, ALU.add))
                link(nc.vector.tensor_tensor(t["thru"][:, 0:1], dst[:, F:F + 1], dst[:, 0:1], ALU.is_equal))
                link(nc.vector.tensor_tensor(t["thru"][:, 1:2], dst[:, 1:2], dst[:, F + 1:F + 2], ALU.is_equal))
                link(nc.vector.tensor_scalar(t["thru"][:, 2:4], t["thru"][:, 0:2], -LOW, LOW, ALU.mult, ALU.add))
                nxt = dst[:, ROWS + 1:F + 2:ROWS].unsqueeze(2)
                link(nc.vector.tensor_tensor(pad["nx"][:, :, 1:], me4, nxt.to_broadcast([Q, C4, ROWS]), ALU.is_equal))
                link(nc.vector.tensor_copy(first[:], firsti[:]))
                link(nc.vector.memset(t["flow"][:], 0.0))
                nextk = first[0:K, 1:NT + 1].rearrange("j (n k) -> j n k", k=K)
                link(nc.vector.tensor_tensor(picked[:], nextk,
                                             t["ident"][0:K, 0:K].unsqueeze(1).to_broadcast([K, NB, K]), ALU.mult))
                link(nc.vector.tensor_reduce(nextcol[:], picked[:], AX.X, ALU.add))
                link(nc.vector.tensor_scalar(later[:], t["cols"][0:K, 0:K + 1], t["part"][0:K, 0:1], None, ALU.is_gt))
                for rows, col in ((K, nextcol[:]), (K + 1, first[:, 0:NT:K])):
                    to = t["flow"][0:rows, :, 0, :] if rows == K else t["flow"][0:rows, :, 1, :]
                    link(nc.vector.tensor_tensor(to[:, :, 0:K], first[0:rows, 0:NT].rearrange("j (n k) -> j n k", k=K),
                                                 col.unsqueeze(2).to_broadcast([rows, NB, K]), ALU.is_equal))
                    link(nc.vector.tensor_tensor(to[:, :, K:K + 1], first[0:rows, K:NT + 1:K].unsqueeze(2),
                                                 col.unsqueeze(2), ALU.is_equal))
                link(nc.vector.tensor_tensor(t["flow"][0:K, :, 0, :], t["flow"][0:K, :, 0, :],
                                             later[:].unsqueeze(1).to_broadcast([K, NB, K + 1]), ALU.mult))
                link(nc.vector.tensor_scalar(t["flow"][0:K + 1, :, 1, :], t["flow"][0:K + 1, :, 1, :],
                                             t["ident"][0:K + 1, K:K + 1], None, ALU.mult))
                for k in range(K):
                    link(nc.vector.tensor_scalar(t["into"][:, k, :], t["cols"][0:K + 1, 0:ROWS + 1], 1.0,
                                                 t["ident"][0:K + 1, k:k + 1], ALU.is_equal, ALU.mult))
                link(nc.vector.tensor_scalar(wk["head"][:], t["same"][:], -1.0, 1.0, ALU.mult, ALU.add))
                link(nc.vector.tensor_copy(wk["lhead"][:], wk["head"][:]))
                link(nc.vector.memset(wk["lhead"][:, 0:F:ROWS], 1.0))
                link(nc.vector.tensor_tensor(wk["tmp"][:], wk["lhead"][:], iotaf[:], ALU.mult))
                link(nc.vector.memset(wk["dstm"][:], 0.0))
                link(nc.vector.tensor_tensor_scan(wk["headpos"][:], wk["dstm"][:], wk["tmp"][:], 0.0, ALU.add, ALU.max))
                for c in range(C4):
                    link(nc.vector.tensor_scalar(pad["row"][:, c, 1:], wk["headpos"][:, c * ROWS:(c + 1) * ROWS],
                                                 float(1 - c * ROWS), None, ALU.add))
                link(nc.vector.tensor_scalar(wk["dstm"][:], me, float(-SKIP), None, ALU.add))
                link(nc.vector.tensor_scalar(pad["sidx"][:, :, 1:], pad["nx"][:, :, 1:], -1.0, 1.0, ALU.mult, ALU.add))
                link(nc.vector.tensor_tensor(pad["sidx"][:, :, 1:], pad["sidx"][:, :, 1:],
                                             wk["lhead"][:].rearrange("q (c p) -> q c p", c=C4), ALU.mult))
                link(nc.vector.tensor_tensor(pad["sidx"][:, :, 1:], pad["sidx"][:, :, 1:],
                                             wk["dstm"][:].rearrange("q (c p) -> q c p", c=C4), ALU.mult))
                link(nc.vector.tensor_scalar(pad["sidx"][:, :, 1:], pad["sidx"][:, :, 1:], float(SKIP), None, ALU.add))
                link(nc.vector.tensor_copy(pad["gidx"][:, :, 1:], src[:, 1:F + 1].rearrange("q (c p) -> q c p", c=C4)))
                link(nc.vector.tensor_copy(pad["didx"][:, :, 1:], me4))
                link(nc.vector.tensor_tensor(wk["sidx3"][:], wk["head"][:], wk["dstm"][:], ALU.mult))
                link(nc.vector.tensor_scalar(wk["sidx3"][:], wk["sidx3"][:], float(SKIP), None, ALU.add))
                seg.vector(link, dve, t, wk["ones"][:], wk["fwd"][:], wk["bwd"][:], "sum")
                for k in (1, 2, 3):
                    link(nc.vector.tensor_scalar(wk[f"has{k}"][:], wk["fwd"][:], k + 0.5, None, ALU.is_gt))
                nc.vector.reciprocal(pad["w1"][:, :, 1:], wk["fwd"][:].rearrange("q (c p) -> q c p", c=C4)
                                     ).then_inc(pe_ready, 1)
                for j, (n, rows) in enumerate(OUTS):
                    dve.wait_ge(transposed, j + 1)
                    nc.vector.tensor_copy(t[n][0:rows, :].rearrange("p (q c) -> p c q", c=C4),
                                          ps[j % 6][0:rows, :, 0:Q]).then_inc(used, 1)
                dve.wait_ge(used, len(OUTS))

            @block.tensor
            def _(pe):
                seg.tensor(pe, t, 0)
                pe.wait_ge(pe_ready, 1)
                for j, (n, rows) in enumerate(OUTS):
                    if j >= 6:
                        pe.wait_ge(used, j - 5)
                    for c in range(C4):
                        if n == "gidx3":
                            s = src[:, 1 + c * ROWS:1 + c * ROWS + P]
                        elif n in pad:
                            s = pad[n][:, c, :]
                        else:
                            s = wk[n][:, c * ROWS:(c + 1) * ROWS]
                        last = nc.tensor.transpose(ps[j % 6][0:rows, c, 0:Q], s, t["ident"][0:Q, 0:Q])
                    last.then_inc(transposed, 1)


class SegTotals:

    def __init__(self, env, ctx, Q, F):
        self.env, self.Q, self.F = env, Q, F
        self.row = env.sb(ctx, "seg_row", [1, 2, P])
        self.carry = env.sb(ctx, "seg_carry", [1, P + 1])
        self.cin = env.sb(ctx, "seg_cin", [P, 1])
        self.psr = env.ps(ctx, "seg_psr", [P, 2, P])
        self.psc = env.ps(ctx, "seg_psc", [P, 1])
        self.ready = env.sem("seg_column_ready")
        self.rows = env.sem("seg_rows_transposed")
        self.scanned = env.sem("seg_carries_scanned")
        self.cols = env.sem("seg_carry_column_done")
        self.ask = []
        self.calls = 0

    def vector(self, link, dve, t, val, fwd, bwd, kind):
        nc, Q, F = self.env.nc, self.Q, self.F
        if kind == "max":
            op0, op1, init, d0, thru = ALU.add, ALU.max, LOW, ("sadd", "nadd"), (2, 3)
        else:
            op0, op1, init, d0, thru = ALU.mult, ALU.add, 0.0, ("same", "nsame"), (0, 1)
        for side, out in ((0, fwd), (1, bwd)):
            def way(ap):
                return ap[:, ::-1] if side else ap
            last = out[:, 0:1] if side else out[:, F - 1:F]
            link(nc.vector.tensor_tensor_scan(way(out), way(t[d0[side]][:]), way(val), init, op0, op1))
            self.ask.append((last, thru[side], side))
            nc.vector.memset(self.carry[:], init).then_inc(self.ready, 1)
            self.calls += 1
            n = self.calls
            dve.wait_ge(self.rows, n)
            link(nc.vector.tensor_copy(self.row[:, :, 0:Q], self.psr[0:1, :, 0:Q]))
            to = self.carry[:, 0:Q] if side else self.carry[:, 1:Q + 1]
            nc.vector.tensor_tensor_scan(way(to), way(self.row[:, 1, 0:Q]), way(self.row[:, 0, 0:Q]),
                                         init, op0, op1).then_inc(self.scanned, 1)
            dve.wait_ge(self.cols, n)
            link(nc.vector.tensor_copy(self.cin[0:Q, :], self.psc[0:Q, :]))
            link(nc.vector.tensor_tensor_scan(way(out), way(t[d0[side]][:]), way(val), self.cin[0:Q, 0:1], op0, op1))
        if kind == "max":
            link(nc.vector.tensor_tensor(fwd, fwd, bwd, ALU.max))
        else:
            link(nc.vector.tensor_tensor(fwd, fwd, bwd, ALU.add))
            link(nc.vector.tensor_tensor(fwd, fwd, val, ALU.subtract))

    def tensor(self, pe, t, since):
        nc, Q = self.env.nc, self.Q
        for n, (last, thru, side) in enumerate(self.ask[since:], since):
            pe.wait_ge(self.ready, n + 1)
            nc.tensor.transpose(self.psr[0:1, 0, 0:Q], last, t["ident"][0:Q, 0:Q])
            nc.tensor.transpose(self.psr[0:1, 1, 0:Q], t["thru"][:, thru:thru + 1],
                                t["ident"][0:Q, 0:Q]).then_inc(self.rows, 1)
            pe.wait_ge(self.scanned, n + 1)
            nc.tensor.matmul(self.psc[0:Q, :], self.carry[0:1, side:side + Q], t["one"][0:1, 0:1],
                             start=True, stop=True).then_inc(self.cols, 1)


def logits_phase(env, a, t, edge_rows, agg, scratch):
    nc, x = env.nc, a["x"]
    N, E = x.shape[0], a["src"].shape[0]
    NB = E // (ROWS * K)
    NG = agg.shape[0] // GROUP
    ZB = -(-NG // (NB // 2))
    with env.phase() as ctx:
        g = [env.sb(ctx, f"rows_src_dst{b}", [P, K, 2, D]) for b in range(2)]
        prod = env.sb(ctx, "prod", [P, K, 2 * D])
        w = env.sb(ctx, "head_tail_w", [P, 2 * D])
        zeros = env.sb(ctx, "zeros", [P, T * D])
        idx = [env.sb(ctx, f"idx{b}", [P, 2, K], I32) for b in range(2)]
        begun = env.sem("dma_series_begun")
        cleared, idx_ready, w_loaded = env.sem("cleared"), env.sem("idx_ready"), env.sem("w_loaded")
        gathered = [env.sem(f"gathered{b}") for b in range(2)]
        stored = [env.sem(f"stored{b}") for b in range(2)]
        used, multiplied, zeroed = env.sem("rows_used"), env.sem("multiplied"), env.sem("zeroed")
        with nc.Block() as block:
            @block.gpsimd
            def _(pool):
                bound = pool.to_reg(N - 1)

                def body(i, first, last):
                    for b in range(2):
                        n = 2 * i + b
                        pool.wait_ge(idx_ready, n + 1)
                        if not first:
                            pool.wait_ge(used, n - 1)
                            pool.wait_ge(stored[b], 16 * i)
                        pool.sem_inc(begun, 1)
                        for k in range(K):
                            for s in range(2):
                                pool.indirect_dma_start(
                                    out=g[b][:, k, s, :], out_offset=None, in_=x[:, :],
                                    in_offset=bass.IndirectOffsetOnAxis(ap=idx[b][:, s, k:k + 1], axis=0),
                                    bounds_check=bound, oob_is_err=False).then_inc(gathered[b], 16)
                pool.wait_ge(cleared, 1)
                rounds(pool, NB // 2, body)

            @block.sync
            def _(sp):
                sp.dma_start(w[:, 0:D], a["head_w"].unsqueeze(0).to_broadcast([P, D])).then_inc(w_loaded, 16)
                sp.dma_start(w[:, D:], a["tail_w"].unsqueeze(0).to_broadcast([P, D])).then_inc(w_loaded, 16)

                def body(i, first, last):
                    for b in range(2):
                        n = 2 * i + b
                        sp.wait_ge(gathered[b], 16 * 2 * K * (i + 1))
                        sp.dma_start(edge_rows[bass.ds(n * P, P), :].rearrange("p (k d) -> p k d", k=K),
                                     g[b][:, :, 0, :]).then_inc(stored[b], 16)
                rounds(sp, NB // 2, body)
                for b in range(2):
                    sp.wait_ge(stored[b], 16 * (NB // 2))
                sp.wait_ge(w_loaded, 32)

            @block.scalar
            def _(act):
                act.wait_ge(cleared, 1)
                pads = scratch[0].shape[0] - N
                for s in scratch:
                    act.dma_start(s[N:N + pads, :], zeros[0:pads, 0:D]).then_inc(zeroed, 16)
                zero_groups = NG // ZB
                with act.Fori(0, zero_groups) as i:
                    act.wait_ge(used, (i + 1) * (NB // zero_groups))
                    for z in range(ZB):
                        act.dma_start(agg[bass.ds((i * ZB + z) * GROUP, GROUP), :].rearrange("(p t) d -> p (t d)", p=P),
                                      zeros[:, :]).then_inc(zeroed, 16)
                act.wait_ge(zeroed, 16 * (zero_groups * ZB + len(scratch)))

            @block.vector
            def _(dve):
                nc.vector.memset(g[0][:], 0.0)
                nc.vector.memset(g[1][:], 0.0)
                nc.vector.memset(zeros[:], 0.0).then_inc(cleared, 1)

                def indices(i, b, free):
                    if free:
                        dve.wait_ge(gathered[b], 16 * 2 * K * i)
                    nc.vector.tensor_copy(idx[b][:, 0, :], t["gidx"][:, bass.ds((2 * i + b) * K, K)])
                    nc.vector.tensor_copy(idx[b][:, 1, :], t["didx"][:, bass.ds((2 * i + b) * K, K)]).then_inc(idx_ready, 1)

                def body(i, first, last):
                    for b in range(2):
                        n = 2 * i + b
                        dve.wait_ge(gathered[b], 16 * 2 * K * (i + 1))
                        if not (first and b == 0):
                            dve.wait_ge(used, n)
                        nc.vector.tensor_tensor(prod[:], g[b][:].rearrange("p k s d -> p k (s d)"),
                                                w[:].unsqueeze(1).to_broadcast([P, K, 2 * D]), ALU.mult).then_inc(multiplied, 1)
                        if not last:
                            indices(i + 1, b, True)
                        dve.wait_ge(multiplied, n + 1)
                        nc.vector.tensor_reduce(t["logit"][:, bass.ds(n * K, K)], prod[:], AX.X, ALU.add).then_inc(used, 1)
                indices(0, 0, False)
                indices(0, 1, False)
                dve.wait_ge(w_loaded, 32)
                rounds(dve, NB // 2, body)
                dve.wait_ge(used, NB)


def softmax_phase(env, a, t):
    nc = env.nc
    E = a["src"].shape[0]
    NT = E // ROWS
    Q = NT // C4
    F = C4 * ROWS
    NR = a["rel_w"].shape[0]
    with env.phase() as ctx:
        lg, ex, fwd, bwd, et = (env.sb(ctx, n, [Q, F]) for n in ("lg", "ex", "fwd", "bwd", "et"))
        w = env.sb(ctx, "w0pad", [Q, C4, ROWS + 1])
        sc = env.sb(ctx, "rel_and_biases", [P, NR + 2])
        psl = env.ps(ctx, "psl", [P, C4, P])
        psw = env.ps(ctx, "psw", [P, C4, P])
        loaded, to_edges, ready, done = (env.sem(n) for n in ("sm_loaded", "sm_to_edges", "sm_ready", "sm_to_rows"))
        shifted, expd, chain = env.sem("sm_shifted"), env.sem("sm_exp"), env.sem("sm_chain")
        seg = SegTotals(env, ctx, Q, F)
        with nc.Block() as block:
            @block.sync
            def _(sp):
                for dram, lo, hi in ((a["rel_w"], 0, NR), (a["head_b"], NR, NR + 1), (a["tail_b"], NR + 1, NR + 2)):
                    sp.dma_start(sc[:, lo:hi], dram.unsqueeze(0).to_broadcast([P, hi - lo])).then_inc(loaded, 16)
                sp.wait_ge(loaded, 48)

            @block.vector
            def _(dve):
                link = Chain(dve, chain)
                dve.wait_ge(to_edges, 1)
                link(nc.vector.tensor_copy(lg[:].rearrange("q (c p) -> q c p", c=C4), psl[0:Q, :, 1:ROWS + 1]))
                link(nc.vector.tensor_copy(et[:], t["etype_i"][:, :]))
                dve.wait_ge(loaded, 48)
                link(nc.vector.tensor_scalar(lg[:], lg[:], sc[0:Q, NR:NR + 1], sc[0:Q, NR + 1:NR + 2], ALU.add, ALU.add))
                for r in range(NR):
                    link(nc.vector.tensor_scalar(ex[:], et[:], float(r), sc[0:Q, r:r + 1], ALU.is_equal, ALU.mult))
                    link(nc.vector.tensor_tensor(lg[:], lg[:], ex[:], ALU.add))
                seg.vector(link, dve, t, lg[:], fwd[:], bwd[:], "max")
                nc.vector.tensor_tensor(lg[:], lg[:], fwd[:], ALU.subtract).then_inc(shifted, 1)
                dve.wait_ge(expd, 1)
                seg.vector(link, dve, t, ex[:], fwd[:], bwd[:], "sum")
                link(nc.vector.reciprocal(fwd[:], fwd[:]))
                link(nc.vector.memset(w[:, :, 0:1], 0.0))
                nc.vector.tensor_tensor(w[:, :, 1:], ex[:].rearrange("q (c p) -> q c p", c=C4),
                                        fwd[:].rearrange("q (c p) -> q c p", c=C4), ALU.mult).then_inc(ready, 1)
                dve.wait_ge(done, 1)
                link(nc.vector.tensor_copy(t["w0"][0:ROWS + 1, :].rearrange("p (q c) -> p c q", c=C4),
                                           psw[0:ROWS + 1, :, 0:Q]))

            @block.scalar
            def _(act):
                act.wait_ge(shifted, 1)
                nc.scalar.activation(ex[:], lg[:], ACT.Exp).then_inc(expd, 1)

            @block.tensor
            def _(pe):
                by_tile = t["logit"][:].rearrange("p (q c) -> p c q", c=C4)
                for c in range(C4):
                    last = nc.tensor.transpose(psl[0:Q, c, :], by_tile[:, c, :], t["ident"][:])
                last.then_inc(to_edges, 1)
                seg.tensor(pe, t, 0)
                pe.wait_ge(ready, 1)
                for c in range(C4):
                    last = nc.tensor.transpose(psw[0:ROWS + 1, c, 0:Q], w[:, c, :], t["ident"][0:Q, 0:Q])
                last.then_inc(done, 1)


def edge_sums_phase(env, a, t, table, agg, layer, edge_rows):
    nc = env.nc
    N, E = a["x"].shape[0], a["src"].shape[0]
    NB = E // (ROWS * K)
    IT = NB // 2
    R1 = ROWS + 1
    K1 = K + 1
    gated, projected = layer == 2, layer == 1
    gathers = layer != 0
    weights = {0: "w0", 1: "w1", 2: None}[layer]
    with env.phase() as ctx:
        g = [env.sb(ctx, f"rows{b}", [P, K, D]) for b in range(2)]
        r = [env.sb(ctx, f"messages{b}", [P, K, D]) for b in range(2)] if gated else g
        s = [env.sb(ctx, f"onehot{b}", [P, K, R1]) for b in range(2)]
        over = [env.sb(ctx, f"goes_on{b}", [P, K * K]) for b in range(2)]
        flow = [env.sb(ctx, f"flow{b}", [K1, 2, K1]) for b in range(2)]
        left = [env.sb(ctx, f"left{b}", [K, D]) for b in range(2)]
        came = [env.sb(ctx, f"came{b}", [K1, D]) for b in range(2)]
        res = [env.sb(ctx, f"sums{b}", [P, K, D]) for b in range(2)]
        gi = [env.sb(ctx, f"gi{b}", [P, K], I32) for b in range(2)]
        si = [env.sb(ctx, f"si{b}", [P, K], I32) for b in range(2)]
        acc = [env.ps(ctx, f"acc{b}", [P, K, D]) for b in range(2)]
        small = env.ps(ctx, "small", [P, 3, D])
        psl, psa = small[0:K1, 0:2, :], small[:, 2, 0:R1]
        if gated or projected:
            mat = env.sb(ctx, "mat", [P, D])
            rt = [env.sb(ctx, f"transposed{h}", [P, HALF, P]) for h in range(2)]
            pst = env.ps(ctx, "pst", [P, HALF, P])
            psx = [env.ps(ctx, f"psx{h}", [P, HALF, D]) for h in range(2 if projected else 1)]
        if projected:
            raw = [env.sb(ctx, f"raw_sums{b}", [P, K, D]) for b in range(2)]
        if gated:
            ea = [env.sb(ctx, f"ea{b}", [P, K, a["ea"].shape[1]]) for b in range(2)]
            eat = [env.sb(ctx, f"eat{b}", [P, R1]) for b in range(2)]
            ew = env.sb(ctx, "edge_w_blocks", [P, K, D])
            ews = [env.sb(ctx, f"gates{h}", [P, HALF, D]) for h in range(2)]
            pse = env.ps(ctx, "pse", [P, HALF, D])
        S = env.sem
        arrived = [S(f"rows_arrived{b}") for b in range(2)]
        scattered = [S(f"scattered{b}") for b in range(2)]
        ea_loaded = [S(f"ea_loaded{b}") for b in range(2)]
        pe_begun = S("flow_begun")
        begun, cleared, gi_ready, onehot_ready, compared = (
            S("dma_series_begun"), S("cleared"), S("gi_ready"), S("onehot_ready"), S("compared"))
        left_summed, left_copied, came_summed, came_copied, summed, res_ready = (
            S("left_summed"), S("left_copied"), S("came_summed"), S("came_copied"), S("summed"), S("res_ready"))
        mats, transposed, tcopied, product, product_used, raw_ready = (
            S("mats_loaded"), S("transposed"), S("transposed_copied"), S("product"), S("product_used"), S("raw_ready"))
        ea_transposed, ea_copied, gates_done, gates_copied = (
            S("ea_transposed"), S("ea_copied"), S("gates_done"), S("gates_copied"))
        PER = 16 * (K if gathers else 1)
        EW = a["ea"].shape[1]
        MATS = 16 * (1 + (K if gated else 0))
        with nc.Block() as block:
            @block.gpsimd
            def _(pool):
                bound = pool.to_reg(N - 1)

                def scatter(n, b):
                    if projected:
                        pool.wait_ge(product_used, 2 * n + 2)
                    else:
                        pool.wait_ge(res_ready, n + 1)
                    pool.sem_inc(begun, 1)
                    for k in range(K):
                        pool.indirect_dma_start(
                            out=agg[0:N, :], out_offset=bass.IndirectOffsetOnAxis(ap=si[b][:, k:k + 1], axis=0),
                            in_=res[b][:, k, :], in_offset=None,
                            bounds_check=bound, oob_is_err=False).then_inc(scattered[b], 16)

                def body(i, first, last):
                    for b in range(2):
                        n = 2 * i + b
                        if gathers:
                            pool.wait_ge(gi_ready, n + 1)
                            if gated:
                                wait_past(pool, transposed, 2 * (n - 1))
                            else:
                                wait_past(pool, summed, n - 1)
                            pool.sem_inc(begun, 1)
                            for k in range(K):
                                pool.indirect_dma_start(
                                    out=g[b][:, k, :], out_offset=None, in_=table[0:N, :],
                                    in_offset=bass.IndirectOffsetOnAxis(ap=gi[b][:, k:k + 1], axis=0),
                                    bounds_check=bound, oob_is_err=False).then_inc(arrived[b], 16)
                        if not first:
                            scatter(n - 2, b)
                pool.wait_ge(cleared, 1)
                rounds_from_one(pool, IT, body)
                for b in range(2):
                    scatter(NB - 2 + b, b)
                for b in range(2):
                    pool.wait_ge(scattered[b], 16 * K * IT)

            @block.sync
            def _(sp):
                sp.wait_ge(cleared, 1)
                if gated or projected:
                    sp.dma_start(mat[:], (a["W2"] if gated else a["W_neigh"])[:, :]).then_inc(mats, 16)
                if gated:
                    for k in range(K):
                        sp.dma_start(ew[EW * k:EW * (k + 1), k, :], a["edge_w"][:, :]).then_inc(mats, 16)

                def body(i, first, last):
                    for b in range(2):
                        n = 2 * i + b
                        if not gathers:
                            wait_past(sp, summed, n - 1)
                            sp.dma_start(flat(g[b][:]), edge_rows[bass.ds(n * P, P), :]).then_inc(arrived[b], 16)
                        if gated:
                            wait_past(sp, ea_transposed, n - 1)
                            e0 = n * (K * ROWS)
                            with nc.allow_non_contiguous_dma(reason="rows of edge attributes"):
                                sp.dma_start(ea[b][0:ROWS, :, :],
                                             a["ea"][bass.ds(e0, K * ROWS), :].rearrange("(k p) j -> p k j", k=K)
                                             ).then_inc(ea_loaded[b], 16)
                if gated or not gathers:
                    rounds_from_one(sp, IT, body)
                if gated or projected:
                    sp.wait_ge(mats, MATS)

            @block.tensor
            def _(pe):
                if gated or projected:
                    pe.wait_ge(mats, MATS)

                def through_matrix(n, h):
                    pe.wait_ge(tcopied, 2 * n + h + 1)
                    for k in range(HALF):
                        last = nc.tensor.matmul(psx[h % len(psx)][0:R1, k, :], rt[h][:, k, 0:R1], mat[:],
                                                start=True, stop=True)
                    last.then_inc(product, 1)

                def pre(n, i, b):
                    pe.wait_ge(ea_loaded[b], 16 * (i + 1))
                    nc.tensor.transpose(psa[:, 0:ROWS], flat(ea[b][0:ROWS, :, :]), t["ident"][0:ROWS, 0:ROWS]
                                        ).then_inc(ea_transposed, 1)
                    pe.wait_ge(arrived[b], PER * (i + 1))
                    for h in range(2):
                        c = 2 * n + h
                        wait_past(pe, tcopied, c)
                        for k in range(HALF):
                            last = nc.tensor.transpose(pst[:, k, 0:R1], g[b][0:R1, h * HALF + k, :],
                                                       t["ident"][0:R1, 0:R1])
                        last.then_inc(transposed, 1)
                        if h == 0:
                            pe.wait_ge(ea_copied, n + 1)
                        wait_past(pe, gates_copied, c)
                        for k in range(HALF):
                            last = nc.tensor.matmul(pse[0:R1, k, :], eat[b][:, :], ew[:, h * HALF + k, :],
                                                    start=True, stop=True)
                        last.then_inc(gates_done, 1)
                        wait_past(pe, product_used, c)
                        through_matrix(n, h)

                def sums(n, i, b):
                    pe.wait_ge(onehot_ready, n + 1)
                    if gated:
                        pe.wait_ge(product_used, 2 * n + 2)
                    else:
                        pe.wait_ge(arrived[b], PER * (i + 1))
                    for k in range(K):
                        last = nc.tensor.matmul(psl[0:K, 0, :], over[b][0:R1, k * K:(k + 1) * K], r[b][0:R1, k, :],
                                                start=(k == 0), stop=(k == K - 1))
                    last.then_inc(left_summed, 1)
                    pe.wait_ge(left_copied, n + 1)
                    pe.sem_inc(pe_begun, 1)
                    nc.tensor.matmul(psl[:, 1, :], flow[b][0:K, 0, :], left[b][:], start=True, stop=False)
                    nc.tensor.matmul(psl[:, 1, :], flow[b][:, 1, :], came[1 - b][:], start=False, stop=True
                                     ).then_inc(came_summed, 1)
                    pe.wait_ge(came_copied, n + 1)
                    wait_past(pe, raw_ready if projected else res_ready, n - 1)
                    for k in range(K):
                        nc.tensor.matmul(acc[b][0:R1, k, :], s[b][0:R1, k, :], r[b][0:R1, k, :], start=True, stop=False)
                        last = nc.tensor.matmul(acc[b][0:R1, k, :], t["into"][:, k, :], came[b][:], start=False, stop=True)
                    last.then_inc(summed, 1)

                def post(n, b):
                    pe.wait_ge(raw_ready, n + 1)
                    for h in range(2):
                        c = 2 * n + h
                        wait_past(pe, tcopied, c)
                        for k in range(HALF):
                            last = nc.tensor.transpose(pst[:, k, 0:R1], raw[b][0:R1, h * HALF + k, :],
                                                       t["ident"][0:R1, 0:R1])
                        last.then_inc(transposed, 1)
                        wait_past(pe, product_used, c - 1)
                        through_matrix(n, h)

                def body(i, first, last):
                    for b in range(2):
                        n = 2 * i + b
                        if gated:
                            pre(n, i, b)
                        sums(n, i, b)
                        if projected and not (first and b == 0):
                            post(n - 1, 1 - b)
                rounds_from_one(pe, IT, body)
                if projected:
                    post(NB - 1, 1)

            @block.scalar
            def _(act):
                def transposed_rows(n, h):
                    act.wait_ge(transposed, 2 * n + h + 1)
                    nc.scalar.copy(rt[h][:, :, 0:R1], pst[:, :, 0:R1]).then_inc(tcopied, 1)

                def body(i, first, last):
                    for b in range(2):
                        n = 2 * i + b
                        if gated:
                            act.wait_ge(ea_transposed, n + 1)
                            nc.scalar.copy(eat[b][:, 1:R1], psa[:, 0:ROWS]).then_inc(ea_copied, 1)
                            for h in range(2):
                                transposed_rows(n, h)
                                act.wait_ge(gates_done, 2 * n + h + 1)
                                wait_past(act, product_used, 2 * n + h - 1)
                                nc.scalar.copy(ews[h][0:R1, :, :], pse[0:R1, :, :]).then_inc(gates_copied, 1)
                        act.wait_ge(left_summed, n + 1)
                        nc.scalar.copy(left[b][:], psl[0:K, 0, :]).then_inc(left_copied, 1)
                        act.wait_ge(came_summed, n + 1)
                        nc.scalar.copy(came[b][:], psl[:, 1, :]).then_inc(came_copied, 1)
                        if projected and not (first and b == 0):
                            for h in range(2):
                                transposed_rows(n - 1, h)
                act.wait_ge(cleared, 1)
                rounds_from_one(act, IT, body)
                if projected:
                    for h in range(2):
                        transposed_rows(NB - 1, h)

            @block.vector
            def _(dve):
                nc.vector.memset(came[1][:], 0.0)
                for b in range(2):
                    nc.vector.memset(g[b][:], 0.0)
                    nc.vector.memset(res[b][:], 0.0)
                    nc.vector.memset(over[b][:], 0.0)
                    nc.vector.memset(s[b][:], 0.0)
                    if gated:
                        nc.vector.memset(eat[b][:], 0.0)
                if gated:
                    nc.vector.memset(ew[:], 0.0)
                nc.vector.memset(t["zero"][:], 0.0).then_inc(cleared, 1)
                dve.wait_ge(cleared, 1)

                def gather_indices(n, i, b):
                    if gathers:
                        wait_past(dve, arrived[b], PER * i)
                        nc.vector.tensor_copy(gi[b][:], t["gidx"][:, bass.ds(n * K, K)]).then_inc(gi_ready, 1)

                def onehots(n, b):
                    at = bass.ds(n * K, K)
                    wait_past(dve, summed, n - 1)
                    row = t["row"][:, at].unsqueeze(2).to_broadcast([P, K, ROWS])
                    cols = t["cols"][:, 1:R1].unsqueeze(1).to_broadcast([P, K, ROWS])
                    nc.vector.tensor_copy(flow[b][:].rearrange("j a k -> j (a k)"),
                                          t["flow"][:].rearrange("j n a k -> j (n a k)")[:, bass.ds(n * (2 * K1), 2 * K1)])
                    one = nc.vector.tensor_tensor(s[b][:, :, 1:R1], row, cols, ALU.is_equal)
                    diagonal = over[b][:, 0:K * K:K + 1]
                    if weights:
                        one.then_inc(compared, 1)
                        nc.vector.tensor_tensor(diagonal, t["nx"][:, at], t[weights][:, at], ALU.mult)
                        dve.wait_ge(compared, n + 1)
                        nc.vector.tensor_tensor(s[b][:, :, 1:R1], s[b][:, :, 1:R1],
                                                t[weights][:, at].unsqueeze(2).to_broadcast([P, K, ROWS]),
                                                ALU.mult).then_inc(onehot_ready, 1)
                    else:
                        nc.vector.tensor_copy(diagonal, t["nx"][:, at]).then_inc(onehot_ready, 1)

                def gate(n, b):
                    for h in range(2):
                        c = 2 * n + h
                        dve.wait_ge(product, c + 1)
                        dve.wait_ge(gates_copied, c + 1)
                        nc.vector.tensor_tensor(r[b][0:R1, h * HALF:(h + 1) * HALF, :], psx[0][0:R1, :, :],
                                                ews[h][0:R1, :, :], ALU.mult).then_inc(product_used, 1)

                def scatter_indices(n, i, b):
                    wait_past(dve, scattered[b], 16 * K * i)
                    nc.vector.tensor_copy(si[b][:], t["sidx"][:, bass.ds(n * K, K)])

                def finish(n, i, b):
                    dve.wait_ge(summed, n + 1)
                    if projected:
                        wait_past(dve, transposed, 2 * (n - 1))
                        nc.vector.tensor_copy(flat(raw[b][0:R1, :, :]), flat(acc[b][0:R1, :, :])).then_inc(raw_ready, 1)
                    else:
                        scatter_indices(n, i, b)
                        nc.vector.tensor_copy(flat(res[b][0:R1, :, :]), flat(acc[b][0:R1, :, :])).then_inc(res_ready, 1)

                def projections(n, i, b):
                    scatter_indices(n, i, b)
                    for h in range(2):
                        dve.wait_ge(product, 2 * n + h + 1)
                        nc.vector.tensor_copy(res[b][0:R1, h * HALF:(h + 1) * HALF, :], psx[h][0:R1, :, :]
                                              ).then_inc(product_used, 1)

                def body(i, first, last):
                    for b in range(2):
                        n = 2 * i + b
                        if not (last and b == 1):
                            gather_indices(n + 1, i + b, 1 - b)
                        onehots(n, b)
                        if gated:
                            gate(n, b)
                        if not (first and b == 0):
                            finish(n - 1, i - 1 + b, 1 - b)
                        if projected and not first:
                            projections(n - 2, i - 1, b)
                gather_indices(0, 0, 0)
                rounds_from_two(dve, IT, body)
                finish(NB - 1, IT - 1, 1)
                if projected:
                    projections(NB - 2, IT - 1, 0)
                    projections(NB - 1, IT - 1, 1)


def layer3_constants_phase(env, a, t):
    nc = env.nc
    with env.phase() as ctx:
        loaded, chain = env.sem("l3_loaded"), env.sem("l3_chain")
        w = [env.sb(ctx, f"w{l}", [P, D]) for l in range(2)]
        bl = [env.sb(ctx, f"bl{l}", [P, D]) for l in range(2)]
        bcol = [env.sb(ctx, f"bcol{l}", [P, 1]) for l in range(2)]
        cw = [env.sb(ctx, f"cw{l}", [P, 4]) for l in range(2)]
        cb = [env.sb(ctx, f"cb{l}", [P, 1]) for l in range(2)]
        scw = env.sb(ctx, "sum_cw", [P, 2])
        col = env.sb(ctx, "blank_column", [P, 2])
        diag = env.sb(ctx, "diag", [P, 2, D])
        prod = env.sb(ctx, "prod", [P, D])
        ps = env.ps(ctx, "ps", [P, 2, D])
        ready, spread = env.sem("l3_diag_ready"), env.sem("l3_spread")
        N_LOADS = 8 * 2
        with nc.Block() as block:
            @block.sync
            def _(sp):
                for l in range(2):
                    sp.dma_start(w[l][:], a[f"W3_{l}"][:, :]).then_inc(loaded, 16)
                    sp.dma_start(bl[l][:], a[f"blank{l}"].unsqueeze(0).to_broadcast([P, D])).then_inc(loaded, 16)
                    sp.dma_start(bcol[l][:], a[f"b{l}"].unsqueeze(1)).then_inc(loaded, 16)
                    sp.dma_start(cw[l][:], a[f"cw{l}"].unsqueeze(0).to_broadcast([P, 4])).then_inc(loaded, 16)
                    sp.dma_start(cb[l][:], a[f"cb{l}"].unsqueeze(0).to_broadcast([P, 1])).then_inc(loaded, 16)
                    sp.dma_start(t[f"a{l}"][:], a[f"a{l}"].unsqueeze(0).to_broadcast([P, 1])).then_inc(loaded, 16)
                    sp.dma_start(t[f"g{l}"][:], a[f"g{l}"].unsqueeze(0).to_broadcast([P, D])).then_inc(loaded, 16)
                    sp.dma_start(t[f"be{l}"][:], a[f"be{l}"].unsqueeze(0).to_broadcast([P, D])).then_inc(loaded, 16)
                sp.wait_ge(loaded, 16 * N_LOADS)

            @block.vector
            def _(dve):
                link = Chain(dve, chain)
                nc.vector.memset(t["ones"][:], 1.0)
                for k in range(1, 4):
                    nc.vector.tensor_scalar(t["shift"][:, k - 1, :], t["cols"][:], float(k), t["part"][:, 0:1],
                                            ALU.add, ALU.is_equal)
                dve.wait_ge(loaded, 16 * N_LOADS)
                for l in range(2):
                    for k in range(4):
                        nc.vector.tensor_scalar(t[f"cwi{l}"][:, k, :], t["ident"][:], cw[l][:, k:k + 1], None, ALU.mult)
                    link(nc.vector.tensor_tensor(prod[:], w[l][:], bl[l][:], ALU.mult))
                    link(nc.vector.tensor_reduce(col[:, l:l + 1], prod[:], AX.X, ALU.add))
                    link(nc.vector.tensor_tensor(col[:, l:l + 1], col[:, l:l + 1], bcol[l][:], ALU.add))
                    link(nc.vector.tensor_reduce(scw[:, l:l + 1], cw[l][:], AX.X, ALU.add))
                    nc.vector.tensor_scalar(diag[:, l, :], t["ident"][:], col[:, l:l + 1], None, ALU.mult).then_inc(ready, 1)
                dve.wait_ge(spread, 1)
                for l in range(2):
                    link(nc.vector.tensor_copy(t[f"bp{l}"][:], ps[:, l, :]))
                    link(nc.vector.tensor_scalar(t[f"c{l}"][:], t[f"bp{l}"][:], scw[:, l:l + 1], cb[l][:, 0:1],
                                                 ALU.mult, ALU.add))

            @block.tensor
            def _(pe):
                pe.wait_ge(ready, 2)
                for l in range(2):
                    last = nc.tensor.matmul(ps[:, l, :], t["ones"][:], diag[:, l, :], start=True, stop=True)
                last.then_inc(spread, 1)


def edge_sorts_phase(env, a, t, table, agg, l):
    nc = env.nc
    N, E = a["x"].shape[0], a["src"].shape[0]
    NB = E // (ROWS * K)
    IT = NB // 2
    with env.phase() as ctx:
        g = [env.sb(ctx, f"rows{b}", [P, K, D]) for b in range(2)]
        v = [env.sb(ctx, f"slots{b}", [P, 4, K, D]) for b in range(2)]
        mn, mx = (env.sb(ctx, n, [P, 2, K, D]) for n in ("pair_min", "pair_max"))
        mid = [env.sb(ctx, f"middle{b}", [P, 2, K, D]) for b in range(2)]
        res = [env.sb(ctx, f"res{b}", [P, K, D]) for b in range(2)]
        gi = [env.sb(ctx, f"gi{b}", [P, K], I32) for b in range(2)]
        si = [env.sb(ctx, f"si{b}", [P, K], I32) for b in range(2)]
        has = [env.sb(ctx, f"has{b}", [P, 3, K]) for b in range(2)]
        psv = [env.ps(ctx, f"psv{j}", [P, HALF, D]) for j in range(4)]
        psw = [env.ps(ctx, f"psw{h}", [P, HALF, D]) for h in range(2)]
        S = env.sem
        begun = S("dma_series_begun")
        cleared, idx_ready, blanked = S("cleared"), S("idx_ready"), S("rows_less_blank")
        gathered = [S(f"gathered{b}") for b in range(2)]
        scattered = [S(f"scattered{b}") for b in range(2)]
        shifted, masked, pairs, ends, ordered = S("shifted"), S("masked"), S("pairs"), S("ends"), S("ordered")
        weighted, res_ready = S("weighted"), S("res_ready")
        with nc.Block() as block:
            @block.gpsimd
            def _(pool):
                bound = pool.to_reg(N - 1)

                def scatter(n, b):
                    pool.wait_ge(res_ready, 2 * n + 2)
                    pool.sem_inc(begun, 1)
                    for k in range(K):
                        pool.indirect_dma_start(
                            out=agg[0:N, :], out_offset=bass.IndirectOffsetOnAxis(ap=si[b][:, k:k + 1], axis=0),
                            in_=res[b][:, k, :], in_offset=None,
                            bounds_check=bound, oob_is_err=False).then_inc(scattered[b], 16)

                def body(i, first, last):
                    for b in range(2):
                        n = 2 * i + b
                        pool.wait_ge(idx_ready, n + 1)
                        if not first:
                            pool.wait_ge(blanked, n - 1)
                        pool.sem_inc(begun, 1)
                        for k in range(K):
                            pool.indirect_dma_start(
                                out=g[b][:, k, :], out_offset=None, in_=table[0:N, :],
                                in_offset=bass.IndirectOffsetOnAxis(ap=gi[b][:, k:k + 1], axis=0),
                                bounds_check=bound, oob_is_err=False).then_inc(gathered[b], 16)
                        if not first:
                            scatter(n - 2, b)
                pool.wait_ge(cleared, 1)
                rounds(pool, IT, body)
                scatter(NB - 2, 0)
                scatter(NB - 1, 1)
                for b in range(2):
                    pool.wait_ge(scattered[b], 16 * K * IT)

            @block.vector
            def _(dve):
                nc.vector.memset(g[0][:], 0.0)
                nc.vector.memset(g[1][:], 0.0).then_inc(cleared, 1)

                def gather_indices(n, i, b):
                    wait_past(dve, gathered[b], 16 * K * i)
                    nc.vector.tensor_copy(gi[b][:], t["gidx3"][:, bass.ds(n * K, K)]).then_inc(idx_ready, 1)

                def less_blank(n, i, b):
                    wait_past(dve, masked, 6 * (n - 1))
                    for k in range(3):
                        nc.vector.tensor_copy(has[b][:, k, :], t[f"has{k + 1}"][:, bass.ds(n * K, K)])
                    dve.wait_ge(gathered[b], 16 * K * (i + 1))
                    wait_past(dve, weighted, 2 * (n - 1))
                    nc.vector.tensor_tensor(v[b][:, 0, :, :], g[b][:],
                                            t[f"bp{l}"][:].unsqueeze(1).to_broadcast([P, K, D]),
                                            ALU.subtract).then_inc(blanked, 1)

                def sort(n, i, b):
                    wait_past(dve, scattered[b], 16 * K * i)
                    nc.vector.tensor_copy(si[b][:], t["sidx3"][:, bass.ds(n * K, K)])
                    dve.wait_ge(masked, 6 * (n + 1))
                    wait_past(dve, ordered, n)
                    nc.vector.tensor_tensor(mn[:], v[b][:, 0:4:2, :, :], v[b][:, 1:4:2, :, :], ALU.min)
                    nc.vector.tensor_tensor(mx[:], v[b][:, 0:4:2, :, :], v[b][:, 1:4:2, :, :], ALU.max).then_inc(pairs, 1)
                    dve.wait_ge(pairs, n + 1)
                    nc.vector.tensor_tensor(v[b][:, 1, :, :], mn[:, 0, :, :], mn[:, 1, :, :], ALU.max)
                    nc.vector.tensor_tensor(v[b][:, 2, :, :], mx[:, 0, :, :], mx[:, 1, :, :], ALU.min).then_inc(ends, 1)
                    nc.vector.tensor_tensor(v[b][:, 0, :, :], mn[:, 0, :, :], mn[:, 1, :, :], ALU.min)
                    nc.vector.tensor_tensor(v[b][:, 3, :, :], mx[:, 0, :, :], mx[:, 1, :, :], ALU.max)
                    dve.wait_ge(ends, n + 1)
                    nc.vector.tensor_tensor(mid[b][:, 0, :, :], v[b][:, 1, :, :], v[b][:, 2, :, :], ALU.min)
                    nc.vector.tensor_tensor(mid[b][:, 1, :, :], v[b][:, 1, :, :], v[b][:, 2, :, :], ALU.max
                                            ).then_inc(ordered, 1)

                def body(i, first, last):
                    for b in range(2):
                        n = 2 * i + b
                        if not (last and b == 1):
                            gather_indices(n + 1, i + b, 1 - b)
                        less_blank(n, i, b)
                        if not (first and b == 0):
                            sort(n - 1, i - 1 + b, 1 - b)
                gather_indices(0, 0, 0)
                rounds_from_two(dve, IT, body)
                sort(NB - 1, IT - 1, 1)

            @block.tensor
            def _(pe):
                def body(i, first, last):
                    for b in range(2):
                        n = 2 * i + b
                        pe.wait_ge(blanked, n + 1)
                        for k in range(3):
                            for h in range(2):
                                j = 2 * k + h
                                if not (first and b == 0 and j < 4):
                                    pe.wait_ge(masked, 6 * n + j - 3)
                                nc.tensor.matmul(psv[(6 * b + j) % 4][:].rearrange("p k d -> p (k d)"),
                                                 t["shift"][:, k, :], flat(v[b][:, 0, h * HALF:(h + 1) * HALF, :]),
                                                 start=True, stop=True).then_inc(shifted, 1)
                        if not (first and b == 0):
                            weigh(pe, n - 1, 1 - b, first)

                def weigh(pe, n, b, first):
                    pe.wait_ge(ordered, n + 1)
                    for h in range(2):
                        if not first:
                            pe.wait_ge(res_ready, 2 * n + h - 1)
                        part = slice(h * HALF, (h + 1) * HALF)
                        parts = [v[b][:, 0, part, :], mid[b][:, 0, part, :], mid[b][:, 1, part, :], v[b][:, 3, part, :]]
                        for k, s in enumerate(parts):
                            last = nc.tensor.matmul(flat(psw[h][:]), t[f"cwi{l}"][:, k, :], flat(s),
                                                    start=(k == 0), stop=(k == 3))
                        last.then_inc(weighted, 1)
                rounds(pe, IT, body)
                weigh(pe, NB - 1, 1, False)

            @block.scalar
            def _(act):
                def out(n, i, b, free):
                    for h in range(2):
                        act.wait_ge(weighted, 2 * n + h + 1)
                        if free and h == 0:
                            act.wait_ge(scattered[b], 16 * K * i)
                        nc.scalar.copy(res[b][:, h * HALF:(h + 1) * HALF, :], psw[h][:]).then_inc(res_ready, 1)

                def body(i, first, last):
                    for b in range(2):
                        n = 2 * i + b
                        for k in range(3):
                            for h in range(2):
                                j = 2 * k + h
                                act.wait_ge(shifted, 6 * n + j + 1)
                                for q in range(HALF):
                                    ins = nc.scalar.activation(v[b][:, k + 1, h * HALF + q, :],
                                                               psv[(6 * b + j) % 4][:, q, :], ACT.Copy,
                                                               scale=has[b][:, k, h * HALF + q:h * HALF + q + 1])
                                ins.then_inc(masked, 1)
                        if not (first and b == 0):
                            out(n - 1, i if b == 1 else i - 1, 1 - b, not first)
                rounds_from_one(act, IT, body)
                out(NB - 1, IT - 1, 1, True)


def rounds_from(peeled, engine, n, body):
    for i in range(min(peeled, n)):
        body(i, i == 0, i == n - 1)
    if n > peeled + 1:
        with engine.Fori(peeled, n - 1) as i:
            body(i, False, False)
    if n > peeled:
        body(n - 1, False, True)


def rounds_from_one(engine, n, body):
    rounds_from(2, engine, n, body)


def rounds_from_two(engine, n, body):
    rounds_from(2, engine, n, body)


def rows_of(dram, tile, n, N, whole):
    if whole:
        return [(dram[bass.ds(n * GROUP, GROUP), :].rearrange("(p t) d -> p (t d)", p=P), flat(tile[:]))]
    r0, left = n * GROUP, N - n * GROUP
    full, part = left // T, left % T
    pairs = [(dram[r0:r0 + full * T, :].rearrange("(p t) d -> p (t d)", p=full), flat(tile[0:full, :, :]))]
    if part:
        pairs.append((dram[r0 + full * T:N, :].unsqueeze(0), tile[full:full + 1, 0:part, :]))
    return pairs


class Loads:

    def __init__(self, env, ctx, arrays, N, NG):
        self.arrays, self.N, self.NG = arrays, N, NG
        self.bufs = {n: [env.sb(ctx, f"{n}{b}", [P, T, D]) for b in range(2)] for n in arrays}
        self.sems = {n: [env.sem(f"{n}_loaded{b}") for b in range(2)] for n in arrays}

    def pairs(self, name, n, b, last):
        dram = self.arrays[name]
        whole = not (last and b == 1) or dram.shape[0] == self.NG * GROUP
        return rows_of(dram, self.bufs[name][b], n, self.N, whole)

    def issue(self, sp, name, n, b, last):
        for dram, tile in self.pairs(name, n, b, last):
            sp.dma_start(tile, dram).then_inc(self.sems[name][b], 16)

    def wait(self, engine, name, i, b, last):
        engine.wait_ge(self.sems[name][b], 16 * i + 16 * len(self.pairs(name, 2 * i + b, b, last)))


def node_norm_phase(env, a, t, layer, arrays, out):
    nc = env.nc
    N = a["x"].shape[0]
    NG = -(-N // GROUP)
    IT = NG // 2
    banks = [(c, min(HALF, T - c)) for c in range(0, T, HALF)]
    NBK = len(banks)
    with env.phase() as ctx:
        ld = Loads(env, ctx, arrays, N, NG)
        xb, ab = ld.bufs["x"], ld.bufs["agg"]
        o = [env.sb(ctx, f"out{b}", [P, T, D]) for b in range(2)]
        st = env.sb(ctx, "stats", [P, T, 6])
        sm = {n: env.sb(ctx, n, [P, T]) for n in ("msum", "mdiff", "m2", "dsq", "v4", "var")}
        std = [env.sb(ctx, f"std{b}", [P, T]) for b in range(2)]
        rstd = [env.sb(ctx, f"rstd{b}", [P, T]) for b in range(2)]
        nbias = [env.sb(ctx, f"nbias{b}", [P, T]) for b in range(2)]
        S = env.sem
        pre_done, summed, var_ready, std_ready, norm_ready = (
            S("pool_done"), S("residual_summed"), S("variance_ready"), S("std_ready"), S("factors_ready"))
        pool_step, chain, normed = S("pool_step"), S("vector_chain"), S("normalised")
        stored = [S(f"out_stored{b}") for b in range(2)]
        consts = S("consts_loaded")
        if layer in (1, 2):
            bias = env.sb(ctx, "bias", [P, D])
        if layer == 1:
            wself = env.sb(ctx, "w_self", [P, D])
            xt = [env.sb(ctx, f"xt{j}", [P, HALF, P]) for j in range(2)]
            pst = [env.ps(ctx, f"pst{j}", [P, HALF, P]) for j in range(2)]
            psx = [env.ps(ctx, f"psx{j}", [P, HALF, D]) for j in range(2)]
            xtr, xcp, prod, added = S("x_transposed"), S("x_copied"), S("x_times_w"), S("product_added")
        NCONST = {0: 0, 1: 2, 2: 1, 3: 0}[layer]
        sum_buf = ld.bufs["x4"] if layer == 3 else xb
        with nc.Block() as block:
            @block.sync
            def _(sp):
                if layer in (1, 2):
                    sp.dma_start(bias[:], a[f"b_{layer}"].unsqueeze(0).to_broadcast([P, D])).then_inc(consts, 16)
                if layer == 1:
                    sp.dma_start(wself[:], a["W_self"][:, :]).then_inc(consts, 16)

                def body(i, first, last):
                    for b in range(2):
                        n = 2 * i + b
                        if not first:
                            sp.wait_ge(normed, n - 1)
                        for name in arrays:
                            ld.issue(sp, name, n, b, last)
                rounds_from_one(sp, IT, body)
                if NCONST:
                    sp.wait_ge(consts, 16 * NCONST)

            @block.gpsimd
            def _(pool):
                if layer == 0:
                    return

                def body(i, first, last):
                    for b in range(2):
                        n = 2 * i + b
                        ld.wait(pool, "agg", i, b, last)
                        if layer == 3:
                            nc.gpsimd.tensor_tensor(ab[b][:], ab[b][:], t["bn_scale"][:].unsqueeze(1).to_broadcast([P, T, D]),
                                                    ALU.mult).then_inc(pool_step, 1)
                            ld.wait(pool, "x", i, b, last)
                            pool.wait_ge(pool_step, n + 1)
                            nc.gpsimd.tensor_tensor(ab[b][:], ab[b][:], xb[b][:], ALU.add).then_inc(pre_done, 1)
                        else:
                            nc.gpsimd.tensor_tensor(ab[b][:], ab[b][:], bias[:].unsqueeze(1).to_broadcast([P, T, D]),
                                                    ALU.add).then_inc(pre_done, 1)
                if NCONST:
                    pool.wait_ge(consts, 16 * NCONST)
                rounds(pool, IT, body)

            if layer == 1:
                @block.tensor
                def _(pe):
                    pe.wait_ge(consts, 16 * NCONST)

                    def body(i, first, last):
                        for b in range(2):
                            n = 2 * i + b
                            ld.wait(pe, "x", i, b, last)

                            def times_w(j):
                                c, w = banks[j]
                                q = NBK * n + j
                                pe.wait_ge(xcp, q + 1)
                                if not (first and NBK * b + j < 2):
                                    pe.wait_ge(added, q - 1)
                                for k in range(w):
                                    m = nc.tensor.matmul(psx[(NBK * b + j) % 2][:, k, :], xt[(NBK * b + j) % 2][:, k, :],
                                                         wself[:], start=True, stop=True)
                                m.then_inc(prod, 1)
                            for j, (c, w) in enumerate(banks):
                                q = NBK * n + j
                                if not (first and NBK * b + j < 2):
                                    pe.wait_ge(xcp, q - 1)
                                for k in range(w):
                                    m = nc.tensor.transpose(pst[(NBK * b + j) % 2][:, k, :], xb[b][:, c + k, :], t["ident"][:])
                                m.then_inc(xtr, 1)
                                if j:
                                    times_w(j - 1)
                            times_w(NBK - 1)
                    rounds(pe, IT, body)

            @block.vector
            def _(dve):
                if NCONST:
                    dve.wait_ge(consts, 16 * NCONST)
                LINKS = 5 + (2 if layer == 3 else 0)

                def body(i, first, last):
                    link = Chain(dve, chain, 2 * LINKS * i)
                    for b in range(2):
                        n = 2 * i + b
                        x, s = xb[b], sum_buf[b]
                        for name in arrays:
                            ld.wait(dve, name, i, b, last)
                        if layer == 3:
                            link(nc.vector.tensor_tensor(s[:], s[:], t["bn_alpha"][:].unsqueeze(1).to_broadcast([P, T, D]), ALU.mult))
                            link(nc.vector.tensor_tensor(s[:], s[:], t["bn_shift"][:].unsqueeze(1).to_broadcast([P, T, D]), ALU.add))
                        if layer:
                            dve.wait_ge(pre_done, n + 1)
                        if layer == 1:
                            s = ab[b]
                            link(nc.vector.tensor_tensor(s[:], x[:], ab[b][:], ALU.add))
                            for j, (c, w) in enumerate(banks):
                                dve.wait_ge(prod, NBK * n + j + 1)
                                nc.vector.tensor_tensor(s[:, c:c + w, :], s[:, c:c + w, :],
                                                        psx[(NBK * b + j) % 2][:, 0:w, :], ALU.add).then_inc(added, 1)
                            dve.wait_ge(added, NBK * (n + 1))
                        else:
                            link(nc.vector.tensor_tensor(s[:], s[:], ab[b][:], ALU.add))
                        for k in range(T):
                            ins = nc.vector.bn_stats(st[:, k, :], s[:, k, :])
                        link(ins)
                        nc.vector.tensor_tensor(sm["msum"][:], st[:, :, 1], st[:, :, 4], ALU.add)
                        nc.vector.tensor_tensor(sm["m2"][:], st[:, :, 2], st[:, :, 5], ALU.add)
                        link(nc.vector.tensor_tensor(sm["mdiff"][:], st[:, :, 1], st[:, :, 4], ALU.subtract))
                        nc.vector.tensor_scalar(sm["v4"][:], sm["m2"][:], 1.0 / D, EPS, ALU.mult, ALU.add)
                        link(nc.vector.scalar_tensor_tensor(sm["dsq"][:], sm["mdiff"][:], 0.25, sm["mdiff"][:],
                                                            ALU.mult, ALU.mult))
                        nc.vector.tensor_tensor(sm["var"][:], sm["v4"][:], sm["dsq"][:], ALU.add).then_inc(var_ready, 1)
                        dve.wait_ge(std_ready, n + 1)
                        link(nc.vector.reciprocal(rstd[b][:], std[b][:]))
                        nc.vector.scalar_tensor_tensor(nbias[b][:], sm["msum"][:], -0.5, rstd[b][:],
                                                       ALU.mult, ALU.mult).then_inc(norm_ready, 1)
                    assert link.n == 2 * LINKS, link.n
                rounds(dve, IT, body)

            @block.scalar
            def _(act):
                def body(i, first, last):
                    for b in range(2):
                        n = 2 * i + b
                        if layer == 1:
                            for j, (c, w) in enumerate(banks):
                                q = NBK * n + j
                                act.wait_ge(xtr, q + 1)
                                if not (first and NBK * b + j < 2):
                                    act.wait_ge(prod, q - 1)
                                nc.scalar.copy(xt[(NBK * b + j) % 2][:, 0:w, :], pst[(NBK * b + j) % 2][:, 0:w, :]).then_inc(xcp, 1)
                        act.wait_ge(var_ready, n + 1)
                        nc.scalar.activation(std[b][:], sm["var"][:], ACT.Sqrt).then_inc(std_ready, 1)
                        act.wait_ge(norm_ready, n + 1)
                        if not first:
                            act.wait_ge(stored[b], 16 * i)
                        s = ab[b] if layer == 1 else sum_buf[b]
                        for k in range(T):
                            ins = nc.scalar.activation(o[b][:, k, :], s[:, k, :], ACT.Identity,
                                                       bias=nbias[b][:, k:k + 1], scale=rstd[b][:, k:k + 1])
                        ins.then_inc(normed, 1)
                        act.wait_ge(normed, n + 1)
                        for dram, tile in rows_of(out, o[b], n, N, not (last and b == 1)):
                            act.dma_start(dram, tile).then_inc(stored[b], 16)
                rounds(act, IT, body)
                act.wait_ge(stored[0], 16 * IT)
                act.wait_ge(stored[1], 16 * (IT - 1) + 16 * len(rows_of(out, o[1], NG - 1, N, False)))


def bn_stats_phase(env, a, t, x, agg, l):
    nc = env.nc
    N = a["x"].shape[0]
    NG = -(-N // GROUP)
    IT = NG // 2
    chunks = [(c, min(HALF, T - c)) for c in range(0, T, HALF)]
    with env.phase() as ctx:
        ld = Loads(env, ctx, {"x": x, "agg": agg}, N, NG)
        xb, ab = ld.bufs["x"], ld.bufs["agg"]
        h = [env.sb(ctx, f"h{b}", [P, T, D]) for b in range(2)]
        sq = [env.sb(ctx, f"sq{b}", [P, T, D]) for b in range(2)]
        acc = env.sb(ctx, "h_sums", [P, T, D])
        acc2 = env.sb(ctx, "sq_sums", [P, HALF, D])
        f = {n: env.sb(ctx, n, [P, D]) for n in ("mean", "ex2", "var", "std", "rstd", "tmp")}
        ps = [env.ps(ctx, f"ps{b}", [P, HALF, D]) for b in range(2)]
        psm = env.ps(ctx, "psm", [P, HALF, D])
        S = env.sem
        h_ready, squared, sq_summed, sq_added, chain = (
            S("h_ready"), S("squared"), S("squares_summed"), S("squares_added"), S("bn_chain"))
        acc_ready, acc_summed, var_ready, std_ready, h_added = (
            S("acc_ready"), S("acc_summed"), S("var_ready"), S("std_ready"), S("h_added"))
        with nc.Block() as block:
            @block.sync
            def _(sp):
                def body(i, first, last):
                    for b in range(2):
                        n = 2 * i + b
                        if not first:
                            sp.wait_ge(h_ready, n - 1)
                        ld.issue(sp, "x", n, b, last)
                        ld.issue(sp, "agg", n, b, last)
                rounds_from_one(sp, IT, body)

            @block.vector
            def _(dve):
                nc.vector.memset(acc[:], 0.0).then_inc(h_added, 1)
                nc.vector.memset(acc2[:], 0.0).then_inc(sq_added, 1)

                def add_squares(n, b):
                    dve.wait_ge(sq_summed, n + 1)
                    dve.wait_ge(sq_added, n + 1)
                    nc.vector.tensor_tensor(acc2[:], acc2[:], ps[b][:], ALU.add).then_inc(sq_added, 1)

                def body(i, first, last):
                    for b in range(2):
                        n = 2 * i + b
                        ld.wait(dve, "x", i, b, last)
                        ld.wait(dve, "agg", i, b, last)
                        if not first:
                            dve.wait_ge(squared, n - 1)
                        nc.vector.scalar_tensor_tensor(h[b][:], xb[b][:], t[f"a{l}"][:, 0:1], ab[b][:],
                                                       ALU.mult, ALU.add).then_inc(h_ready, 1)
                        if not (first and b == 0):
                            add_squares(n - 1, 1 - b)
                        dve.wait_ge(h_ready, n + 1)
                        dve.wait_ge(h_added, n + 1)
                        nc.vector.tensor_tensor(acc[:], acc[:], h[b][:], ALU.add).then_inc(h_added, 1)
                rounds(dve, IT, body)
                add_squares(NG - 1, 1)
                link = Chain(dve, chain)
                dve.wait_ge(sq_added, NG + 1)
                dve.wait_ge(acc_summed, 1)
                link(nc.vector.tensor_reduce(f["mean"][:], psm[:].rearrange("p k d -> p d k"), AX.X, ALU.add))
                link(nc.vector.tensor_reduce(f["ex2"][:], acc2[:].rearrange("p k d -> p d k"), AX.X, ALU.add))
                link(nc.vector.tensor_scalar(f["mean"][:], f["mean"][:], 1.0 / N, None, ALU.mult))
                link(nc.vector.tensor_scalar(f["ex2"][:], f["ex2"][:], 1.0 / N, EPS, ALU.mult, ALU.add))
                link(nc.vector.tensor_tensor(f["tmp"][:], f["mean"][:], f["mean"][:], ALU.mult))
                nc.vector.tensor_tensor(f["var"][:], f["ex2"][:], f["tmp"][:], ALU.subtract).then_inc(var_ready, 1)
                dve.wait_ge(std_ready, 1)
                link(nc.vector.reciprocal(f["rstd"][:], f["std"][:]))
                link(nc.vector.tensor_tensor(t["bn_scale"][:], t[f"g{l}"][:], f["rstd"][:], ALU.mult))
                link(nc.vector.tensor_scalar(t["bn_alpha"][:], t["bn_scale"][:], t[f"a{l}"][:, 0:1], 1.0, ALU.mult, ALU.add))
                link(nc.vector.tensor_tensor(f["mean"][:], f["mean"][:], t[f"c{l}"][:], ALU.add))
                link(nc.vector.tensor_tensor(f["tmp"][:], t[f"c{l}"][:], f["mean"][:], ALU.subtract))
                link(nc.vector.tensor_tensor(f["tmp"][:], f["tmp"][:], t["bn_scale"][:], ALU.mult))
                link(nc.vector.tensor_tensor(t["bn_shift"][:], f["tmp"][:], t[f"be{l}"][:], ALU.add))

            @block.scalar
            def _(act):
                def body(i, first, last):
                    for b in range(2):
                        n = 2 * i + b
                        act.wait_ge(h_ready, n + 1)
                        if not first:
                            act.wait_ge(sq_summed, n - 1)
                        nc.scalar.activation(sq[b][:], h[b][:], ACT.Square).then_inc(squared, 1)
                rounds(act, IT, body)
                act.wait_ge(var_ready, 1)
                nc.scalar.activation(f["std"][:], f["var"][:], ACT.Sqrt).then_inc(std_ready, 1)

            @block.tensor
            def _(pe):
                def body(i, first, last):
                    for b in range(2):
                        n = 2 * i + b
                        pe.wait_ge(squared, n + 1)
                        if not first:
                            pe.wait_ge(sq_added, n)
                        for c, w in chunks:
                            m = nc.tensor.matmul(flat(ps[b][:, 0:w, :]), t["ones"][:], flat(sq[b][:, c:c + w, :]),
                                                 start=(c == 0), stop=(c + w == T))
                        m.then_inc(sq_summed, 1)
                rounds(pe, IT, body)
                pe.wait_ge(h_added, NG + 1)
                for c, w in chunks:
                    m = nc.tensor.matmul(flat(psm[:, 0:w, :]), t["ones"][:], flat(acc[:, c:c + w, :]),
                                         start=(c == 0), stop=(c + w == T))
                m.then_inc(acc_summed, 1)


def bn_apply_phase(env, a, t, x, agg, out):
    nc = env.nc
    N = a["x"].shape[0]
    NG = -(-N // GROUP)
    IT = NG // 2
    with env.phase() as ctx:
        ld = Loads(env, ctx, {"x": x, "agg": agg}, N, NG)
        xb, ab = ld.bufs["x"], ld.bufs["agg"]
        o = [env.sb(ctx, f"o{b}", [P, T, D]) for b in range(2)]
        S = env.sem
        scaled, chain, done = S("agg_scaled"), S("apply_chain"), S("apply_done")
        stored = [S(f"apply_stored{b}") for b in range(2)]
        with nc.Block() as block:
            @block.sync
            def _(sp):
                def body(i, first, last):
                    for b in range(2):
                        n = 2 * i + b
                        if not first:
                            sp.wait_ge(done, n - 1)
                        ld.issue(sp, "x", n, b, last)
                        ld.issue(sp, "agg", n, b, last)
                rounds_from_one(sp, IT, body)

            @block.gpsimd
            def _(pool):
                def body(i, first, last):
                    for b in range(2):
                        ld.wait(pool, "agg", i, b, last)
                        nc.gpsimd.tensor_tensor(ab[b][:], ab[b][:], t["bn_scale"][:].unsqueeze(1).to_broadcast([P, T, D]),
                                                ALU.mult).then_inc(scaled, 1)
                rounds(pool, IT, body)

            @block.vector
            def _(dve):
                def body(i, first, last):
                    link = Chain(dve, chain, 4 * i)
                    for b in range(2):
                        n = 2 * i + b
                        ld.wait(dve, "x", i, b, last)
                        if not first:
                            dve.wait_ge(stored[b], 16 * i)
                        link(nc.vector.tensor_tensor(o[b][:], xb[b][:], t["bn_alpha"][:].unsqueeze(1).to_broadcast([P, T, D]), ALU.mult))
                        link(nc.vector.tensor_tensor(o[b][:], o[b][:], t["bn_shift"][:].unsqueeze(1).to_broadcast([P, T, D]), ALU.add))
                        dve.wait_ge(scaled, n + 1)
                        nc.vector.tensor_tensor(o[b][:], o[b][:], ab[b][:], ALU.add).then_inc(done, 1)
                rounds(dve, IT, body)

            @block.scalar
            def _(act):
                def body(i, first, last):
                    for b in range(2):
                        n = 2 * i + b
                        act.wait_ge(done, n + 1)
                        for dram, tile in rows_of(out, o[b], n, N, not (last and b == 1)):
                            act.dma_start(dram, tile).then_inc(stored[b], 16)
                rounds(act, IT, body)
                act.wait_ge(stored[0], 16 * IT)
                act.wait_ge(stored[1], 16 * (IT - 1) + 16 * len(rows_of(out, o[1], NG - 1, N, False)))


def gnn_program(nc, a, out):
    N, E = a["x"].shape[0], a["src"].shape[0]
    NT = E // ROWS
    NPAD = -(-N // GROUP) * GROUP
    Q, F = NT // C4, C4 * ROWS
    x1, x2, x3, x4, agg = (nc.dram_tensor(n, (NPAD, D), F32).ap() for n in ("x1", "x2", "x3", "x4", "agg"))
    edge_rows = nc.dram_tensor("edge_rows", (NT // K * P, K * D), F32).ap()
    with ExitStack() as ctx:
        env = Env(nc, ctx)
        t = {}
        for n in ("gidx", "didx", "sidx", "gidx3", "sidx3"):
            t[n] = env.sb(ctx, n, [P, NT], I32)
        for n in ("row", "nx", "w0", "w1", "has1", "has2", "has3", "logit"):
            t[n] = env.sb(ctx, n, [P, NT])
        for n in ("same", "nsame", "sadd", "nadd"):
            t[n] = env.sb(ctx, n, [Q, F])
        t["flow"] = env.sb(ctx, "flow", [K + 1, NT // K, 2, K + 1])
        t["into"] = env.sb(ctx, "into", [K + 1, K, ROWS + 1])
        t["etype_i"] = env.sb(ctx, "etype_i", [Q, F], I32)
        t["thru"] = env.sb(ctx, "thru", [Q, 4])
        t["one"] = env.sb(ctx, "one", [1, 1])
        t["zero"] = env.sb(ctx, "zero", [1, D])
        t["part"] = env.sb(ctx, "part", [P, 1])
        for n in ("cols", "ident", "ones", "bn_scale", "bn_alpha", "bn_shift", "g0", "g1", "be0", "be1", "bp0", "bp1", "c0", "c1"):
            t[n] = env.sb(ctx, n, [P, P])
        for l in range(2):
            t[f"a{l}"] = env.sb(ctx, f"a{l}", [P, 1])
            t[f"cwi{l}"] = env.sb(ctx, f"cwi{l}", [P, 4, P])
        t["shift"] = env.sb(ctx, "shift", [P, 3, P])

        tables_phase(env, a, t)
        layer3_constants_phase(env, a, t)
        logits_phase(env, a, t, edge_rows, agg, [x1, x2, x3, x4])
        softmax_phase(env, a, t)
        edge_sums_phase(env, a, t, None, agg, 0, edge_rows)
        node_norm_phase(env, a, t, 0, {"x": a["x"], "agg": agg}, x1)
        edge_sums_phase(env, a, t, x1, agg, 1, None)
        node_norm_phase(env, a, t, 1, {"x": x1, "agg": agg}, x2)
        edge_sums_phase(env, a, t, x2, agg, 2, None)
        node_norm_phase(env, a, t, 2, {"x": x2, "agg": agg}, x3)
        edge_sorts_phase(env, a, t, x3, agg, 0)
        bn_stats_phase(env, a, t, x3, agg, 0)
        bn_apply_phase(env, a, t, x3, agg, x4)
        edge_sorts_phase(env, a, t, x4, agg, 1)
        bn_stats_phase(env, a, t, x4, agg, 1)
        node_norm_phase(env, a, t, 3, {"x": x3, "x4": x4, "agg": agg}, out)


_NAMES = {
    "x": "x", "src": "src", "dst": "dst", "edge_attr_16": "ea", "edge_type_8": "etype",
    "L0_gnn_head_w": "head_w", "L0_gnn_head_b": "head_b", "L0_gnn_tail_w": "tail_w", "L0_gnn_tail_b": "tail_b",
    "L0_gnn_rel_w": "rel_w", "L1_gnn_W_self": "W_self", "L1_gnn_W_neigh": "W_neigh", "L1_gnn_b": "b_1",
    "L2_gnn_W": "W2", "L2_gnn_edge_w": "edge_w", "L2_gnn_b": "b_2",
    "L3_gnn_W0": "W3_0", "L3_gnn_b0": "b0", "L3_gnn_cw0": "cw0", "L3_gnn_cb0": "cb0", "L3_gnn_a0": "a0",
    "L3_gnn_g0": "g0", "L3_gnn_be0": "be0", "L3_gnn_blank0": "blank0",
    "L3_gnn_W1": "W3_1", "L3_gnn_b1": "b1", "L3_gnn_cw1": "cw1", "L3_gnn_cb1": "cb1", "L3_gnn_a1": "a1",
    "L3_gnn_g1": "g1", "L3_gnn_be1": "be1", "L3_gnn_blank1": "blank1",
}


def kernel(**inputs):
    import numpy as _np
    import concourse.bacc as _bacc
    from concourse import mybir as _mybir
    from concourse.bass_utils import run_bass_kernel_spmd as _run

    nc = _bacc.Bacc("TRN2", target_bir_lowering=False, num_devices=1)
    arrays, args = {}, {}
    for name, short in _NAMES.items():
        v = _np.ascontiguousarray(inputs[name])
        arrays[f"in_{name}"] = v
        args[short] = nc.dram_tensor(f"in_{name}", v.shape, _mybir.dt.from_np(v.dtype), kind="ExternalInput").ap()
    out = nc.dram_tensor("out_x", inputs["x"].shape, _mybir.dt.float32, kind="ExternalOutput").ap()
    gnn_program(nc, args, out)
    r = _run(nc, [arrays], core_ids=[0])
    return r.results[0]["out_x"]
```

```python
import concourse.bass as bass
from concourse import mybir
from contextlib import ExitStack, contextmanager

F32, I32 = mybir.dt.float32, mybir.dt.int32
ALU, ACT, AX = mybir.AluOpType, mybir.ActivationFunctionType, mybir.AxisListType

P = 128
D = 128
ROWS = 125
K = 8
HALF = K // 2
T = 17
GROUP = P * T
C4 = 4
SKIP = 1 << 23
LOW = -1.0e30
EPS = 1e-5


class Chain:

    def __init__(self, engine, sem, base=0):
        self.engine, self.sem, self.base, self.n = engine, sem, base, 0

    def __call__(self, ins):
        self.n += 1
        ins.then_inc(self.sem, 1)
        self.engine.wait_ge(self.sem, self.base + self.n)


class Env:

    def __init__(self, nc, ctx):
        self.nc, self.ctx, self.count, self.sems = nc, ctx, 0, []

    def sem(self, name):
        self.count += 1
        self.sems.append(self.nc.alloc_semaphore(name=f"{name}_{self.count}"))
        return self.sems[-1]

    @contextmanager
    def phase(self):
        with ExitStack() as ctx:
            yield ctx
        self.nc.clear_and_free_semaphores(self.sems)
        self.nc.all_engine_barrier()
        self.sems = []

    def sb(self, ctx, name, shape, dt=F32):
        self.count += 1
        return ctx.enter_context(self.nc.sbuf_tensor(f"{name}_{self.count}", shape, dt))

    def ps(self, ctx, name, shape):
        self.count += 1
        return ctx.enter_context(self.nc.psum_tensor(f"{name}_{self.count}", shape, F32))


def wait_past(engine, sem, value):
    if not isinstance(value, int) or value > 0:
        engine.wait_ge(sem, value)


def flat(ap):
    return ap.rearrange("p a b -> p (a b)")


def rounds(engine, n, body, peeled=1):
    for i in range(min(peeled, n)):
        body(i, i == 0, i == n - 1)
    if n > peeled + 1:
        with engine.Fori(peeled, n - 1) as i:
            body(i, False, False)
    if n > peeled:
        body(n - 1, False, True)


def tables_phase(env, a, t):
    nc = env.nc
    E = a["src"].shape[0]
    NT = E // ROWS
    Q = NT // C4
    F = C4 * ROWS
    with env.phase() as ctx:
        dsti = env.sb(ctx, "dsti", [Q, F + 4], I32)
        srci = env.sb(ctx, "srci", [Q, F + 4], I32)
        dst = env.sb(ctx, "dst", [Q, F + 4])
        src = env.sb(ctx, "src", [Q, F + 4])
        wk = {n: env.sb(ctx, n, [Q, F]) for n in
              ("head", "lhead", "pos", "dstm", "tmp", "ones", "fwd", "bwd", "has1", "has2", "has3", "sidx3", "headpos")}
        pad = {n: env.sb(ctx, n, [Q, C4, ROWS + 1]) for n in ("gidx", "didx", "sidx", "row", "nx", "w1")}
        iotaf = env.sb(ctx, "iotaf", [Q, F])
        ps = [env.ps(ctx, f"ps{k}", [P, C4, P]) for k in range(6)]
        loaded, filled, iotas = env.sem("tables_loaded"), env.sem("tables_filled"), env.sem("tables_iotas")
        chain, transposed, used = env.sem("tables_chain"), env.sem("tables_transposed"), env.sem("tables_used")
        pe_ready = env.sem("tables_ready_for_pe")
        NB = NT // K
        firsti = env.sb(ctx, "firsti", [K + 1, NT + 1], I32)
        first = env.sb(ctx, "first", [K + 1, NT + 1])
        picked = env.sb(ctx, "picked", [K, NB, K])
        nextcol = env.sb(ctx, "nextcol", [K, NB])
        later = env.sb(ctx, "later", [K, K + 1])
        seg = SegTotals(env, ctx, Q, F)
        N_LOADS = 7
        OUTS = [("gidx", ROWS + 1), ("didx", ROWS + 1), ("sidx", ROWS + 1), ("row", ROWS + 1), ("nx", ROWS + 1),
                ("w1", ROWS + 1), ("has1", ROWS), ("has2", ROWS), ("has3", ROWS), ("sidx3", ROWS), ("gidx3", P)]
        with nc.Block() as block:
            @block.sync
            def _(sp):
                sp.wait_ge(filled, 1)
                with nc.allow_non_contiguous_dma(reason="halo columns"):
                    for tile, dram in ((dsti, a["dst"]), (srci, a["src"])):
                        v = dram.rearrange("(q f) -> q f", q=Q)
                        sp.dma_start(tile[:, 1:F + 1], v[:, :]).then_inc(loaded, 16)
                        sp.dma_start(tile[0:Q - 1, F + 1:F + 4], v[1:Q, 0:3]).then_inc(loaded, 16)
                        if tile is dsti:
                            sp.dma_start(tile[1:Q, 0:1], v[0:Q - 1, F - 1:F]).then_inc(loaded, 16)
                    sp.dma_start(t["etype_i"][:, :], a["etype"].rearrange("(q f) -> q f", q=Q)).then_inc(loaded, 16)
                    sp.dma_start(firsti[:, 0:NT], a["dst"].rearrange("(n p) -> n p", p=ROWS)[:, 0:1].rearrange("n o -> o n")
                                 .to_broadcast([K + 1, NT])).then_inc(loaded, 16)
                sp.wait_ge(loaded, 16 * N_LOADS)

            @block.gpsimd
            def _(pool):
                nc.gpsimd.iota(iotaf[:], [[1, F]], base=0, channel_multiplier=0,
                               allow_small_or_imprecise_dtypes=True)
                nc.gpsimd.iota(t["cols"][:], [[1, P]], base=0, channel_multiplier=0,
                               allow_small_or_imprecise_dtypes=True)
                nc.gpsimd.iota(t["part"][:], [[0, 1]], base=0, channel_multiplier=1,
                               allow_small_or_imprecise_dtypes=True).then_inc(iotas, 1)

            @block.vector
            def _(dve):
                nc.vector.memset(dsti[:], -1)
                nc.vector.memset(firsti[:], -1)
                nc.vector.memset(srci[:], SKIP).then_inc(filled, 1)
                for n in ("gidx", "didx", "sidx", "gidx3", "sidx3"):
                    nc.vector.memset(t[n][:], SKIP)
                for n in ("row", "nx", "w1", "w0", "has1", "has2", "has3"):
                    nc.vector.memset(t[n][:], 0.0)
                nc.vector.memset(t["one"][:], 1.0)
                nc.vector.memset(wk["ones"][:], 1.0)
                for n in ("gidx", "didx", "sidx"):
                    nc.vector.memset(pad[n][:, :, 0:1], float(SKIP))
                for n in ("row", "nx", "w1"):
                    nc.vector.memset(pad[n][:, :, 0:1], 0.0)
                link = Chain(dve, chain)
                dve.wait_ge(iotas, 1)
                link(nc.vector.tensor_scalar(t["ident"][:], t["cols"][:], t["part"][:, 0:1], None, ALU.is_equal))
                dve.wait_ge(loaded, 16 * N_LOADS)
                link(nc.vector.tensor_copy(dst[:], dsti[:]))
                link(nc.vector.tensor_copy(src[:], srci[:]))
                me, before, after = dst[:, 1:F + 1], dst[:, 0:F], dst[:, 2:F + 2]
                me4 = me.rearrange("q (c p) -> q c p", c=C4)
                link(nc.vector.tensor_tensor(t["same"][:], me, before, ALU.is_equal))
                link(nc.vector.tensor_tensor(t["nsame"][:], me, after, ALU.is_equal))
                link(nc.vector.tensor_scalar(t["sadd"][:], t["same"][:], -LOW, LOW, ALU.mult, ALU.add))
                link(nc.vector.tensor_scalar(t["nadd"][:], t["nsame"][:], -LOW, LOW, ALU.mult, ALU.add))
                link(nc.vector.tensor_tensor(t["thru"][:, 0:1], dst[:, F:F + 1], dst[:, 0:1], ALU.is_equal))
                link(nc.vector.tensor_tensor(t["thru"][:, 1:2], dst[:, 1:2], dst[:, F + 1:F + 2], ALU.is_equal))
                link(nc.vector.tensor_scalar(t["thru"][:, 2:4], t["thru"][:, 0:2], -LOW, LOW, ALU.mult, ALU.add))
                nxt = dst[:, ROWS + 1:F + 2:ROWS].unsqueeze(2)
                link(nc.vector.tensor_tensor(pad["nx"][:, :, 1:], me4, nxt.to_broadcast([Q, C4, ROWS]), ALU.is_equal))
                link(nc.vector.tensor_copy(first[:], firsti[:]))
                link(nc.vector.memset(t["flow"][:], 0.0))
                nextk = first[0:K, 1:NT + 1].rearrange("j (n k) -> j n k", k=K)
                link(nc.vector.tensor_tensor(picked[:], nextk,
                                             t["ident"][0:K, 0:K].unsqueeze(1).to_broadcast([K, NB, K]), ALU.mult))
                link(nc.vector.tensor_reduce(nextcol[:], picked[:], AX.X, ALU.add))
                link(nc.vector.tensor_scalar(later[:], t["cols"][0:K, 0:K + 1], t["part"][0:K, 0:1], None, ALU.is_gt))
                for rows, col in ((K, nextcol[:]), (K + 1, first[:, 0:NT:K])):
                    to = t["flow"][0:rows, :, 0, :] if rows == K else t["flow"][0:rows, :, 1, :]
                    link(nc.vector.tensor_tensor(to[:, :, 0:K], first[0:rows, 0:NT].rearrange("j (n k) -> j n k", k=K),
                                                 col.unsqueeze(2).to_broadcast([rows, NB, K]), ALU.is_equal))
                    link(nc.vector.tensor_tensor(to[:, :, K:K + 1], first[0:rows, K:NT + 1:K].unsqueeze(2),
                                                 col.unsqueeze(2), ALU.is_equal))
                link(nc.vector.tensor_tensor(t["flow"][0:K, :, 0, :], t["flow"][0:K, :, 0, :],
                                             later[:].unsqueeze(1).to_broadcast([K, NB, K + 1]), ALU.mult))
                link(nc.vector.tensor_scalar(t["flow"][0:K + 1, :, 1, :], t["flow"][0:K + 1, :, 1, :],
                                             t["ident"][0:K + 1, K:K + 1], None, ALU.mult))
                for k in range(K):
                    link(nc.vector.tensor_scalar(t["into"][:, k, :], t["cols"][0:K + 1, 0:ROWS + 1], 1.0,
                                                 t["ident"][0:K + 1, k:k + 1], ALU.is_equal, ALU.mult))
                link(nc.vector.tensor_scalar(wk["head"][:], t["same"][:], -1.0, 1.0, ALU.mult, ALU.add))
                link(nc.vector.tensor_copy(wk["lhead"][:], wk["head"][:]))
                link(nc.vector.memset(wk["lhead"][:, 0:F:ROWS], 1.0))
                link(nc.vector.tensor_tensor(wk["tmp"][:], wk["lhead"][:], iotaf[:], ALU.mult))
                link(nc.vector.memset(wk["dstm"][:], 0.0))
                link(nc.vector.tensor_tensor_scan(wk["headpos"][:], wk["dstm"][:], wk["tmp"][:], 0.0, ALU.add, ALU.max))
                for c in range(C4):
                    link(nc.vector.tensor_scalar(pad["row"][:, c, 1:], wk["headpos"][:, c * ROWS:(c + 1) * ROWS],
                                                 float(1 - c * ROWS), None, ALU.add))
                link(nc.vector.tensor_scalar(wk["dstm"][:], me, float(-SKIP), None, ALU.add))
                link(nc.vector.tensor_scalar(pad["sidx"][:, :, 1:], pad["nx"][:, :, 1:], -1.0, 1.0, ALU.mult, ALU.add))
                link(nc.vector.tensor_tensor(pad["sidx"][:, :, 1:], pad["sidx"][:, :, 1:],
                                             wk["lhead"][:].rearrange("q (c p) -> q c p", c=C4), ALU.mult))
                link(nc.vector.tensor_tensor(pad["sidx"][:, :, 1:], pad["sidx"][:, :, 1:],
                                             wk["dstm"][:].rearrange("q (c p) -> q c p", c=C4), ALU.mult))
                link(nc.vector.tensor_scalar(pad["sidx"][:, :, 1:], pad["sidx"][:, :, 1:], float(SKIP), None, ALU.add))
                link(nc.vector.tensor_copy(pad["gidx"][:, :, 1:], src[:, 1:F + 1].rearrange("q (c p) -> q c p", c=C4)))
                link(nc.vector.tensor_copy(pad["didx"][:, :, 1:], me4))
                link(nc.vector.tensor_tensor(wk["sidx3"][:], wk["head"][:], wk["dstm"][:], ALU.mult))
                link(nc.vector.tensor_scalar(wk["sidx3"][:], wk["sidx3"][:], float(SKIP), None, ALU.add))
                seg.vector(link, dve, t, wk["ones"][:], wk["fwd"][:], wk["bwd"][:], "sum")
                for k in (1, 2, 3):
                    link(nc.vector.tensor_scalar(wk[f"has{k}"][:], wk["fwd"][:], k + 0.5, None, ALU.is_gt))
                nc.vector.reciprocal(pad["w1"][:, :, 1:], wk["fwd"][:].rearrange("q (c p) -> q c p", c=C4)
                                     ).then_inc(pe_ready, 1)
                for j, (n, rows) in enumerate(OUTS):
                    dve.wait_ge(transposed, j + 1)
                    nc.vector.tensor_copy(t[n][0:rows, :].rearrange("p (q c) -> p c q", c=C4),
                                          ps[j % 6][0:rows, :, 0:Q]).then_inc(used, 1)
                dve.wait_ge(used, len(OUTS))

            @block.tensor
            def _(pe):
                seg.tensor(pe, t, 0)
                pe.wait_ge(pe_ready, 1)
                for j, (n, rows) in enumerate(OUTS):
                    if j >= 6:
                        pe.wait_ge(used, j - 5)
                    for c in range(C4):
                        if n == "gidx3":
                            s = src[:, 1 + c * ROWS:1 + c * ROWS + P]
                        elif n in pad:
                            s = pad[n][:, c, :]
                        else:
                            s = wk[n][:, c * ROWS:(c + 1) * ROWS]
                        last = nc.tensor.transpose(ps[j % 6][0:rows, c, 0:Q], s, t["ident"][0:Q, 0:Q])
                    last.then_inc(transposed, 1)


class SegTotals:

    def __init__(self, env, ctx, Q, F):
        self.env, self.Q, self.F = env, Q, F
        self.row = env.sb(ctx, "seg_row", [1, 2, P])
        self.carry = env.sb(ctx, "seg_carry", [1, P + 1])
        self.cin = env.sb(ctx, "seg_cin", [P, 1])
        self.psr = env.ps(ctx, "seg_psr", [P, 2, P])
        self.psc = env.ps(ctx, "seg_psc", [P, 1])
        self.ready = env.sem("seg_column_ready")
        self.rows = env.sem("seg_rows_transposed")
        self.scanned = env.sem("seg_carries_scanned")
        self.cols = env.sem("seg_carry_column_done")
        self.ask = []
        self.calls = 0

    def vector(self, link, dve, t, val, fwd, bwd, kind):
        nc, Q, F = self.env.nc, self.Q, self.F
        if kind == "max":
            op0, op1, init, d0, thru = ALU.add, ALU.max, LOW, ("sadd", "nadd"), (2, 3)
        else:
            op0, op1, init, d0, thru = ALU.mult, ALU.add, 0.0, ("same", "nsame"), (0, 1)
        for side, out in ((0, fwd), (1, bwd)):
            def way(ap):
                return ap[:, ::-1] if side else ap
            last = out[:, 0:1] if side else out[:, F - 1:F]
            link(nc.vector.tensor_tensor_scan(way(out), way(t[d0[side]][:]), way(val), init, op0, op1))
            self.ask.append((last, thru[side], side))
            nc.vector.memset(self.carry[:], init).then_inc(self.ready, 1)
            self.calls += 1
            n = self.calls
            dve.wait_ge(self.rows, n)
            link(nc.vector.tensor_copy(self.row[:, :, 0:Q], self.psr[0:1, :, 0:Q]))
            to = self.carry[:, 0:Q] if side else self.carry[:, 1:Q + 1]
            nc.vector.tensor_tensor_scan(way(to), way(self.row[:, 1, 0:Q]), way(self.row[:, 0, 0:Q]),
                                         init, op0, op1).then_inc(self.scanned, 1)
            dve.wait_ge(self.cols, n)
            link(nc.vector.tensor_copy(self.cin[0:Q, :], self.psc[0:Q, :]))
            link(nc.vector.tensor_tensor_scan(way(out), way(t[d0[side]][:]), way(val), self.cin[0:Q, 0:1], op0, op1))
        if kind == "max":
            link(nc.vector.tensor_tensor(fwd, fwd, bwd, ALU.max))
        else:
            link(nc.vector.tensor_tensor(fwd, fwd, bwd, ALU.add))
            link(nc.vector.tensor_tensor(fwd, fwd, val, ALU.subtract))

    def tensor(self, pe, t, since):
        nc, Q = self.env.nc, self.Q
        for n, (last, thru, side) in enumerate(self.ask[since:], since):
            pe.wait_ge(self.ready, n + 1)
            nc.tensor.transpose(self.psr[0:1, 0, 0:Q], last, t["ident"][0:Q, 0:Q])
            nc.tensor.transpose(self.psr[0:1, 1, 0:Q], t["thru"][:, thru:thru + 1],
                                t["ident"][0:Q, 0:Q]).then_inc(self.rows, 1)
            pe.wait_ge(self.scanned, n + 1)
            nc.tensor.matmul(self.psc[0:Q, :], self.carry[0:1, side:side + Q], t["one"][0:1, 0:1],
                             start=True, stop=True).then_inc(self.cols, 1)


def logits_phase(env, a, t, edge_rows, agg, scratch):
    nc, x = env.nc, a["x"]
    N, E = x.shape[0], a["src"].shape[0]
    NB = E // (ROWS * K)
    NG = agg.shape[0] // GROUP
    ZB = -(-NG // (NB // 2))
    with env.phase() as ctx:
        g = [env.sb(ctx, f"rows_src_dst{b}", [P, K, 2, D]) for b in range(2)]
        prod = env.sb(ctx, "prod", [P, K, 2 * D])
        w = env.sb(ctx, "head_tail_w", [P, 2 * D])
        zeros = env.sb(ctx, "zeros", [P, T * D])
        idx = [env.sb(ctx, f"idx{b}", [P, 2, K], I32) for b in range(2)]
        begun = env.sem("dma_series_begun")
        cleared, idx_ready, w_loaded = env.sem("cleared"), env.sem("idx_ready"), env.sem("w_loaded")
        gathered = [env.sem(f"gathered{b}") for b in range(2)]
        stored = [env.sem(f"stored{b}") for b in range(2)]
        used, multiplied, zeroed = env.sem("rows_used"), env.sem("multiplied"), env.sem("zeroed")
        with nc.Block() as block:
            @block.gpsimd
            def _(pool):
                bound = pool.to_reg(N - 1)

                def body(i, first, last):
                    for b in range(2):
                        n = 2 * i + b
                        pool.wait_ge(idx_ready, n + 1)
                        if not first:
                            pool.wait_ge(used, n - 1)
                            pool.wait_ge(stored[b], 16 * i)
                        pool.sem_inc(begun, 1)
                        for k in range(K):
                            for s in range(2):
                                pool.indirect_dma_start(
                                    out=g[b][:, k, s, :], out_offset=None, in_=x[:, :],
                                    in_offset=bass.IndirectOffsetOnAxis(ap=idx[b][:, s, k:k + 1], axis=0),
                                    bounds_check=bound, oob_is_err=False).then_inc(gathered[b], 16)
                pool.wait_ge(cleared, 1)
                rounds(pool, NB // 2, body)

            @block.sync
            def _(sp):
                sp.dma_start(w[:, 0:D], a["head_w"].unsqueeze(0).to_broadcast([P, D])).then_inc(w_loaded, 16)
                sp.dma_start(w[:, D:], a["tail_w"].unsqueeze(0).to_broadcast([P, D])).then_inc(w_loaded, 16)

                def body(i, first, last):
                    for b in range(2):
                        n = 2 * i + b
                        sp.wait_ge(gathered[b], 16 * 2 * K * (i + 1))
                        sp.dma_start(edge_rows[bass.ds(n * P, P), :].rearrange("p (k d) -> p k d", k=K),
                                     g[b][:, :, 0, :]).then_inc(stored[b], 16)
                rounds(sp, NB // 2, body)
                for b in range(2):
                    sp.wait_ge(stored[b], 16 * (NB // 2))
                sp.wait_ge(w_loaded, 32)

            @block.scalar
            def _(act):
                act.wait_ge(cleared, 1)
                pads = scratch[0].shape[0] - N
                for s in scratch:
                    act.dma_start(s[N:N + pads, :], zeros[0:pads, 0:D]).then_inc(zeroed, 16)
                zero_groups = NG // ZB
                with act.Fori(0, zero_groups) as i:
                    act.wait_ge(used, (i + 1) * (NB // zero_groups))
                    for z in range(ZB):
                        act.dma_start(agg[bass.ds((i * ZB + z) * GROUP, GROUP), :].rearrange("(p t) d -> p (t d)", p=P),
                                      zeros[:, :]).then_inc(zeroed, 16)
                act.wait_ge(zeroed, 16 * (zero_groups * ZB + len(scratch)))

            @block.vector
            def _(dve):
                nc.vector.memset(g[0][:], 0.0)
                nc.vector.memset(g[1][:], 0.0)
                nc.vector.memset(zeros[:], 0.0).then_inc(cleared, 1)

                def indices(i, b, free):
                    if free:
                        dve.wait_ge(gathered[b], 16 * 2 * K * i)
                    nc.vector.tensor_copy(idx[b][:, 0, :], t["gidx"][:, bass.ds((2 * i + b) * K, K)])
                    nc.vector.tensor_copy(idx[b][:, 1, :], t["didx"][:, bass.ds((2 * i + b) * K, K)]).then_inc(idx_ready, 1)

                def body(i, first, last):
                    for b in range(2):
                        n = 2 * i + b
                        dve.wait_ge(gathered[b], 16 * 2 * K * (i + 1))
                        if not (first and b == 0):
                            dve.wait_ge(used, n)
                        nc.vector.tensor_tensor(prod[:], g[b][:].rearrange("p k s d -> p k (s d)"),
                                                w[:].unsqueeze(1).to_broadcast([P, K, 2 * D]), ALU.mult).then_inc(multiplied, 1)
                        if not last:
                            indices(i + 1, b, True)
                        dve.wait_ge(multiplied, n + 1)
                        nc.vector.tensor_reduce(t["logit"][:, bass.ds(n * K, K)], prod[:], AX.X, ALU.add).then_inc(used, 1)
                indices(0, 0, False)
                indices(0, 1, False)
                dve.wait_ge(w_loaded, 32)
                rounds(dve, NB // 2, body)
                dve.wait_ge(used, NB)


def softmax_phase(env, a, t):
    nc = env.nc
    E = a["src"].shape[0]
    NT = E // ROWS
    Q = NT // C4
    F = C4 * ROWS
    NR = a["rel_w"].shape[0]
    with env.phase() as ctx:
        lg, ex, fwd, bwd, et = (env.sb(ctx, n, [Q, F]) for n in ("lg", "ex", "fwd", "bwd", "et"))
        w = env.sb(ctx, "w0pad", [Q, C4, ROWS + 1])
        sc = env.sb(ctx, "rel_and_biases", [P, NR + 2])
        psl = env.ps(ctx, "psl", [P, C4, P])
        psw = env.ps(ctx, "psw", [P, C4, P])
        loaded, to_edges, ready, done = (env.sem(n) for n in ("sm_loaded", "sm_to_edges", "sm_ready", "sm_to_rows"))
        shifted, expd, chain = env.sem("sm_shifted"), env.sem("sm_exp"), env.sem("sm_chain")
        seg = SegTotals(env, ctx, Q, F)
        with nc.Block() as block:
            @block.sync
            def _(sp):
                for dram, lo, hi in ((a["rel_w"], 0, NR), (a["head_b"], NR, NR + 1), (a["tail_b"], NR + 1, NR + 2)):
                    sp.dma_start(sc[:, lo:hi], dram.unsqueeze(0).to_broadcast([P, hi - lo])).then_inc(loaded, 16)
                sp.wait_ge(loaded, 48)

            @block.vector
            def _(dve):
                link = Chain(dve, chain)
                dve.wait_ge(to_edges, 1)
                link(nc.vector.tensor_copy(lg[:].rearrange("q (c p) -> q c p", c=C4), psl[0:Q, :, 1:ROWS + 1]))
                link(nc.vector.tensor_copy(et[:], t["etype_i"][:, :]))
                dve.wait_ge(loaded, 48)
                link(nc.vector.tensor_scalar(lg[:], lg[:], sc[0:Q, NR:NR + 1], sc[0:Q, NR + 1:NR + 2], ALU.add, ALU.add))
                for r in range(NR):
                    link(nc.vector.tensor_scalar(ex[:], et[:], float(r), sc[0:Q, r:r + 1], ALU.is_equal, ALU.mult))
                    link(nc.vector.tensor_tensor(lg[:], lg[:], ex[:], ALU.add))
                seg.vector(link, dve, t, lg[:], fwd[:], bwd[:], "max")
                nc.vector.tensor_tensor(lg[:], lg[:], fwd[:], ALU.subtract).then_inc(shifted, 1)
                dve.wait_ge(expd, 1)
                seg.vector(link, dve, t, ex[:], fwd[:], bwd[:], "sum")
                link(nc.vector.reciprocal(fwd[:], fwd[:]))
                link(nc.vector.memset(w[:, :, 0:1], 0.0))
                nc.vector.tensor_tensor(w[:, :, 1:], ex[:].rearrange("q (c p) -> q c p", c=C4),
                                        fwd[:].rearrange("q (c p) -> q c p", c=C4), ALU.mult).then_inc(ready, 1)
                dve.wait_ge(done, 1)
                link(nc.vector.tensor_copy(t["w0"][0:ROWS + 1, :].rearrange("p (q c) -> p c q", c=C4),
                                           psw[0:ROWS + 1, :, 0:Q]))

            @block.scalar
            def _(act):
                act.wait_ge(shifted, 1)
                nc.scalar.activation(ex[:], lg[:], ACT.Exp).then_inc(expd, 1)

            @block.tensor
            def _(pe):
                by_tile = t["logit"][:].rearrange("p (q c) -> p c q", c=C4)
                for c in range(C4):
                    last = nc.tensor.transpose(psl[0:Q, c, :], by_tile[:, c, :], t["ident"][:])
                last.then_inc(to_edges, 1)
                seg.tensor(pe, t, 0)
                pe.wait_ge(ready, 1)
                for c in range(C4):
                    last = nc.tensor.transpose(psw[0:ROWS + 1, c, 0:Q], w[:, c, :], t["ident"][0:Q, 0:Q])
                last.then_inc(done, 1)


def edge_sums_phase(env, a, t, table, agg, layer, edge_rows):
    nc = env.nc
    N, E = a["x"].shape[0], a["src"].shape[0]
    NB = E // (ROWS * K)
    IT = NB // 2
    R1 = ROWS + 1
    K1 = K + 1
    gated, projected = layer == 2, layer == 1
    gathers = layer != 0
    weights = {0: "w0", 1: "w1", 2: None}[layer]
    with env.phase() as ctx:
        g = [env.sb(ctx, f"rows{b}", [P, K, D]) for b in range(2)]
        r = [env.sb(ctx, f"messages{b}", [P, K, D]) for b in range(2)] if gated else g
        s = [env.sb(ctx, f"onehot{b}", [P, K, R1]) for b in range(2)]
        over = [env.sb(ctx, f"goes_on{b}", [P, K * K]) for b in range(2)]
        flow = [env.sb(ctx, f"flow{b}", [K1, 2, K1]) for b in range(2)]
        left = [env.sb(ctx, f"left{b}", [K, D]) for b in range(2)]
        came = [env.sb(ctx, f"came{b}", [K1, D]) for b in range(2)]
        res = [env.sb(ctx, f"sums{b}", [P, K, D]) for b in range(2)]
        gi = [env.sb(ctx, f"gi{b}", [P, K], I32) for b in range(2)]
        si = [env.sb(ctx, f"si{b}", [P, K], I32) for b in range(2)]
        acc = [env.ps(ctx, f"acc{b}", [P, K, D]) for b in range(2)]
        small = env.ps(ctx, "small", [P, 3, D])
        psl, psa = small[0:K1, 0:2, :], small[:, 2, 0:R1]
        if gated or projected:
            mat = env.sb(ctx, "mat", [P, D])
            rt = [env.sb(ctx, f"transposed{h}", [P, HALF, P]) for h in range(2)]
            pst = env.ps(ctx, "pst", [P, HALF, P])
            psx = [env.ps(ctx, f"psx{h}", [P, HALF, D]) for h in range(2 if projected else 1)]
        if projected:
            raw = [env.sb(ctx, f"raw_sums{b}", [P, K, D]) for b in range(2)]
        if gated:
            ea = [env.sb(ctx, f"ea{b}", [P, K, a["ea"].shape[1]]) for b in range(2)]
            eat = [env.sb(ctx, f"eat{b}", [P, R1]) for b in range(2)]
            ew = env.sb(ctx, "edge_w_blocks", [P, K, D])
            ews = [env.sb(ctx, f"gates{h}", [P, HALF, D]) for h in range(2)]
            pse = env.ps(ctx, "pse", [P, HALF, D])
        S = env.sem
        arrived = [S(f"rows_arrived{b}") for b in range(2)]
        scattered = [S(f"scattered{b}") for b in range(2)]
        ea_loaded = [S(f"ea_loaded{b}") for b in range(2)]
        pe_begun = S("flow_begun")
        begun, cleared, gi_ready, onehot_ready, compared = (
            S("dma_series_begun"), S("cleared"), S("gi_ready"), S("onehot_ready"), S("compared"))
        left_summed, left_copied, came_summed, came_copied, summed, res_ready = (
            S("left_summed"), S("left_copied"), S("came_summed"), S("came_copied"), S("summed"), S("res_ready"))
        mats, transposed, tcopied, product, product_used, raw_ready = (
            S("mats_loaded"), S("transposed"), S("transposed_copied"), S("product"), S("product_used"), S("raw_ready"))
        ea_transposed, ea_copied, gates_done, gates_copied = (
            S("ea_transposed"), S("ea_copied"), S("gates_done"), S("gates_copied"))
        PER = 16 * (K if gathers else 1)
        EW = a["ea"].shape[1]
        MATS = 16 * (1 + (K if gated else 0))
        with nc.Block() as block:
            @block.gpsimd
            def _(pool):
                bound = pool.to_reg(N - 1)

                def scatter(n, b):
                    if projected:
                        pool.wait_ge(product_used, 2 * n + 2)
                    else:
                        pool.wait_ge(res_ready, n + 1)
                    pool.sem_inc(begun, 1)
                    for k in range(K):
                        pool.indirect_dma_start(
                            out=agg[0:N, :], out_offset=bass.IndirectOffsetOnAxis(ap=si[b][:, k:k + 1], axis=0),
                            in_=res[b][:, k, :], in_offset=None,
                            bounds_check=bound, oob_is_err=False).then_inc(scattered[b], 16)

                def body(i, first, last):
                    for b in range(2):
                        n = 2 * i + b
                        if gathers:
                            pool.wait_ge(gi_ready, n + 1)
                            if gated:
                                wait_past(pool, transposed, 2 * (n - 1))
                            else:
                                wait_past(pool, summed, n - 1)
                            pool.sem_inc(begun, 1)
                            for k in range(K):
                                pool.indirect_dma_start(
                                    out=g[b][:, k, :], out_offset=None, in_=table[0:N, :],
                                    in_offset=bass.IndirectOffsetOnAxis(ap=gi[b][:, k:k + 1], axis=0),
                                    bounds_check=bound, oob_is_err=False).then_inc(arrived[b], 16)
                        if not first:
                            scatter(n - 2, b)
                pool.wait_ge(cleared, 1)
                rounds(pool, IT, body, peeled=2)
                for b in range(2):
                    scatter(NB - 2 + b, b)
                for b in range(2):
                    pool.wait_ge(scattered[b], 16 * K * IT)

            @block.sync
            def _(sp):
                sp.wait_ge(cleared, 1)
                if gated or projected:
                    sp.dma_start(mat[:], (a["W2"] if gated else a["W_neigh"])[:, :]).then_inc(mats, 16)
                if gated:
                    for k in range(K):
                        sp.dma_start(ew[EW * k:EW * (k + 1), k, :], a["edge_w"][:, :]).then_inc(mats, 16)

                def body(i, first, last):
                    for b in range(2):
                        n = 2 * i + b
                        if not gathers:
                            wait_past(sp, summed, n - 1)
                            sp.dma_start(flat(g[b][:]), edge_rows[bass.ds(n * P, P), :]).then_inc(arrived[b], 16)
                        if gated:
                            wait_past(sp, ea_transposed, n - 1)
                            e0 = n * (K * ROWS)
                            with nc.allow_non_contiguous_dma(reason="rows of edge attributes"):
                                sp.dma_start(ea[b][0:ROWS, :, :],
                                             a["ea"][bass.ds(e0, K * ROWS), :].rearrange("(k p) j -> p k j", k=K)
                                             ).then_inc(ea_loaded[b], 16)
                if gated or not gathers:
                    rounds(sp, IT, body, peeled=2)
                if gated or projected:
                    sp.wait_ge(mats, MATS)

            @block.tensor
            def _(pe):
                if gated or projected:
                    pe.wait_ge(mats, MATS)

                def through_matrix(n, h):
                    pe.wait_ge(tcopied, 2 * n + h + 1)
                    for k in range(HALF):
                        last = nc.tensor.matmul(psx[h % len(psx)][0:R1, k, :], rt[h][:, k, 0:R1], mat[:],
                                                start=True, stop=True)
                    last.then_inc(product, 1)

                def pre(n, i, b):
                    pe.wait_ge(ea_loaded[b], 16 * (i + 1))
                    nc.tensor.transpose(psa[:, 0:ROWS], flat(ea[b][0:ROWS, :, :]), t["ident"][0:ROWS, 0:ROWS]
                                        ).then_inc(ea_transposed, 1)
                    pe.wait_ge(arrived[b], PER * (i + 1))
                    for h in range(2):
                        c = 2 * n + h
                        wait_past(pe, tcopied, c)
                        for k in range(HALF):
                            last = nc.tensor.transpose(pst[:, k, 0:R1], g[b][0:R1, h * HALF + k, :],
                                                       t["ident"][0:R1, 0:R1])
                        last.then_inc(transposed, 1)
                        if h == 0:
                            pe.wait_ge(ea_copied, n + 1)
                        wait_past(pe, gates_copied, c)
                        for k in range(HALF):
                            last = nc.tensor.matmul(pse[0:R1, k, :], eat[b][:, :], ew[:, h * HALF + k, :],
                                                    start=True, stop=True)
                        last.then_inc(gates_done, 1)
                        wait_past(pe, product_used, c)
                        through_matrix(n, h)

                def sum_left(n, i, b):
                    pe.wait_ge(onehot_ready, n + 1)
                    if gated:
                        pe.wait_ge(product_used, 2 * n + 2)
                    else:
                        pe.wait_ge(arrived[b], PER * (i + 1))
                    for k in range(K):
                        last = nc.tensor.matmul(psl[0:K, 0, :], over[b][0:R1, k * K:(k + 1) * K], r[b][0:R1, k, :],
                                                start=(k == 0), stop=(k == K - 1))
                    last.then_inc(left_summed, 1)

                def pass_on(n, b):
                    pe.wait_ge(left_copied, n + 1)
                    pe.sem_inc(pe_begun, 1)
                    nc.tensor.matmul(psl[:, 1, :], flow[b][0:K, 0, :], left[b][:], start=True, stop=False)
                    nc.tensor.matmul(psl[:, 1, :], flow[b][:, 1, :], came[1 - b][:], start=False, stop=True
                                     ).then_inc(came_summed, 1)

                def sum_tiles(n, b, h):
                    if h == 0:
                        wait_past(pe, raw_ready if projected else res_ready, n - 1)
                    for k in range(h * HALF, (h + 1) * HALF):
                        nc.tensor.matmul(acc[b][0:R1, k, :], s[b][0:R1, k, :], r[b][0:R1, k, :],
                                         start=(k == h * HALF), stop=False)

                def add_came(n, b):
                    pe.wait_ge(came_copied, n + 1)
                    for k in range(K):
                        last = nc.tensor.matmul(acc[b][0:R1, k, :], t["into"][:, k, :], came[b][:], start=False,
                                                stop=(k % HALF == HALF - 1))
                    last.then_inc(summed, 1)

                def transpose_sums(n, h, b):
                    if h == 0:
                        pe.wait_ge(raw_ready, n + 1)
                    wait_past(pe, tcopied, 2 * n + h)
                    for k in range(HALF):
                        last = nc.tensor.transpose(pst[:, k, 0:R1], raw[b][0:R1, h * HALF + k, :],
                                                   t["ident"][0:R1, 0:R1])
                    last.then_inc(transposed, 1)

                def project(n, h):
                    wait_past(pe, product_used, 2 * n + h - 1)
                    through_matrix(n, h)

                def body(i, first, last):
                    for b in range(2):
                        n = 2 * i + b
                        behind = projected and not (first and b == 0)
                        if gated:
                            pre(n, i, b)
                        sum_left(n, i, b)
                        if behind:
                            transpose_sums(n - 1, 0, 1 - b)
                        sum_tiles(n, b, 0)
                        pass_on(n, b)
                        if behind:
                            project(n - 1, 0)
                            transpose_sums(n - 1, 1, 1 - b)
                        sum_tiles(n, b, 1)
                        add_came(n, b)
                        if behind:
                            project(n - 1, 1)
                rounds(pe, IT, body, peeled=2)
                if projected:
                    for h in range(2):
                        transpose_sums(NB - 1, h, 1)
                        project(NB - 1, h)

            @block.scalar
            def _(act):
                def transposed_rows(n, h):
                    act.wait_ge(transposed, 2 * n + h + 1)
                    nc.scalar.copy(rt[h][:, :, 0:R1], pst[:, :, 0:R1]).then_inc(tcopied, 1)

                def body(i, first, last):
                    for b in range(2):
                        n = 2 * i + b
                        if gated:
                            act.wait_ge(ea_transposed, n + 1)
                            nc.scalar.copy(eat[b][:, 1:R1], psa[:, 0:ROWS]).then_inc(ea_copied, 1)
                            for h in range(2):
                                transposed_rows(n, h)
                                act.wait_ge(gates_done, 2 * n + h + 1)
                                wait_past(act, product_used, 2 * n + h - 1)
                                nc.scalar.copy(ews[h][0:R1, :, :], pse[0:R1, :, :]).then_inc(gates_copied, 1)
                        act.wait_ge(left_summed, n + 1)
                        nc.scalar.copy(left[b][:], psl[0:K, 0, :]).then_inc(left_copied, 1)
                        if projected and not (first and b == 0):
                            transposed_rows(n - 1, 0)
                        act.wait_ge(came_summed, n + 1)
                        nc.scalar.copy(came[b][:], psl[:, 1, :]).then_inc(came_copied, 1)
                        if projected and not (first and b == 0):
                            transposed_rows(n - 1, 1)
                act.wait_ge(cleared, 1)
                rounds(act, IT, body, peeled=2)
                if projected:
                    for h in range(2):
                        transposed_rows(NB - 1, h)

            @block.vector
            def _(dve):
                nc.vector.memset(came[1][:], 0.0)
                for b in range(2):
                    nc.vector.memset(g[b][:], 0.0)
                    nc.vector.memset(res[b][:], 0.0)
                    nc.vector.memset(over[b][:], 0.0)
                    if gated:
                        nc.vector.memset(eat[b][:], 0.0)
                    last_clear = nc.vector.memset(s[b][:], 0.0)
                if gated:
                    last_clear = nc.vector.memset(ew[:], 0.0)
                last_clear.then_inc(cleared, 1)
                dve.wait_ge(cleared, 1)

                def gather_indices(n, i, b):
                    if gathers:
                        wait_past(dve, arrived[b], PER * i)
                        nc.vector.tensor_copy(gi[b][:], t["gidx"][:, bass.ds(n * K, K)]).then_inc(gi_ready, 1)

                def onehots(n, b):
                    at = bass.ds(n * K, K)
                    wait_past(dve, summed, n - 1)
                    row = t["row"][:, at].unsqueeze(2).to_broadcast([P, K, ROWS])
                    cols = t["cols"][:, 1:R1].unsqueeze(1).to_broadcast([P, K, ROWS])
                    nc.vector.tensor_copy(flow[b][:].rearrange("j a k -> j (a k)"),
                                          t["flow"][:].rearrange("j n a k -> j (n a k)")[:, bass.ds(n * (2 * K1), 2 * K1)])
                    one = nc.vector.tensor_tensor(s[b][:, :, 1:R1], row, cols, ALU.is_equal)
                    diagonal = over[b][:, 0:K * K:K + 1]
                    if weights:
                        one.then_inc(compared, 1)
                        nc.vector.tensor_tensor(diagonal, t["nx"][:, at], t[weights][:, at], ALU.mult)
                        dve.wait_ge(compared, n + 1)
                        nc.vector.tensor_tensor(s[b][:, :, 1:R1], s[b][:, :, 1:R1],
                                                t[weights][:, at].unsqueeze(2).to_broadcast([P, K, ROWS]),
                                                ALU.mult).then_inc(onehot_ready, 1)
                    else:
                        nc.vector.tensor_copy(diagonal, t["nx"][:, at]).then_inc(onehot_ready, 1)

                def gate(n, b):
                    for h in range(2):
                        c = 2 * n + h
                        dve.wait_ge(product, c + 1)
                        dve.wait_ge(gates_copied, c + 1)
                        nc.vector.tensor_tensor(r[b][0:R1, h * HALF:(h + 1) * HALF, :], psx[0][0:R1, :, :],
                                                ews[h][0:R1, :, :], ALU.mult).then_inc(product_used, 1)

                def scatter_indices(n, i, b):
                    wait_past(dve, scattered[b], 16 * K * i)
                    nc.vector.tensor_copy(si[b][:], t["sidx"][:, bass.ds(n * K, K)])

                def finish(n, i, b):
                    dve.wait_ge(summed, n + 1)
                    if projected:
                        wait_past(dve, transposed, 2 * (n - 1))
                        nc.vector.tensor_copy(flat(raw[b][0:R1, :, :]), flat(acc[b][0:R1, :, :])).then_inc(raw_ready, 1)
                    else:
                        scatter_indices(n, i, b)
                        nc.vector.tensor_copy(flat(res[b][0:R1, :, :]), flat(acc[b][0:R1, :, :])).then_inc(res_ready, 1)

                def projections(n, i, b):
                    scatter_indices(n, i, b)
                    for h in range(2):
                        dve.wait_ge(product, 2 * n + h + 1)
                        nc.vector.tensor_copy(res[b][0:R1, h * HALF:(h + 1) * HALF, :], psx[h][0:R1, :, :]
                                              ).then_inc(product_used, 1)

                def body(i, first, last):
                    for b in range(2):
                        n = 2 * i + b
                        if not (last and b == 1):
                            gather_indices(n + 1, i + b, 1 - b)
                        onehots(n, b)
                        if gated:
                            gate(n, b)
                        if not (first and b == 0):
                            finish(n - 1, i - 1 + b, 1 - b)
                        if projected and not first:
                            projections(n - 2, i - 1, b)
                gather_indices(0, 0, 0)
                rounds(dve, IT, body, peeled=2)
                finish(NB - 1, IT - 1, 1)
                if projected:
                    projections(NB - 2, IT - 1, 0)
                    projections(NB - 1, IT - 1, 1)


def layer3_constants_phase(env, a, t):
    nc = env.nc
    with env.phase() as ctx:
        loaded, chain = env.sem("l3_loaded"), env.sem("l3_chain")
        w = [env.sb(ctx, f"w{l}", [P, D]) for l in range(2)]
        bl = [env.sb(ctx, f"bl{l}", [P, D]) for l in range(2)]
        bcol = [env.sb(ctx, f"bcol{l}", [P, 1]) for l in range(2)]
        cw = [t[f"cw{l}"] for l in range(2)]
        cb = [env.sb(ctx, f"cb{l}", [P, 1]) for l in range(2)]
        scw = env.sb(ctx, "sum_cw", [P, 2])
        col = env.sb(ctx, "blank_column", [P, 2])
        diag = env.sb(ctx, "diag", [P, 2, D])
        prod = env.sb(ctx, "prod", [P, D])
        ps = env.ps(ctx, "ps", [P, 2, D])
        ready, spread = env.sem("l3_diag_ready"), env.sem("l3_spread")
        N_LOADS = 8 * 2
        with nc.Block() as block:
            @block.sync
            def _(sp):
                for l in range(2):
                    sp.dma_start(w[l][:], a[f"W3_{l}"][:, :]).then_inc(loaded, 16)
                    sp.dma_start(bl[l][:], a[f"blank{l}"].unsqueeze(0).to_broadcast([P, D])).then_inc(loaded, 16)
                    sp.dma_start(bcol[l][:], a[f"b{l}"].unsqueeze(1)).then_inc(loaded, 16)
                    sp.dma_start(cw[l][:], a[f"cw{l}"].unsqueeze(0).to_broadcast([P, 4])).then_inc(loaded, 16)
                    sp.dma_start(cb[l][:], a[f"cb{l}"].unsqueeze(0).to_broadcast([P, 1])).then_inc(loaded, 16)
                    sp.dma_start(t[f"a{l}"][:], a[f"a{l}"].unsqueeze(0).to_broadcast([P, 1])).then_inc(loaded, 16)
                    sp.dma_start(t[f"g{l}"][:], a[f"g{l}"].unsqueeze(0).to_broadcast([P, D])).then_inc(loaded, 16)
                    sp.dma_start(t[f"be{l}"][:], a[f"be{l}"].unsqueeze(0).to_broadcast([P, D])).then_inc(loaded, 16)
                sp.wait_ge(loaded, 16 * N_LOADS)

            @block.vector
            def _(dve):
                link = Chain(dve, chain)
                nc.vector.memset(t["ones"][:], 1.0)
                for k in range(1, 4):
                    nc.vector.tensor_scalar(t["shift"][:, k - 1, :], t["cols"][:], float(k), t["part"][:, 0:1],
                                            ALU.add, ALU.is_equal)
                dve.wait_ge(loaded, 16 * N_LOADS)
                for l in range(2):
                    for k in (1, 2):
                        nc.vector.tensor_scalar(t[f"cwi{l}"][:, k - 1, :], t["ident"][:], cw[l][:, k:k + 1], None, ALU.mult)
                    link(nc.vector.tensor_tensor(prod[:], w[l][:], bl[l][:], ALU.mult))
                    link(nc.vector.tensor_reduce(col[:, l:l + 1], prod[:], AX.X, ALU.add))
                    link(nc.vector.tensor_tensor(col[:, l:l + 1], col[:, l:l + 1], bcol[l][:], ALU.add))
                    link(nc.vector.tensor_reduce(scw[:, l:l + 1], cw[l][:], AX.X, ALU.add))
                    nc.vector.tensor_scalar(diag[:, l, :], t["ident"][:], col[:, l:l + 1], None, ALU.mult).then_inc(ready, 1)
                dve.wait_ge(spread, 1)
                for l in range(2):
                    link(nc.vector.tensor_copy(t[f"bp{l}"][:], ps[:, l, :]))
                    link(nc.vector.tensor_scalar(t[f"c{l}"][:], t[f"bp{l}"][:], scw[:, l:l + 1], cb[l][:, 0:1],
                                                 ALU.mult, ALU.add))

            @block.tensor
            def _(pe):
                pe.wait_ge(ready, 2)
                for l in range(2):
                    last = nc.tensor.matmul(ps[:, l, :], t["ones"][:], diag[:, l, :], start=True, stop=True)
                last.then_inc(spread, 1)


def edge_sorts_phase(env, a, t, table, agg, l):
    nc = env.nc
    N, E = a["x"].shape[0], a["src"].shape[0]
    NB = E // (ROWS * K)
    IT = NB // 2
    with env.phase() as ctx:
        g = [env.sb(ctx, f"rows{b}", [P, K, D]) for b in range(2)]
        v = [env.sb(ctx, f"slots{b}", [P, 4, K, D]) for b in range(2)]
        mn, mx = (env.sb(ctx, n, [P, 2, K, D]) for n in ("pair_min", "pair_max"))
        order = [env.sb(ctx, f"order{b}", [P, 4, K, D]) for b in range(2)]
        res = [env.sb(ctx, f"res{b}", [P, K, D]) for b in range(2)]
        gi = [env.sb(ctx, f"gi{b}", [P, K], I32) for b in range(2)]
        si = [env.sb(ctx, f"si{b}", [P, K], I32) for b in range(2)]
        has = [env.sb(ctx, f"has{b}", [P, 3, K]) for b in range(2)]
        psv = [env.ps(ctx, f"psv{j}", [P, HALF, D]) for j in range(4)]
        psw = [env.ps(ctx, f"psw{b}", [P, K, D]) for b in range(2)]
        S = env.sem
        begun = S("dma_series_begun")
        cleared, idx_ready, blanked = S("cleared"), S("idx_ready"), S("rows_less_blank")
        gathered = [S(f"gathered{b}") for b in range(2)]
        scattered = [S(f"scattered{b}") for b in range(2)]
        shifted, masked, pairs, ends, ordered = S("shifted"), S("masked"), S("pairs"), S("ends"), S("ordered")
        weighted, least_added, res_ready = S("middle_weighted"), S("least_added"), S("res_ready")
        with nc.Block() as block:
            @block.gpsimd
            def _(pool):
                bound = pool.to_reg(N - 1)

                def scatter(n, b):
                    pool.wait_ge(res_ready, n + 1)
                    pool.sem_inc(begun, 1)
                    for k in range(K):
                        pool.indirect_dma_start(
                            out=agg[0:N, :], out_offset=bass.IndirectOffsetOnAxis(ap=si[b][:, k:k + 1], axis=0),
                            in_=res[b][:, k, :], in_offset=None,
                            bounds_check=bound, oob_is_err=False).then_inc(scattered[b], 16)

                def gather(n, b):
                    pool.wait_ge(idx_ready, n + 1)
                    wait_past(pool, blanked, n - 1)
                    pool.sem_inc(begun, 1)
                    for k in range(K):
                        pool.indirect_dma_start(
                            out=g[b][:, k, :], out_offset=None, in_=table[0:N, :],
                            in_offset=bass.IndirectOffsetOnAxis(ap=gi[b][:, k:k + 1], axis=0),
                            bounds_check=bound, oob_is_err=False).then_inc(gathered[b], 16)

                def body(i, first, last):
                    gather(2 * i + 1, 1)
                    if not first:
                        scatter(2 * i - 2, 0)
                    if not last:
                        gather(2 * i + 2, 0)
                    if not first:
                        scatter(2 * i - 1, 1)
                pool.wait_ge(cleared, 1)
                gather(0, 0)
                rounds(pool, IT, body)
                scatter(NB - 2, 0)
                scatter(NB - 1, 1)
                for b in range(2):
                    pool.wait_ge(scattered[b], 16 * K * IT)

            @block.vector
            def _(dve):
                nc.vector.memset(g[0][:], 0.0)
                nc.vector.memset(g[1][:], 0.0).then_inc(cleared, 1)

                def gather_indices(n, i, b):
                    wait_past(dve, gathered[b], 16 * K * i)
                    nc.vector.tensor_copy(gi[b][:], t["gidx3"][:, bass.ds(n * K, K)]).then_inc(idx_ready, 1)

                def less_blank(n, i, b):
                    wait_past(dve, masked, 6 * (n - 1))
                    for k in range(3):
                        nc.vector.tensor_copy(has[b][:, k, :], t[f"has{k + 1}"][:, bass.ds(n * K, K)])
                    dve.wait_ge(gathered[b], 16 * K * (i + 1))
                    wait_past(dve, ordered, n - 1)
                    nc.vector.tensor_tensor(v[b][:, 0, :, :], g[b][:],
                                            t[f"bp{l}"][:].unsqueeze(1).to_broadcast([P, K, D]),
                                            ALU.subtract).then_inc(blanked, 1)

                def sort(n, i, b):
                    dve.wait_ge(masked, 6 * (n + 1))
                    wait_past(dve, ordered, n)
                    nc.vector.tensor_tensor(mn[:], v[b][:, 0:4:2, :, :], v[b][:, 1:4:2, :, :], ALU.min)
                    nc.vector.tensor_tensor(mx[:], v[b][:, 0:4:2, :, :], v[b][:, 1:4:2, :, :], ALU.max).then_inc(pairs, 1)
                    dve.wait_ge(pairs, n + 1)
                    nc.vector.tensor_tensor(v[b][:, 1, :, :], mn[:, 0, :, :], mn[:, 1, :, :], ALU.max)
                    nc.vector.tensor_tensor(v[b][:, 2, :, :], mx[:, 0, :, :], mx[:, 1, :, :], ALU.min).then_inc(ends, 1)
                    wait_past(dve, res_ready, n - 1)
                    nc.vector.tensor_tensor(order[b][:, 0, :, :], mn[:, 0, :, :], mn[:, 1, :, :], ALU.min)
                    nc.vector.tensor_tensor(order[b][:, 3, :, :], mx[:, 0, :, :], mx[:, 1, :, :], ALU.max)
                    dve.wait_ge(ends, n + 1)
                    nc.vector.tensor_tensor(order[b][:, 1, :, :], v[b][:, 1, :, :], v[b][:, 2, :, :], ALU.min)
                    nc.vector.tensor_tensor(order[b][:, 2, :, :], v[b][:, 1, :, :], v[b][:, 2, :, :], ALU.max
                                            ).then_inc(ordered, 1)

                def finish(n, i, b):
                    wait_past(dve, scattered[b], 16 * K * i)
                    nc.vector.tensor_copy(si[b][:], t["sidx3"][:, bass.ds(n * K, K)])
                    dve.wait_ge(weighted, n + 1)
                    nc.vector.scalar_tensor_tensor(res[b][:], order[b][:, 0, :, :], t[f"cw{l}"][:, 0:1], psw[b][:],
                                                   ALU.mult, ALU.add).then_inc(least_added, 1)
                    dve.wait_ge(least_added, n + 1)
                    nc.vector.scalar_tensor_tensor(res[b][:], order[b][:, 3, :, :], t[f"cw{l}"][:, 3:4], res[b][:],
                                                   ALU.mult, ALU.add).then_inc(res_ready, 1)

                def body(i, first, last):
                    for b in range(2):
                        n = 2 * i + b
                        if not (last and b == 1):
                            gather_indices(n + 1, i + b, 1 - b)
                        less_blank(n, i, b)
                        if not (first and b == 0):
                            sort(n - 1, i - 1 + b, 1 - b)
                        if not first:
                            finish(n - 2, i - 1, b)
                gather_indices(0, 0, 0)
                rounds(dve, IT, body, peeled=2)
                sort(NB - 1, IT - 1, 1)
                finish(NB - 2, IT - 1, 0)
                finish(NB - 1, IT - 1, 1)

            @block.tensor
            def _(pe):
                def body(i, first, last):
                    for b in range(2):
                        n = 2 * i + b
                        pe.wait_ge(blanked, n + 1)
                        for k in range(3):
                            for h in range(2):
                                j = 2 * k + h
                                if not (first and b == 0 and j < 4):
                                    pe.wait_ge(masked, 6 * n + j - 3)
                                nc.tensor.matmul(psv[(6 * b + j) % 4][:].rearrange("p k d -> p (k d)"),
                                                 t["shift"][:, k, :], flat(v[b][:, 0, h * HALF:(h + 1) * HALF, :]),
                                                 start=True, stop=True).then_inc(shifted, 1)
                        if not (first and b == 0):
                            weigh(n - 1, 1 - b)

                def weigh(n, b):
                    pe.wait_ge(ordered, n + 1)
                    wait_past(pe, least_added, n - 1)
                    for h in range(2):
                        part = slice(h * HALF, (h + 1) * HALF)
                        for k in (1, 2):
                            last = nc.tensor.matmul(flat(psw[b][:, part, :]), t[f"cwi{l}"][:, k - 1, :],
                                                    flat(order[b][:, k, part, :]), start=(k == 1), stop=(k == 2))
                    last.then_inc(weighted, 1)
                rounds(pe, IT, body, peeled=2)
                weigh(NB - 1, 1)

            @block.scalar
            def _(act):
                def body(i, first, last):
                    for b in range(2):
                        n = 2 * i + b
                        for k in range(3):
                            for h in range(2):
                                j = 2 * k + h
                                act.wait_ge(shifted, 6 * n + j + 1)
                                for q in range(HALF):
                                    ins = nc.scalar.activation(v[b][:, k + 1, h * HALF + q, :],
                                                               psv[(6 * b + j) % 4][:, q, :], ACT.Copy,
                                                               scale=has[b][:, k, h * HALF + q:h * HALF + q + 1])
                                ins.then_inc(masked, 1)
                rounds(act, IT, body)


def rows_of(dram, tile, n, N, whole):
    if whole:
        return [(dram[bass.ds(n * GROUP, GROUP), :].rearrange("(p t) d -> p (t d)", p=P), flat(tile[:]))]
    r0, left = n * GROUP, N - n * GROUP
    full, part = left // T, left % T
    pairs = [(dram[r0:r0 + full * T, :].rearrange("(p t) d -> p (t d)", p=full), flat(tile[0:full, :, :]))]
    if part:
        pairs.append((dram[r0 + full * T:N, :].unsqueeze(0), tile[full:full + 1, 0:part, :]))
    return pairs


class Loads:

    def __init__(self, env, ctx, arrays, N, NG):
        self.arrays, self.N, self.NG = arrays, N, NG
        self.bufs = {n: [env.sb(ctx, f"{n}{b}", [P, T, D]) for b in range(2)] for n in arrays}
        self.sems = {n: [env.sem(f"{n}_loaded{b}") for b in range(2)] for n in arrays}

    def pairs(self, name, n, b, last):
        dram = self.arrays[name]
        whole = not (last and b == 1) or dram.shape[0] == self.NG * GROUP
        return rows_of(dram, self.bufs[name][b], n, self.N, whole)

    def issue(self, sp, name, n, b, last):
        for dram, tile in self.pairs(name, n, b, last):
            sp.dma_start(tile, dram).then_inc(self.sems[name][b], 16)

    def wait(self, engine, name, i, b, last):
        engine.wait_ge(self.sems[name][b], 16 * i + 16 * len(self.pairs(name, 2 * i + b, b, last)))


def node_norm_phase(env, a, t, layer, arrays, out):
    nc = env.nc
    N = a["x"].shape[0]
    NG = -(-N // GROUP)
    IT = NG // 2
    banks = [(c, min(HALF, T - c)) for c in range(0, T, HALF)]
    NBK = len(banks)
    with env.phase() as ctx:
        ld = Loads(env, ctx, arrays, N, NG)
        xb, ab = ld.bufs["x"], ld.bufs["agg"]
        s = [env.sb(ctx, f"sum{b}", [P, T, D]) for b in range(2)]
        o = [env.sb(ctx, f"out{b}", [P, T, D]) for b in range(2)]
        st = env.sb(ctx, "stats", [P, T, 6])
        msum, var, std, rstd, nbias = (
            [env.sb(ctx, f"{n}{b}", [P, T]) for b in range(2)] for n in ("msum", "var", "std", "rstd", "nbias"))
        sm = {n: env.sb(ctx, n, [P, T]) for n in ("mdiff", "m2", "dsq", "v4")}
        S = env.sem
        pre_done, added, var_ready, std_ready, norm_ready = (
            S("pool_done"), S("loads_added"), S("variance_ready"), S("std_ready"), S("factors_ready"))
        pool_step, chain, normed, factor_step = S("pool_step"), S("vector_chain"), S("normalised"), S("factor_step")
        stored = [S(f"out_stored{b}") for b in range(2)]
        consts = S("consts_loaded")
        xtr, xcp, prod, prod_added = S("x_transposed"), S("x_copied"), S("x_times_w"), S("product_added")
        if layer in (1, 2):
            bias = env.sb(ctx, "bias", [P, D])
        if layer == 1:
            wself = env.sb(ctx, "w_self", [P, D])
            xt = [env.sb(ctx, f"xt{j}", [P, HALF, P]) for j in range(2)]
            pst = [env.ps(ctx, f"pst{j}", [P, HALF, P]) for j in range(2)]
            psx = [env.ps(ctx, f"psx{j}", [P, HALF, D]) for j in range(4)]
        NCONST = {0: 0, 1: 2, 2: 1, 3: 0}[layer]
        begun = S("load_begun")
        if layer:
            u = [env.sb(ctx, f"pool_share{b}", [P, T, D]) for b in range(2)]

        PSX = [z % 4 for z in range(2 * NBK)]

        def over_rows(vec):
            return vec[:].unsqueeze(1).to_broadcast([P, T, D])
        with nc.Block() as block:
            @block.sync
            def _(sp):
                if layer in (1, 2):
                    sp.dma_start(bias[:], a[f"b_{layer}"].unsqueeze(0).to_broadcast([P, D])).then_inc(consts, 16)
                if layer == 1:
                    sp.dma_start(wself[:], a["W_self"][:, :]).then_inc(consts, 16)

                def body(i, first, last):
                    for b in range(2):
                        n = 2 * i + b
                        for name in arrays:
                            if layer == 3:
                                wait_past(sp, {"agg": pool_step, "x": pre_done, "x4": added}[name], n - 1)
                            elif layer and name == "agg":
                                wait_past(sp, pre_done, n - 1)
                            else:
                                wait_past(sp, added, n - 1)
                                if layer == 1:
                                    sp.sem_inc(begun, 1)
                                    wait_past(sp, xtr, NBK * (n - 1))
                            ld.issue(sp, name, n, b, last)
                rounds(sp, IT, body, peeled=2)
                if NCONST:
                    sp.wait_ge(consts, 16 * NCONST)

            if layer:
                @block.gpsimd
                def _(pool):
                    def body(i, first, last):
                        for b in range(2):
                            n = 2 * i + b
                            ld.wait(pool, "agg", i, b, last)
                            if layer == 1:
                                wait_past(pool, prod_added, NBK * (n - 1))
                            else:
                                wait_past(pool, added, n - 1)
                            if layer == 3:
                                nc.gpsimd.tensor_tensor(u[b][:], ab[b][:], over_rows(t["bn_scale"]), ALU.mult
                                                        ).then_inc(pool_step, 1)
                                ld.wait(pool, "x", i, b, last)
                                pool.wait_ge(pool_step, n + 1)
                                nc.gpsimd.tensor_tensor(u[b][:], u[b][:], xb[b][:], ALU.add).then_inc(pre_done, 1)
                            else:
                                nc.gpsimd.tensor_tensor(u[b][:], ab[b][:], over_rows(bias), ALU.add).then_inc(pre_done, 1)
                    if NCONST:
                        pool.wait_ge(consts, 16 * NCONST)
                    rounds(pool, IT, body, peeled=2)

            if layer == 1:
                @block.tensor
                def _(pe):
                    pe.wait_ge(consts, 16 * NCONST)

                    def body(i, first, last):
                        for b in range(2):
                            n = 2 * i + b
                            ld.wait(pe, "x", i, b, last)

                            def times_w(j):
                                c, w = banks[j]
                                q, z = NBK * n + j, NBK * b + j
                                pe.wait_ge(xcp, q + 1)
                                wait_past(pe, prod_added, q - (1 if z < 2 else 3))
                                for k in range(w):
                                    m = nc.tensor.matmul(psx[PSX[z]][:, k, :], xt[z % 2][:, k, :],
                                                         wself[:], start=True, stop=True)
                                m.then_inc(prod, 1)
                            for j, (c, w) in enumerate(banks):
                                q, z = NBK * n + j, NBK * b + j
                                wait_past(pe, xcp, q - 1)
                                for k in range(w):
                                    m = nc.tensor.transpose(pst[z % 2][:, k, :], xb[b][:, c + k, :], t["ident"][:])
                                m.then_inc(xtr, 1)
                                if j:
                                    times_w(j - 1)
                            times_w(NBK - 1)
                    rounds(pe, IT, body, peeled=2)
            @block.vector
            def _(dve):
                if NCONST:
                    dve.wait_ge(consts, 16 * NCONST)
                LINKS = 3 + (2 if layer == 3 else 0)

                def factors(n, b):
                    dve.wait_ge(std_ready, n + 1)
                    nc.vector.reciprocal(rstd[b][:], std[b][:]).then_inc(factor_step, 1)
                    dve.wait_ge(factor_step, n + 1)
                    nc.vector.scalar_tensor_tensor(nbias[b][:], msum[b][:], -0.5, rstd[b][:],
                                                   ALU.mult, ALU.mult).then_inc(norm_ready, 1)

                def body(i, first, last):
                    link = Chain(dve, chain, 2 * LINKS * i)
                    for b in range(2):
                        n = 2 * i + b
                        y = s[b]
                        if layer == 3:
                            main = ld.bufs["x4"][b]
                            ld.wait(dve, "x4", i, b, last)
                            link(nc.vector.tensor_tensor(main[:], main[:], over_rows(t["bn_alpha"]), ALU.mult))
                            link(nc.vector.tensor_tensor(main[:], main[:], over_rows(t["bn_shift"]), ALU.add))
                        else:
                            main = xb[b]
                            ld.wait(dve, "x", i, b, last)
                        if layer:
                            dve.wait_ge(pre_done, n + 1)
                        else:
                            ld.wait(dve, "agg", i, b, last)
                        share = (u if layer else ab)[b]
                        if layer == 1:
                            half = share
                        else:
                            wait_past(dve, normed, n - 1)
                            half = y
                        nc.vector.tensor_tensor(half[:], main[:], share[:], ALU.add).then_inc(added, 1)
                        if not (first and b == 0):
                            factors(n - 1, 1 - b)
                        dve.wait_ge(added, n + 1)
                        if layer == 1:
                            wait_past(dve, normed, n - 1)
                            for j, (c, w) in enumerate(banks):
                                dve.wait_ge(prod, NBK * n + j + 1)
                                nc.vector.tensor_tensor(y[:, c:c + w, :], half[:, c:c + w, :],
                                                        psx[PSX[NBK * b + j]][:, 0:w, :], ALU.add).then_inc(prod_added, 1)
                            dve.wait_ge(prod_added, NBK * (n + 1))
                        for k in range(T):
                            ins = nc.vector.bn_stats(st[:, k, :], y[:, k, :])
                        link(ins)
                        nc.vector.tensor_tensor(msum[b][:], st[:, :, 1], st[:, :, 4], ALU.add)
                        nc.vector.tensor_tensor(sm["m2"][:], st[:, :, 2], st[:, :, 5], ALU.add)
                        link(nc.vector.tensor_tensor(sm["mdiff"][:], st[:, :, 1], st[:, :, 4], ALU.subtract))
                        nc.vector.tensor_scalar(sm["v4"][:], sm["m2"][:], 1.0 / D, EPS, ALU.mult, ALU.add)
                        link(nc.vector.scalar_tensor_tensor(sm["dsq"][:], sm["mdiff"][:], 0.25, sm["mdiff"][:],
                                                            ALU.mult, ALU.mult))
                        nc.vector.tensor_tensor(var[b][:], sm["v4"][:], sm["dsq"][:], ALU.add).then_inc(var_ready, 1)
                    assert link.n == 2 * LINKS, link.n
                rounds(dve, IT, body, peeled=2)
                factors(NG - 1, 1)

            @block.scalar
            def _(act):
                def normalise(b, rows):
                    for k in rows:
                        ins = nc.scalar.activation(o[b][:, k, :], s[b][:, k, :], ACT.Identity,
                                                   bias=nbias[b][:, k:k + 1], scale=rstd[b][:, k:k + 1])
                    return ins

                def may_normalise(n, i, b):
                    act.wait_ge(norm_ready, n + 1)
                    wait_past(act, stored[b], 16 * i)

                def store(n, b, normalised, cut):
                    normalised.then_inc(normed, 1)
                    act.wait_ge(normed, n + 1)
                    for dram, tile in rows_of(out, o[b], n, N, not cut):
                        act.dma_start(dram, tile).then_inc(stored[b], 16)

                def copy_transposed(n, b, j):
                    c, w = banks[j]
                    q, z = NBK * n + j, NBK * b + j
                    act.wait_ge(xtr, q + 1)
                    wait_past(act, prod, q - 1)
                    nc.scalar.copy(xt[z % 2][:, 0:w, :], pst[z % 2][:, 0:w, :]).then_inc(xcp, 1)

                def body(i, first, last):
                    for b in range(2):
                        n = 2 * i + b
                        behind, ahead = not (first and b == 0), layer == 1 and not (last and b == 1)
                        if behind:
                            may_normalise(n - 1, i - 1 + b, 1 - b)
                        for j, (c, w) in enumerate(banks):
                            if ahead:
                                copy_transposed(n + 1, 1 - b, j)
                            if behind:
                                ins = normalise(1 - b, range(c, c + w))
                        if behind:
                            store(n - 1, 1 - b, ins, False)
                        act.wait_ge(var_ready, n + 1)
                        nc.scalar.activation(std[b][:], var[b][:], ACT.Sqrt).then_inc(std_ready, 1)
                if layer == 1:
                    for j in range(NBK):
                        copy_transposed(0, 0, j)
                rounds(act, IT, body, peeled=2)
                may_normalise(NG - 1, IT - 1, 1)
                store(NG - 1, 1, normalise(1, range(T)), True)
                act.wait_ge(stored[0], 16 * IT)
                act.wait_ge(stored[1], 16 * (IT - 1) + 16 * len(rows_of(out, o[1], NG - 1, N, False)))


def bn_stats_phase(env, a, t, x, agg, l):
    nc = env.nc
    N = a["x"].shape[0]
    NG = -(-N // GROUP)
    IT = NG // 2
    chunks = [(c, min(HALF, T - c)) for c in range(0, T, HALF)]
    with env.phase() as ctx:
        ld = Loads(env, ctx, {"x": x, "agg": agg}, N, NG)
        xb, ab = ld.bufs["x"], ld.bufs["agg"]
        h = [env.sb(ctx, f"h{b}", [P, T, D]) for b in range(2)]
        sq = [env.sb(ctx, f"sq{b}", [P, T, D]) for b in range(2)]
        acc = env.sb(ctx, "h_sums", [P, T, D])
        acc2 = env.sb(ctx, "sq_sums", [P, HALF, D])
        f = {n: env.sb(ctx, n, [P, D]) for n in ("mean", "ex2", "var", "std", "rstd", "tmp")}
        ps = [env.ps(ctx, f"ps{b}", [P, HALF, D]) for b in range(2)]
        psm = env.ps(ctx, "psm", [P, HALF, D])
        S = env.sem
        h_ready, squared, sq_summed, sq_added, chain = (
            S("h_ready"), S("squared"), S("squares_summed"), S("squares_added"), S("bn_chain"))
        acc_summed, var_ready, std_ready, h_added = (
            S("acc_summed"), S("var_ready"), S("std_ready"), S("h_added"))
        with nc.Block() as block:
            @block.sync
            def _(sp):
                def body(i, first, last):
                    for b in range(2):
                        n = 2 * i + b
                        if not first:
                            sp.wait_ge(h_ready, n - 1)
                        ld.issue(sp, "x", n, b, last)
                        ld.issue(sp, "agg", n, b, last)
                rounds(sp, IT, body, peeled=2)

            @block.vector
            def _(dve):
                nc.vector.memset(acc[:], 0.0).then_inc(h_added, 1)
                nc.vector.memset(acc2[:], 0.0).then_inc(sq_added, 1)

                def add_squares(n, b):
                    dve.wait_ge(sq_summed, n + 1)
                    dve.wait_ge(sq_added, n + 1)
                    nc.vector.tensor_tensor(acc2[:], acc2[:], ps[b][:], ALU.add).then_inc(sq_added, 1)

                def body(i, first, last):
                    for b in range(2):
                        n = 2 * i + b
                        ld.wait(dve, "x", i, b, last)
                        ld.wait(dve, "agg", i, b, last)
                        if not first:
                            dve.wait_ge(squared, n - 1)
                        nc.vector.scalar_tensor_tensor(h[b][:], xb[b][:], t[f"a{l}"][:, 0:1], ab[b][:],
                                                       ALU.mult, ALU.add).then_inc(h_ready, 1)
                        if not (first and b == 0):
                            add_squares(n - 1, 1 - b)
                        dve.wait_ge(h_ready, n + 1)
                        dve.wait_ge(h_added, n + 1)
                        nc.vector.tensor_tensor(acc[:], acc[:], h[b][:], ALU.add).then_inc(h_added, 1)
                rounds(dve, IT, body)
                add_squares(NG - 1, 1)
                link = Chain(dve, chain)
                dve.wait_ge(sq_added, NG + 1)
                dve.wait_ge(acc_summed, 1)
                link(nc.vector.tensor_reduce(f["mean"][:], psm[:].rearrange("p k d -> p d k"), AX.X, ALU.add))
                link(nc.vector.tensor_reduce(f["ex2"][:], acc2[:].rearrange("p k d -> p d k"), AX.X, ALU.add))
                link(nc.vector.tensor_scalar(f["mean"][:], f["mean"][:], 1.0 / N, None, ALU.mult))
                link(nc.vector.tensor_scalar(f["ex2"][:], f["ex2"][:], 1.0 / N, EPS, ALU.mult, ALU.add))
                link(nc.vector.tensor_tensor(f["tmp"][:], f["mean"][:], f["mean"][:], ALU.mult))
                nc.vector.tensor_tensor(f["var"][:], f["ex2"][:], f["tmp"][:], ALU.subtract).then_inc(var_ready, 1)
                dve.wait_ge(std_ready, 1)
                link(nc.vector.reciprocal(f["rstd"][:], f["std"][:]))
                link(nc.vector.tensor_tensor(t["bn_scale"][:], t[f"g{l}"][:], f["rstd"][:], ALU.mult))
                link(nc.vector.tensor_scalar(t["bn_alpha"][:], t["bn_scale"][:], t[f"a{l}"][:, 0:1], 1.0, ALU.mult, ALU.add))
                link(nc.vector.tensor_tensor(f["mean"][:], f["mean"][:], t[f"c{l}"][:], ALU.add))
                link(nc.vector.tensor_tensor(f["tmp"][:], t[f"c{l}"][:], f["mean"][:], ALU.subtract))
                link(nc.vector.tensor_tensor(f["tmp"][:], f["tmp"][:], t["bn_scale"][:], ALU.mult))
                link(nc.vector.tensor_tensor(t["bn_shift"][:], f["tmp"][:], t[f"be{l}"][:], ALU.add))

            @block.scalar
            def _(act):
                def body(i, first, last):
                    for b in range(2):
                        n = 2 * i + b
                        act.wait_ge(h_ready, n + 1)
                        if not first:
                            act.wait_ge(sq_summed, n - 1)
                        nc.scalar.activation(sq[b][:], h[b][:], ACT.Square).then_inc(squared, 1)
                rounds(act, IT, body)
                act.wait_ge(var_ready, 1)
                nc.scalar.activation(f["std"][:], f["var"][:], ACT.Sqrt).then_inc(std_ready, 1)

            @block.tensor
            def _(pe):
                def body(i, first, last):
                    for b in range(2):
                        n = 2 * i + b
                        pe.wait_ge(squared, n + 1)
                        if not first:
                            pe.wait_ge(sq_added, n)
                        for c, w in chunks:
                            m = nc.tensor.matmul(flat(ps[b][:, 0:w, :]), t["ones"][:], flat(sq[b][:, c:c + w, :]),
                                                 start=(c == 0), stop=(c + w == T))
                        m.then_inc(sq_summed, 1)
                rounds(pe, IT, body)
                pe.wait_ge(h_added, NG + 1)
                for c, w in chunks:
                    m = nc.tensor.matmul(flat(psm[:, 0:w, :]), t["ones"][:], flat(acc[:, c:c + w, :]),
                                         start=(c == 0), stop=(c + w == T))
                m.then_inc(acc_summed, 1)


def bn_apply_phase(env, a, t, x, agg, out):
    nc = env.nc
    N = a["x"].shape[0]
    NG = -(-N // GROUP)
    IT = NG // 2
    with env.phase() as ctx:
        ld = Loads(env, ctx, {"x": x, "agg": agg}, N, NG)
        xb, ab = ld.bufs["x"], ld.bufs["agg"]
        o = [env.sb(ctx, f"o{b}", [P, T, D]) for b in range(2)]
        S = env.sem
        scaled, chain, done = S("agg_scaled"), S("apply_chain"), S("apply_done")
        stored = [S(f"apply_stored{b}") for b in range(2)]
        with nc.Block() as block:
            @block.sync
            def _(sp):
                def body(i, first, last):
                    for b in range(2):
                        n = 2 * i + b
                        if not first:
                            sp.wait_ge(done, n - 1)
                        ld.issue(sp, "x", n, b, last)
                        ld.issue(sp, "agg", n, b, last)
                rounds(sp, IT, body, peeled=2)

            @block.gpsimd
            def _(pool):
                def body(i, first, last):
                    for b in range(2):
                        ld.wait(pool, "agg", i, b, last)
                        nc.gpsimd.tensor_tensor(ab[b][:], ab[b][:], t["bn_scale"][:].unsqueeze(1).to_broadcast([P, T, D]),
                                                ALU.mult).then_inc(scaled, 1)
                rounds(pool, IT, body)

            @block.vector
            def _(dve):
                def body(i, first, last):
                    link = Chain(dve, chain, 4 * i)
                    for b in range(2):
                        n = 2 * i + b
                        ld.wait(dve, "x", i, b, last)
                        if not first:
                            dve.wait_ge(stored[b], 16 * i)
                        link(nc.vector.tensor_tensor(o[b][:], xb[b][:], t["bn_alpha"][:].unsqueeze(1).to_broadcast([P, T, D]), ALU.mult))
                        link(nc.vector.tensor_tensor(o[b][:], o[b][:], t["bn_shift"][:].unsqueeze(1).to_broadcast([P, T, D]), ALU.add))
                        dve.wait_ge(scaled, n + 1)
                        nc.vector.tensor_tensor(o[b][:], o[b][:], ab[b][:], ALU.add).then_inc(done, 1)
                rounds(dve, IT, body)

            @block.scalar
            def _(act):
                def body(i, first, last):
                    for b in range(2):
                        n = 2 * i + b
                        act.wait_ge(done, n + 1)
                        for dram, tile in rows_of(out, o[b], n, N, not (last and b == 1)):
                            act.dma_start(dram, tile).then_inc(stored[b], 16)
                rounds(act, IT, body)
                act.wait_ge(stored[0], 16 * IT)
                act.wait_ge(stored[1], 16 * (IT - 1) + 16 * len(rows_of(out, o[1], NG - 1, N, False)))


def gnn_program(nc, a, out):
    N, E = a["x"].shape[0], a["src"].shape[0]
    NT = E // ROWS
    NPAD = -(-N // GROUP) * GROUP
    Q, F = NT // C4, C4 * ROWS
    x1, x2, x3, x4, agg = (nc.dram_tensor(n, (NPAD, D), F32).ap() for n in ("x1", "x2", "x3", "x4", "agg"))
    edge_rows = nc.dram_tensor("edge_rows", (NT // K * P, K * D), F32).ap()
    with ExitStack() as ctx:
        env = Env(nc, ctx)
        t = {}
        for n in ("gidx", "didx", "sidx", "gidx3", "sidx3"):
            t[n] = env.sb(ctx, n, [P, NT], I32)
        for n in ("row", "nx", "w0", "w1", "has1", "has2", "has3", "logit"):
            t[n] = env.sb(ctx, n, [P, NT])
        for n in ("same", "nsame", "sadd", "nadd"):
            t[n] = env.sb(ctx, n, [Q, F])
        t["flow"] = env.sb(ctx, "flow", [K + 1, NT // K, 2, K + 1])
        t["into"] = env.sb(ctx, "into", [K + 1, K, ROWS + 1])
        t["etype_i"] = env.sb(ctx, "etype_i", [Q, F], I32)
        t["thru"] = env.sb(ctx, "thru", [Q, 4])
        t["one"] = env.sb(ctx, "one", [1, 1])
        t["part"] = env.sb(ctx, "part", [P, 1])
        for n in ("cols", "ident", "ones", "bn_scale", "bn_alpha", "bn_shift", "g0", "g1", "be0", "be1", "bp0", "bp1", "c0", "c1"):
            t[n] = env.sb(ctx, n, [P, P])
        for l in range(2):
            t[f"a{l}"] = env.sb(ctx, f"a{l}", [P, 1])
            t[f"cw{l}"] = env.sb(ctx, f"cw{l}", [P, 4])
            t[f"cwi{l}"] = env.sb(ctx, f"cwi{l}", [P, 2, P])
        t["shift"] = env.sb(ctx, "shift", [P, 3, P])

        tables_phase(env, a, t)
        layer3_constants_phase(env, a, t)
        logits_phase(env, a, t, edge_rows, agg, [x1, x2, x3, x4])
        softmax_phase(env, a, t)
        edge_sums_phase(env, a, t, None, agg, 0, edge_rows)
        node_norm_phase(env, a, t, 0, {"x": a["x"], "agg": agg}, x1)
        edge_sums_phase(env, a, t, x1, agg, 1, None)
        node_norm_phase(env, a, t, 1, {"agg": agg, "x": x1}, x2)
        edge_sums_phase(env, a, t, x2, agg, 2, None)
        node_norm_phase(env, a, t, 2, {"agg": agg, "x": x2}, x3)
        edge_sorts_phase(env, a, t, x3, agg, 0)
        bn_stats_phase(env, a, t, x3, agg, 0)
        bn_apply_phase(env, a, t, x3, agg, x4)
        edge_sorts_phase(env, a, t, x4, agg, 1)
        bn_stats_phase(env, a, t, x4, agg, 1)
        node_norm_phase(env, a, t, 3, {"agg": agg, "x": x3, "x4": x4}, out)


_NAMES = {
    "x": "x", "src": "src", "dst": "dst", "edge_attr_16": "ea", "edge_type_8": "etype",
    "L0_gnn_head_w": "head_w", "L0_gnn_head_b": "head_b", "L0_gnn_tail_w": "tail_w", "L0_gnn_tail_b": "tail_b",
    "L0_gnn_rel_w": "rel_w", "L1_gnn_W_self": "W_self", "L1_gnn_W_neigh": "W_neigh", "L1_gnn_b": "b_1",
    "L2_gnn_W": "W2", "L2_gnn_edge_w": "edge_w", "L2_gnn_b": "b_2",
    "L3_gnn_W0": "W3_0", "L3_gnn_b0": "b0", "L3_gnn_cw0": "cw0", "L3_gnn_cb0": "cb0", "L3_gnn_a0": "a0",
    "L3_gnn_g0": "g0", "L3_gnn_be0": "be0", "L3_gnn_blank0": "blank0",
    "L3_gnn_W1": "W3_1", "L3_gnn_b1": "b1", "L3_gnn_cw1": "cw1", "L3_gnn_cb1": "cb1", "L3_gnn_a1": "a1",
    "L3_gnn_g1": "g1", "L3_gnn_be1": "be1", "L3_gnn_blank1": "blank1",
}


def kernel(**inputs):
    import numpy as _np
    import concourse.bacc as _bacc
    from concourse import mybir as _mybir
    from concourse.bass_utils import run_bass_kernel_spmd as _run

    nc = _bacc.Bacc("TRN2", target_bir_lowering=False, num_devices=1)
    arrays, args = {}, {}
    for name, short in _NAMES.items():
        v = _np.ascontiguousarray(inputs[name])
        arrays[f"in_{name}"] = v
        args[short] = nc.dram_tensor(f"in_{name}", v.shape, _mybir.dt.from_np(v.dtype), kind="ExternalInput").ap()
    out = nc.dram_tensor("out_x", inputs["x"].shape, _mybir.dt.float32, kind="ExternalOutput").ap()
    gnn_program(nc, args, out)
    r = _run(nc, [arrays], core_ids=[0])
    return r.results[0]["out_x"]
```
